# Optimizing a Trainium2 kernel written in Bass

```python
import numpy as np
import jax
import jax.numpy as jnp

def _softmax(x, axis=-1):
    return jax.nn.softmax(x, axis=axis)

def _gelu(x):
    return jax.nn.gelu(x, approximate=True)

def _silu(x):
    return jax.nn.silu(x)

def _sigmoid(x):
    return jax.nn.sigmoid(x)

def _layernorm(x, axis=-1, eps=1e-05):
    m = jnp.mean(x, axis=axis, keepdims=True)
    v = jnp.var(x, axis=axis, keepdims=True)
    return (x - m) / jnp.sqrt(v + eps)

def _scatter_add(tgt, idx, src, axis=0):
    return tgt.at[idx].add(src)

def _segment_sum(src, seg, n):
    return jax.ops.segment_sum(src, seg, n)
kernel_name = 'mk_xattn_ffn_d2_seqx_r8_9d5a94'

def setup_inputs(seed: int=0):
    np.random.seed(seed)
    _w = jnp.asarray

    def _rec_inputs():
        import jax
        import jax.numpy as jnp
        _rk = jax.random.key(seed)
        x = -0.0005207 + 1.001 * jax.random.normal(jax.random.fold_in(_rk, 1), (2, 512, 128), jnp.float32)
        _lenS = 512 - jax.random.randint(jax.random.fold_in(_rk, 7), (2,), 0, max(1, 512 // 4) + 1, jnp.int32)
        _lenS2 = 77 - jax.random.randint(jax.random.fold_in(_rk, 8), (2,), 0, max(1, 77 // 4) + 1, jnp.int32)
        _ctx_1024P = jax.random.normal(jax.random.fold_in(_rk, 11), (2, 16, 128), jnp.float32)
        _ctx_1024c = jax.random.dirichlet(jax.random.fold_in(_rk, 511), 0.3 * jnp.ones((16,), jnp.float32), (2, 77))
        _ctx_1024t = jnp.einsum('bsk,bkd->bsd', _ctx_1024c, _ctx_1024P)
        _ctx_1024t = _ctx_1024t * jax.lax.rsqrt(jnp.mean(jnp.square(_ctx_1024t)) + 1e-12) * 0.953939
        ctx_1024 = -0.000514642 + 1.00011 * (_ctx_1024t + 0.3 * jax.random.normal(jax.random.fold_in(_rk, 611), (2, 77, 128), jnp.float32))
        _validS = jnp.arange(512)[None, :] < _lenS[:, None]
        _validS2 = jnp.arange(77)[None, :] < _lenS2[:, None]
        _causal = jnp.tril(jnp.ones((512, 512), dtype=bool))
        mask_BxS2_bk0 = jnp.logical_not(jnp.broadcast_to(_validS2[:, :], (2, 77)))
        return (x, ctx_1024, mask_BxS2_bk0)
    x, ctx_1024, mask_BxS2_bk0 = _rec_inputs()

    def _L0_xattn_setup():
        import jax, jax.numpy as jnp
        import numpy as np
        import math
        B, S, D, H = (1, 256, 128, 16)
        DK = D // H
        DH = 64
        LOG_T_MIN = math.log(0.1)
        LOG_T_MAX = math.log(10.0)

        def _linear(x, W, b):
            return x @ W.T + b
        key = jax.random.key(seed)
        ks = jax.random.split(key, 20)
        p = 0.02
        return {'query': jax.random.normal(ks[0], (B, S, D), jnp.float32), 'key': jax.random.normal(ks[1], (B, S, D), jnp.float32), 'value': jax.random.normal(ks[2], (B, S, D), jnp.float32), 'Wq': jax.random.normal(ks[3], (D, D), jnp.float32) * p, 'bq': jax.random.normal(ks[4], (D,), jnp.float32) * p, 'Wk': jax.random.normal(ks[5], (D, D), jnp.float32) * p, 'bk': jax.random.normal(ks[6], (D,), jnp.float32) * p, 'Wv': jax.random.normal(ks[7], (D, D), jnp.float32) * p, 'bv': jax.random.normal(ks[8], (D,), jnp.float32) * p, 'Wo': jax.random.normal(ks[9], (D, D), jnp.float32) * p, 'bo': jax.random.normal(ks[10], (D,), jnp.float32) * p, 'w1': jax.random.normal(ks[11], (DH, 3), jnp.float32) * 0.3, 'b1': jax.random.normal(ks[12], (DH,), jnp.float32) * 0.1, 'w2': jax.random.normal(ks[13], (DH, DH), jnp.float32) * 0.1, 'b2': jax.random.normal(ks[14], (DH,), jnp.float32) * 0.1, 'w3': jax.random.normal(ks[15], (1, DH), jnp.float32) * 0.1, 'b3': jnp.full((1,), (LOG_T_MIN + LOG_T_MAX) / 2, jnp.float32)}
    _L0_xattn_all = _L0_xattn_setup()
    _L0_xattn_in = {k: v for k, v in _L0_xattn_all.items() if k in ('Wq', 'bq', 'Wk', 'bk', 'Wv', 'bv', 'Wo', 'bo', 'w1', 'b1', 'w2', 'b2', 'w3', 'b3')}
    del _L0_xattn_all

    def _L0_ffn_setup():
        import jax, jax.numpy as jnp
        import numpy as np
        DIM = 128
        NUM_EXPERTS = 8
        TOP_K = 2
        HIDDEN = int(DIM * 1.5)
        key = jax.random.key(seed)
        k_x, k_r, k_w1, k_w2, k_w3 = jax.random.split(key, 5)
        B, T = (2, 512)
        s_in = 1.0 / np.sqrt(DIM)
        s_h = 1.0 / np.sqrt(HIDDEN)
        return {'x': jax.random.normal(k_x, (B, T, DIM), dtype=jnp.float32), 'Wr': jax.random.uniform(k_r, (DIM, NUM_EXPERTS), minval=-s_in, maxval=s_in, dtype=jnp.float32), 'W1': jax.random.uniform(k_w1, (NUM_EXPERTS, DIM, HIDDEN), minval=-s_in, maxval=s_in, dtype=jnp.float32), 'W2': jax.random.uniform(k_w2, (NUM_EXPERTS, HIDDEN, DIM), minval=-s_h, maxval=s_h, dtype=jnp.float32), 'W3': jax.random.uniform(k_w3, (NUM_EXPERTS, DIM, HIDDEN), minval=-s_in, maxval=s_in, dtype=jnp.float32)}
    _L0_ffn_all = _L0_ffn_setup()
    _L0_ffn_in = {k: v for k, v in _L0_ffn_all.items() if k in ('Wr', 'W1', 'W2', 'W3')}
    del _L0_ffn_all

    def _L1_xattn_setup():
        import jax, jax.numpy as jnp
        import numpy as np
        DIM = 128
        DIM_LATENT = 128
        DIM_HEAD = 64
        INNER = max(DIM, DIM_LATENT)
        HEADS = INNER // DIM_HEAD
        SCALE = DIM_HEAD ** (-0.5)
        LN_EPS = 1e-05
        RMS_EPS = 1e-08

        def layernorm(x, g, b):
            mu = jnp.mean(x, axis=-1, keepdims=True)
            var = jnp.mean(jnp.square(x - mu), axis=-1, keepdims=True)
            return (x - mu) * jax.lax.rsqrt(var + LN_EPS) * g + b

        def rmsnorm(x, gamma):
            n = jnp.linalg.norm(x, axis=-1, keepdims=True) * x.shape[-1] ** (-0.5)
            return x / jnp.maximum(n, RMS_EPS) * gamma
        key = jax.random.key(seed)
        ks = jax.random.split(key, 8)
        b, n, nl = (8, 256, 64)
        x = jax.random.normal(ks[0], (b, n, DIM), dtype=jnp.float32)
        latents = jax.random.normal(ks[1], (b, nl, DIM_LATENT), dtype=jnp.float32)
        mask = jax.random.randint(ks[2], (b, n), 0, 2).astype(bool)
        init = lambda k, shape, fan_in: jax.random.normal(k, shape, jnp.float32) * fan_in ** (-0.5)
        return {'x': x, 'latents': latents, 'mask': mask, 'ln_x_g': jnp.ones((DIM,), jnp.float32), 'ln_x_b': jnp.zeros((DIM,), jnp.float32), 'ln_l_g': jnp.ones((DIM_LATENT,), jnp.float32), 'ln_l_b': jnp.zeros((DIM_LATENT,), jnp.float32), 'q_gamma': jnp.ones((DIM_HEAD,), jnp.float32), 'k_gamma': jnp.ones((DIM_HEAD,), jnp.float32), 'W_q': init(ks[3], (DIM_LATENT, INNER), DIM_LATENT), 'W_kv': init(ks[4], (DIM, 2 * INNER), DIM), 'W_out': init(ks[5], (INNER, DIM_LATENT), INNER), 'b_out': jnp.zeros((DIM_LATENT,), jnp.float32)}
    _L1_xattn_all = _L1_xattn_setup()
    _L1_xattn_in = {k: v for k, v in _L1_xattn_all.items() if k in ('ln_x_g', 'ln_x_b', 'ln_l_g', 'ln_l_b', 'q_gamma', 'k_gamma', 'W_q', 'W_kv', 'W_out', 'b_out')}
    del _L1_xattn_all

    def _L1_ffn_setup():
        import jax, jax.numpy as jnp
        import numpy as np
        N_EXPERTS = 32
        TOP_K = 8
        N_GROUP = 4
        TOPK_GROUP = 2
        ROUTED_SCALING = 2.5

        def _gate(x, gate_w, gate_bias):
            T, E = (x.shape[0], gate_w.shape[0])
            logits = jnp.einsum('th,eh->te', x, gate_w)
            scores = jax.nn.sigmoid(logits)
            scores_choice = scores + gate_bias[None, :]
            grp = scores_choice.reshape(T, N_GROUP, E // N_GROUP)
            top2, _ = jax.lax.top_k(grp, 2)
            group_scores = top2.sum(-1)
            _, grp_idx = jax.lax.top_k(group_scores, TOPK_GROUP)
            group_mask = jax.nn.one_hot(grp_idx, N_GROUP, dtype=scores.dtype).sum(1)
            expert_mask = jnp.repeat(group_mask, E // N_GROUP, axis=1)
            masked = jnp.where(expert_mask > 0, scores_choice, 0.0)
            _, topk_idx = jax.lax.top_k(masked, TOP_K)
            topk_w = jnp.take_along_axis(scores, topk_idx, axis=1)
            topk_w = topk_w / (topk_w.sum(-1, keepdims=True) + 1e-20)
            topk_w = topk_w * ROUTED_SCALING
            return (topk_idx, topk_w)

        def _mlp(x, wg, wu, wd):
            return jnp.einsum('...i,hi->...h', jax.nn.silu(jnp.einsum('...h,ih->...i', x, wg)) * jnp.einsum('...h,ih->...i', x, wu), wd)
        key = jax.random.key(seed)
        ks = jax.random.split(key, 9)
        B, S, H, I = (2, 64, 128, 64)
        w = 0.02
        return {'hidden_states': jax.random.normal(ks[0], (B, S, H), jnp.float32), 'gate_w': jax.random.normal(ks[1], (N_EXPERTS, H), jnp.float32) * w, 'gate_bias': jax.random.normal(ks[2], (N_EXPERTS,), jnp.float32) * w, 'expert_gate': jax.random.normal(ks[3], (N_EXPERTS, I, H), jnp.float32) * w, 'expert_up': jax.random.normal(ks[4], (N_EXPERTS, I, H), jnp.float32) * w, 'expert_down': jax.random.normal(ks[5], (N_EXPERTS, H, I), jnp.float32) * w, 'shared_gate': jax.random.normal(ks[6], (2 * I, H), jnp.float32) * w, 'shared_up': jax.random.normal(ks[7], (2 * I, H), jnp.float32) * w, 'shared_down': jax.random.normal(ks[8], (H, 2 * I), jnp.float32) * w}
    _L1_ffn_all = _L1_ffn_setup()
    _L1_ffn_in = {k: v for k, v in _L1_ffn_all.items() if k in ('gate_w', 'gate_bias', 'expert_gate', 'expert_up', 'expert_down', 'shared_gate', 'shared_up', 'shared_down')}
    del _L1_ffn_all
    return {'x': x, 'ctx_1024': ctx_1024, 'mask_BxS2_bk0': mask_BxS2_bk0, 'L0_xattn_Wq': _L0_xattn_in['Wq'], 'L0_xattn_bq': _L0_xattn_in['bq'], 'L0_xattn_Wk': _L0_xattn_in['Wk'], 'L0_xattn_bk': _L0_xattn_in['bk'], 'L0_xattn_Wv': _L0_xattn_in['Wv'], 'L0_xattn_bv': _L0_xattn_in['bv'], 'L0_xattn_Wo': _L0_xattn_in['Wo'], 'L0_xattn_bo': _L0_xattn_in['bo'], 'L0_xattn_w1': _L0_xattn_in['w1'], 'L0_xattn_b1': _L0_xattn_in['b1'], 'L0_xattn_w2': _L0_xattn_in['w2'], 'L0_xattn_b2': _L0_xattn_in['b2'], 'L0_xattn_w3': _L0_xattn_in['w3'], 'L0_xattn_b3': _L0_xattn_in['b3'], 'L0_ffn_Wr': _L0_ffn_in['Wr'], 'L0_ffn_W1': _L0_ffn_in['W1'], 'L0_ffn_W2': _L0_ffn_in['W2'], 'L0_ffn_W3': _L0_ffn_in['W3'], 'L1_xattn_ln_x_g': _L1_xattn_in['ln_x_g'], 'L1_xattn_ln_x_b': _L1_xattn_in['ln_x_b'], 'L1_xattn_ln_l_g': _L1_xattn_in['ln_l_g'], 'L1_xattn_ln_l_b': _L1_xattn_in['ln_l_b'], 'L1_xattn_q_gamma': _L1_xattn_in['q_gamma'], 'L1_xattn_k_gamma': _L1_xattn_in['k_gamma'], 'L1_xattn_W_q': _L1_xattn_in['W_q'], 'L1_xattn_W_kv': _L1_xattn_in['W_kv'], 'L1_xattn_W_out': _L1_xattn_in['W_out'], 'L1_xattn_b_out': _L1_xattn_in['b_out'], 'L1_ffn_gate_w': _L1_ffn_in['gate_w'], 'L1_ffn_gate_bias': _L1_ffn_in['gate_bias'], 'L1_ffn_expert_gate': _L1_ffn_in['expert_gate'], 'L1_ffn_expert_up': _L1_ffn_in['expert_up'], 'L1_ffn_expert_down': _L1_ffn_in['expert_down'], 'L1_ffn_shared_gate': _L1_ffn_in['shared_gate'], 'L1_ffn_shared_up': _L1_ffn_in['shared_up'], 'L1_ffn_shared_down': _L1_ffn_in['shared_down']}

def reference(x, ctx_1024, mask_BxS2_bk0, L0_xattn_Wq, L0_xattn_bq, L0_xattn_Wk, L0_xattn_bk, L0_xattn_Wv, L0_xattn_bv, L0_xattn_Wo, L0_xattn_bo, L0_xattn_w1, L0_xattn_b1, L0_xattn_w2, L0_xattn_b2, L0_xattn_w3, L0_xattn_b3, L0_ffn_Wr, L0_ffn_W1, L0_ffn_W2, L0_ffn_W3, L1_xattn_ln_x_g, L1_xattn_ln_x_b, L1_xattn_ln_l_g, L1_xattn_ln_l_b, L1_xattn_q_gamma, L1_xattn_k_gamma, L1_xattn_W_q, L1_xattn_W_kv, L1_xattn_W_out, L1_xattn_b_out, L1_ffn_gate_w, L1_ffn_gate_bias, L1_ffn_expert_gate, L1_ffn_expert_up, L1_ffn_expert_down, L1_ffn_shared_gate, L1_ffn_shared_up, L1_ffn_shared_down):
    import jax
    import jax.numpy as jnp

    def _L0_xattn_ref(query, key, value, Wq, bq, Wk, bk, Wv, bv, Wo, bo, w1, b1, w2, b2, w3, b3):
        import jax, jax.numpy as jnp
        import numpy as np
        import math
        B, S, D, H = (1, 256, 128, 16)
        DK = D // H
        DH = 64
        LOG_T_MIN = math.log(0.1)
        LOG_T_MAX = math.log(10.0)

        def _linear(x, W, b):
            return x @ W.T + b
        b, sq, d = query.shape
        sk = key.shape[1]
        h, dk = (H, DK)
        Q = _linear(query, Wq, bq).reshape(b, sq, h, dk).transpose(0, 2, 1, 3)
        K = _linear(key, Wk, bk).reshape(b, sk, h, dk).transpose(0, 2, 1, 3)
        V = _linear(value, Wv, bv).reshape(b, sk, h, dk).transpose(0, 2, 1, 3)
        qk = jnp.einsum('bhqd,bhkd->bhqk', Q, K)
        scores = qk / math.sqrt(dk)
        mean_sim = scores.mean(axis=(-2, -1))
        max_sim = scores.max(axis=-1).mean(axis=-1)
        probs = jax.nn.softmax(scores, axis=-1)
        entropy_proxy = jnp.var(probs, axis=-1, ddof=1).mean(axis=-1)
        feats = jnp.stack([mean_sim, max_sim, entropy_proxy], axis=-1)
        hidden = jax.nn.gelu(_linear(feats, w1, b1), approximate=False)
        hidden = jax.nn.gelu(_linear(hidden, w2, b2), approximate=False)
        log_t = jnp.clip(_linear(hidden, w3, b3), LOG_T_MIN, LOG_T_MAX)
        t = jnp.exp(log_t)[..., None]
        attn_scores = qk / (2.0 * t)
        attn = jax.nn.softmax(attn_scores, axis=-1)
        attn = jnp.nan_to_num(attn, nan=0.0)
        out = jnp.einsum('bhqk,bhkd->bhqd', attn, V)
        out = out.transpose(0, 2, 1, 3).reshape(b, sq, d)
        return _linear(out, Wo, bo)

    def _L0_ffn_ref(x, Wr, W1, W2, W3):
        import jax, jax.numpy as jnp
        import numpy as np
        DIM = 128
        NUM_EXPERTS = 8
        TOP_K = 2
        HIDDEN = int(DIM * 1.5)
        B, T, C = x.shape
        xf = x.reshape(-1, C)
        gate_logits = xf @ Wr
        w, idx = jax.lax.top_k(gate_logits, TOP_K)
        w = jax.nn.softmax(w, axis=-1)
        comb = jnp.sum(w[:, :, None] * jax.nn.one_hot(idx, NUM_EXPERTS, dtype=w.dtype), axis=1)
        h = jnp.einsum('nc,ech->neh', xf, W1)
        g = jnp.einsum('nc,ech->neh', xf, W3)
        y = jnp.einsum('neh,ehc->nec', jax.nn.silu(h) * g, W2)
        out = jnp.einsum('nec,ne->nc', y, comb)
        return out.reshape(B, T, C)

    def _L1_xattn_ref(x, latents, mask, ln_x_g, ln_x_b, ln_l_g, ln_l_b, q_gamma, k_gamma, W_q, W_kv, W_out, b_out):
        import jax, jax.numpy as jnp
        import numpy as np
        DIM = 128
        DIM_LATENT = 128
        DIM_HEAD = 64
        INNER = max(DIM, DIM_LATENT)
        HEADS = INNER // DIM_HEAD
        SCALE = DIM_HEAD ** (-0.5)
        LN_EPS = 1e-05
        RMS_EPS = 1e-08

        def layernorm(x, g, b):
            mu = jnp.mean(x, axis=-1, keepdims=True)
            var = jnp.mean(jnp.square(x - mu), axis=-1, keepdims=True)
            return (x - mu) * jax.lax.rsqrt(var + LN_EPS) * g + b

        def rmsnorm(x, gamma):
            n = jnp.linalg.norm(x, axis=-1, keepdims=True) * x.shape[-1] ** (-0.5)
            return x / jnp.maximum(n, RMS_EPS) * gamma
        b, n, _ = x.shape
        nl = latents.shape[1]
        xn = layernorm(x, ln_x_g, ln_x_b)
        ln = layernorm(latents, ln_l_g, ln_l_b)
        q = ln @ W_q
        kv = jnp.concatenate([xn @ W_kv, ln @ W_kv], axis=1)
        k, v = (kv[..., :INNER], kv[..., INNER:])
        to_heads = lambda t: t.reshape(t.shape[0], t.shape[1], HEADS, DIM_HEAD).transpose(0, 2, 1, 3)
        q, k, v = (to_heads(q), to_heads(k), to_heads(v))
        qn = rmsnorm(q, q_gamma) * SCALE
        kn = rmsnorm(k, k_gamma)
        sim = jnp.einsum('bhid,bhjd->bhij', qn, kn)
        full_mask = jnp.pad(mask, ((0, 0), (0, nl)), constant_values=True)
        neg = -jnp.finfo(sim.dtype).max
        sim = jnp.where(full_mask[:, None, None, :], sim, neg)
        attn = jax.nn.softmax(sim.astype(jnp.float32), axis=-1).astype(sim.dtype)
        out = jnp.einsum('bhij,bhjd->bhid', attn, v)
        out = out.transpose(0, 2, 1, 3).reshape(b, nl, INNER)
        return out @ W_out + b_out

    def _L1_ffn_ref(hidden_states, gate_w, gate_bias, expert_gate, expert_up, expert_down, shared_gate, shared_up, shared_down):
        import jax, jax.numpy as jnp
        import numpy as np
        N_EXPERTS = 32
        TOP_K = 8
        N_GROUP = 4
        TOPK_GROUP = 2
        ROUTED_SCALING = 2.5

        def _gate(x, gate_w, gate_bias):
            T, E = (x.shape[0], gate_w.shape[0])
            logits = jnp.einsum('th,eh->te', x, gate_w)
            scores = jax.nn.sigmoid(logits)
            scores_choice = scores + gate_bias[None, :]
            grp = scores_choice.reshape(T, N_GROUP, E // N_GROUP)
            top2, _ = jax.lax.top_k(grp, 2)
            group_scores = top2.sum(-1)
            _, grp_idx = jax.lax.top_k(group_scores, TOPK_GROUP)
            group_mask = jax.nn.one_hot(grp_idx, N_GROUP, dtype=scores.dtype).sum(1)
            expert_mask = jnp.repeat(group_mask, E // N_GROUP, axis=1)
            masked = jnp.where(expert_mask > 0, scores_choice, 0.0)
            _, topk_idx = jax.lax.top_k(masked, TOP_K)
            topk_w = jnp.take_along_axis(scores, topk_idx, axis=1)
            topk_w = topk_w / (topk_w.sum(-1, keepdims=True) + 1e-20)
            topk_w = topk_w * ROUTED_SCALING
            return (topk_idx, topk_w)

        def _mlp(x, wg, wu, wd):
            return jnp.einsum('...i,hi->...h', jax.nn.silu(jnp.einsum('...h,ih->...i', x, wg)) * jnp.einsum('...h,ih->...i', x, wu), wd)
        orig_shape = hidden_states.shape
        H = orig_shape[-1]
        residuals = hidden_states
        x = hidden_states.reshape(-1, H)
        topk_idx, topk_w = _gate(x, gate_w, gate_bias)
        g = jnp.einsum('th,eih->eti', x, expert_gate)
        u = jnp.einsum('th,eih->eti', x, expert_up)
        outs = jnp.einsum('eti,ehi->eth', jax.nn.silu(g) * u, expert_down)
        outs_t = jnp.transpose(outs, (1, 0, 2))
        gathered = jnp.take_along_axis(outs_t, topk_idx[:, :, None], axis=1)
        final = (gathered * topk_w[:, :, None]).sum(1)
        shared = _mlp(residuals, shared_gate, shared_up, shared_down)
        return final.reshape(orig_shape) + shared
    x = x + _L0_xattn_ref(_layernorm(x, axis=-1), ctx_1024, ctx_1024, L0_xattn_Wq, L0_xattn_bq, L0_xattn_Wk, L0_xattn_bk, L0_xattn_Wv, L0_xattn_bv, L0_xattn_Wo, L0_xattn_bo, L0_xattn_w1, L0_xattn_b1, L0_xattn_w2, L0_xattn_b2, L0_xattn_w3, L0_xattn_b3)
    x = x + _L0_ffn_ref(_layernorm(x, axis=-1), L0_ffn_Wr, L0_ffn_W1, L0_ffn_W2, L0_ffn_W3)
    x = x + _L1_xattn_ref(ctx_1024, _layernorm(x, axis=-1), mask_BxS2_bk0, L1_xattn_ln_x_g, L1_xattn_ln_x_b, L1_xattn_ln_l_g, L1_xattn_ln_l_b, L1_xattn_q_gamma, L1_xattn_k_gamma, L1_xattn_W_q, L1_xattn_W_kv, L1_xattn_W_out, L1_xattn_b_out)
    x = x + _L1_ffn_ref(_layernorm(x, axis=-1), L1_ffn_gate_w, L1_ffn_gate_bias, L1_ffn_expert_gate, L1_ffn_expert_up, L1_ffn_expert_down, L1_ffn_shared_gate, L1_ffn_shared_up, L1_ffn_shared_down)
    return x

_drawn_inputs = setup_inputs


def setup_inputs(seed=0):
    import zlib

    import numpy as np

    out = dict(_drawn_inputs(seed))
    spreads = {'L1_xattn_ln_x_g': (1.0, 0.6),
     'L1_xattn_ln_x_b': (0.0, 0.8),
     'L1_xattn_ln_l_g': (1.0, 0.2),
     'L1_xattn_ln_l_b': (0.0, 0.1),
     'L1_xattn_q_gamma': (1.0, 0.596),
     'L1_xattn_k_gamma': (1.0, 0.6),
     'L1_xattn_b_out': (0.0, 0.1)}
    factors = {'L0_xattn_Wq': 8.0,
     'L0_xattn_bq': 8.0,
     'L0_xattn_Wk': 8.0,
     'L0_xattn_bk': 200.0,
     'L0_xattn_bv': 5.842,
     'L0_xattn_w1': 8.0,
     'L0_xattn_b1': 8.0,
     'L0_xattn_w2': 8.0,
     'L0_xattn_b2': 8.0,
     'L0_xattn_w3': 8.0,
     'L1_ffn_gate_w': 8.0,
     'L1_ffn_gate_bias': 8.0,
     'L1_ffn_expert_gate': 8.0,
     'L1_ffn_expert_up': 8.0,
     'L1_ffn_expert_down': 8.0,
     'L1_ffn_shared_gate': 8.0,
     'L1_ffn_shared_up': 8.0,
     'L1_ffn_shared_down': 8.0}
    for name, (base, spread) in spreads.items():
        noise = np.random.default_rng([zlib.crc32(name.encode()), seed]).standard_normal(out[name].shape)
        drawn = base * np.exp(spread * noise) if base else spread * noise
        out[name] = jnp.asarray(drawn.astype(out[name].dtype))
    for name, factor in factors.items():
        out[name] = (out[name] * factor).astype(out[name].dtype)
    return out
```

```python
from contextlib import ExitStack

import concourse.bass as bass
from concourse import mybir

F32 = mybir.dt.float32
F32R = mybir.dt.float32r
I32 = mybir.dt.int32
ALU = mybir.AluOpType
ACT = mybir.ActivationFunctionType
X_AXIS = mybir.AxisListType.X

P = 128
NB, S, D = 2, 512, 128
TB = S // P
NK = 77
H, DK = 16, 8
NG, HG = 4, 4
GW = HG * NK
NC, CW = 3, 103
MH = 64
E0, HID0 = 8, 192
E1, HID1 = 32, 64
J0 = E0 * HID0 // P
J1 = E1 * HID1 // P
HEADS1, DH1 = 2, 64
LN_EPS = 1e-5
BIG = 3.0e38
LOG_T_MIN, LOG_T_MAX = -2.302585092994046, 2.302585092994046

V_COLS = dict(bq=4, bk=4, lxg=1, lxb=1, llg=1, llb=1, qg=1, kg=1, b1=1, b2=1, w3=1, b3=1,
              w1=3 * MH, gb=E1, bo=D, bv=D, bout=D)
C_COLS = dict(ident=P, hm=HG, nlo=1, vm=NC * HG, eye=H, nlo0=1, nlo1=1)


def offsets(cols):
    at, out = 0, {}
    for name, n in cols.items():
        out[name] = slice(at, at + n)
        at += n
    return out, at


VO, NV = offsets(V_COLS)
CO, NCC = offsets(C_COLS)


def program(nc, x, ctx, mask, vecs, wa, w2t, wr, up0, wdn0, wl1, gw, up1, wdn1, consts, onehot,
            sel0, sel1, out):
    with ExitStack() as stack:
        def sb(name, shape, dt=F32):
            return stack.enter_context(nc.sbuf_tensor(name, shape, dt))

        def sem(name):
            return stack.enter_context(nc.semaphore(name))

        vec = sb("vec", [P, NV])
        cst = sb("cst", [P, NCC])
        ident = cst[:, CO["ident"]]

        def v(name):
            return vec[:, VO[name]]

        X = [sb(f"x_{n}", [P, NB * TB, D]) for n in range(4)]
        XB = sb("xb", [P, NB * TB, D])
        wa_s = sb("wa_s", [P, 4 * D])
        w2t_s = sb("w2t_s", [MH, MH])
        wqr = sb("wqr", [P, NG, 4, 32])
        wkr = sb("wkr", [P, NG, 4, 32])
        w1s = sb("w1s", [P, 3, MH])
        w3r = sb("w3r", [MH, P])
        ctx_s = sb("ctx_s", [NK, NB, D])
        mask_s = sb("mask_s", [1, NB * NK], I32)
        mneg = sb("mneg", [1, NB, NK])
        ones_row = sb("ones_row", [1, P])
        st = sb("st", [P, 5, NB * TB, 6])
        mv = sb("mv", [P, 5, NB * TB, 2])
        ve = sb("ve", [P, 5, NB * TB])
        va = sb("va", [P, 3, NB * TB])
        rstd = sb("rstd", [P, 7, NB * TB])
        mhalf = sb("mhalf", [P, 20])
        xn = sb("xn", [P, TB, D])
        onehr = sb("onehr", [H, H * NK], F32R)
        wl1_s = sb("wl1_s", [P, 4 * D])
        aoT = sb("aoT", [P, S])
        ao = sb("ao", [P, TB, D])
        gqk = sb("gqk", [P, 1])
        NW = (J1 + 1) * P
        raw = sb("raw", [P, 2, NW])
        uph = [sb(f"uph_{n}", [P, NW], F32R) for n in range(2)]
        upl = [sb(f"upl_{n}", [P, NW], F32R) for n in range(2)]
        wdn = sb("wdn", [P, NW])
        rt_s = [sb("wr_s", [P, E0]), sb("gw_s", [P, E1])]
        rth = [sb("wrh", [P, E0], F32R), sb("gwh", [P, E1], F32R)]
        rtl = [sb("wrl", [P, E0], F32R), sb("gwl", [P, E1], F32R)]
        selr = sb("selr", [2 * E1, J1 * P], F32R)
        lg = sb("lg", [P, TB, 2 * E0])
        rv = sb("rv", [P, TB, 8])
        ss = sb("ss", [P, TB + 1, 4])
        kept, stack = stack, stack.enter_context(ExitStack())
        ctxT = sb("ctxT", [P, NB, NK])
        ctxr = sb("ctxr", [P, NB, HG, NK])
        XT = sb("XT", [P, S])
        krep = sb("krep", [P, NG, NB, NK])
        ksum = sb("ksum", [P, NG, NB])
        kbd = sb("kbd", [P, NB, NG, HG, NK])
        khi = sb("khi", [P, H * NK], F32R)
        kf2 = sb("kf2", [P, H * NK])
        kst = sb("kst", [P, H * NK], F32R)
        kst2 = sb("kst2", [P, H * NK], F32R)
        tmpv = sb("tmpv", [CW, NB, NC, D])
        vbd = sb("vbd", [CW, NB, NC, NG, HG, DK + 1])
        qst = sb("qst", [P, NB, NG, S], F32R)
        qsum = sb("qsum", [P, NB, NG])
        mx = sb("mx", [P, NB, TB, H])
        sh = sb("sh", [P, 2, H, NK])
        stats = sb("stats", [P, TB * H, 6])
        sw = sb("sw", [P, 6, TB * H])
        vp = sb("vp", [P, NB, TB * H])
        pk = sb("pk", [P, NB, NG, HG])
        qk1 = sb("qk1", [P, NB, NG])
        h1 = sb("h1", [MH, NB, H])
        h2 = sb("h2", [MH, NB, H])
        lt = sb("lt", [P, NB, 2, H])
        rt = sb("rt", [P, NB, H])
        rd = sb("rd", [H, NB, H])
        rneg = sb("rneg", [H, NB])
        nm2 = sb("nm2", [H, NB, S], F32R)
        e2 = sb("e2", [CW, 2, NC, S])
        omin, onum = (sh[:, n].rearrange("p h k -> p (h k)")[:, 0:TB * H * (DK + 1)] for n in range(2))
        oden = sb("oden", [P, TB, 2, H])
        stack.close()
        stack = kept
        xth, xtl = sb("xth", [P, S], F32R), sb("xtl", [P, S], F32R)
        m8 = sb("m8", [P, TB, 8])
        rp = sb("rp", [P, TB, 2 * E0])
        sc1 = sb("sc1", [P, 8, TB, E1])
        g8 = sb("g8", [P, TB, 4, 8])
        gsm = sb("gsm", [P, 2, TB])
        comb = sb("comb", [P, TB, 2 * E1])
        cth = sb("cth", [2 * E1, S], F32R)
        ct = sb("ct", [2 * E1, S], F32R)
        sil = sb("sil", [P, 3, S])
        silw = sb("silw", [P, 2, S])
        u = sb("u", [P, 3, S])
        yT = sb("yT", [P, S])
        LT = sb("LT", [P, S])
        xc = sb("xc", [NK, NB, D])
        ctxnT = sb("ctxnT", [P, NB, NK])
        sq = sb("sq", [P, TB + 1, 2 * D])
        ssm = sb("ssm", [P, TB + 1, 4])
        rs = sb("rs", [P, TB + 1, 4])
        qkn = sb("qkn", [P, TB + 1, 2 * D])
        V1 = sb("V1", [P, TB + 1, D])
        QT = sb("QT", [P, S])
        KT = sb("KT", [P, S + NK])
        nmx = sb("nmx", [P, TB * HEADS1])
        E = sb("E", [P, 2, S + NK])
        ET = sb("ET", [P, 2, 5, P])
        den = sb("den", [P, TB * HEADS1])
        rden = sb("rden", [P, TB * HEADS1])

        PS = stack.enter_context(nc.psum_tensor("PS", [P, 8, 512], F32))

        d_x = [sem(f"d_x{b}") for b in range(NB)]
        (d_vec, d_ctx, d_wa, d_oneh, d_w0, d_sel0, d_up0, d_dn0, d_l1, d_sel1, d_up1, d_dn1, d_out) = (sem(n) for n in (
            "d_vec", "d_ctx", "d_wa", "d_oneh", "d_w0", "d_sel0", "d_up0", "d_dn0", "d_l1", "d_sel1", "d_up1",
            "d_dn1", "d_out"))
        k_raw2 = sem("k_raw2")
        dve_step, act_step, pool_step = sem("dve_step"), sem("act_step"), sem("pool_step")
        (pool_const, ve_ready, rstd_ready, xn_ready, xnT_done, xb_ready, x_done) = (sem(n) for n in (
            "pool_const", "ve_ready", "rstd_ready", "xn_ready", "xnT_done", "xb_ready", "x_done"))
        (w_small, ctxT_done, ctxT_copied, krep_mm, k_raw, k_hi, k_ready, v_mm, v_ready) = (sem(n) for n in (
            "w_small", "ctxT_done", "ctxT_copied", "krep_mm", "k_raw", "k_hi", "k_ready", "v_mm", "v_ready"))
        (XT_ready, q_mm, q_hi, q_ready, sc1_mm, sc1_out, e1_ready, feats, hid_mm, hid_act, logt_mm, logt_in,
         invt_raw, mxT_done, nm2_ready, onehot_ready, sc2_mm, e2_ready, pv_mm) = (sem(n) for n in (
             "XT_ready", "q_mm", "q_hi", "q_ready", "sc1_mm", "sc1_out", "e1_ready", "feats", "hid_mm", "hid_act",
             "logt_mm", "logt_in", "invt_raw", "mxT_done", "nm2_ready", "onehot_ready", "sc2_mm", "e2_ready",
             "pv_mm"))
        ao_ready, aoT_done, aoT_copied, oproj_mm = (sem(n) for n in (
            "ao_ready", "aoT_done", "aoT_copied", "oproj_mm"))
        (sel_ready, up_hi, up_lo, rt_hi, rt_lo, xth_ready, xtl_ready, lg_mm, gate_in, gate_exp, comb_ready, combT_done,
         cth_ready, ct_ready, hid_up, gate_up, wb_mm, sil_ready, silw_ready, u_ready, down_mm, yT_copied, y_mm) = (
             sem(n) for n in (
                 "sel_ready", "up_hi", "up_lo", "rt_hi", "rt_lo", "xth_ready", "xtl_ready", "lg_mm", "gate_in",
                 "gate_exp", "comb_ready", "combT_done", "cth_ready", "ct_ready", "hid_up", "gate_up", "wb_mm",
                 "sil_ready", "silw_ready", "u_ready", "down_mm", "yT_copied", "y_mm"))
        (cve_ready, crstd_ready, xc_ready, xcT_done, ctxn_ready, LT_ready, proj_mm, sq_ready, ssm_ready, rs_ready,
         qkn_ready, V_ready, qT_done, QT_ready, KT_ready, sc_mm, max_ready, E_ready, ET_done, ET_dve, ET_act,
         pv1_mm) = (sem(n) for n in (
             "cve_ready", "crstd_ready", "xc_ready", "xcT_done", "ctxn_ready", "LT_ready", "proj_mm", "sq_ready",
             "ssm_ready", "rs_ready", "qkn_ready", "V_ready", "qT_done", "QT_ready", "KT_ready", "sc_mm",
             "max_ready", "E_ready", "ET_done", "ET_dve", "ET_act", "pv1_mm"))

        NCH = [J0, J1 + 1]
        NWB = [J0, J1]
        NE = [E0, E1]
        WLEN = [J0 * P, NW]
        ISQ = DK ** -0.5
        NI = TB * HEADS1

        def chunks_before(layer, b):
            return (0 if layer == 0 else NB * NCH[0]) + b * NCH[layer]

        def weighted_before(layer, b):
            return (0 if layer == 0 else NB * NWB[0]) + b * NWB[layer]

        def tiles(b):
            return slice(TB * b, TB * b + TB)

        def crows(c):
            return min(CW, GW - CW * c)

        def bc(ap, shape):
            return ap.broadcast_to(shape)

        block = stack.enter_context(nc.Block())

        @block.sync
        def _(sp):
            for b in range(NB):
                sp.dma_start(X[0][:, tiles(b), :], x[S * b:S * b + S].rearrange("(t p) c -> p t c", p=P)
                             ).then_inc(d_x[b], 16)
                if b == 0:
                    sp.dma_start(ctx_s[:, :, :], ctx.rearrange("b k c -> k b c")).then_inc(d_ctx, 16)
                    sp.dma_start(mask_s[:, :], mask).then_inc(d_ctx, 16)
            sp.dma_start(raw[0:H, 1, 0:H * NK], onehot).then_inc(d_oneh, 16)
            sp.dma_start(raw[0:2 * E0, 0, 0:J0 * P], sel0).then_inc(d_sel0, 16)
            sp.dma_start(rt_s[0][:, :], wr).then_inc(d_w0, 16)
            sp.dma_start(rt_s[1][:, :], gw).then_inc(d_w0, 16)
            sp.dma_start(wdn[:, 0:J0 * D].rearrange("p (j c) -> p j c", j=J0), wdn0.rearrange("(j p) c -> p j c", p=P)
                         ).then_inc(d_dn0, 16)
            sp.wait_ge(sel_ready, 1)
            sp.dma_start(raw[:, 0, 0:J0 * P], up0[0]).then_inc(d_up0, 16)
            sp.wait_ge(onehot_ready, 1)
            sp.dma_start(raw[:, 1, 0:J0 * P], up0[1]).then_inc(d_up0, 16)
            sp.dma_start(wl1_s[:, :], wl1).then_inc(d_l1, 16)
            sp.wait_ge(up_lo, 2)
            sp.dma_start(raw[0:2 * E1, 0, 0:J1 * P], sel1).then_inc(d_sel1, 16)
            sp.wait_ge(down_mm, NB * J0)
            sp.dma_start(wdn[:, :].rearrange("p (j c) -> p j c", c=D), wdn1.rearrange("(j p) c -> p j c", p=P)
                         ).then_inc(d_dn1, 16)
            sp.dma_start(raw[:, 1, :], up1[1]).then_inc(d_up1, 16)
            sp.wait_ge(sel_ready, 2)
            sp.dma_start(raw[:, 0, :], up1[0]).then_inc(d_up1, 16)
            for b in range(NB):
                sp.wait_ge(x_done, 3 * NB + b + 1)
                sp.dma_start(out[S * b:S * b + S].rearrange("(t p) c -> p t c", p=P), X[0][:, tiles(b), :]
                             ).then_inc(d_out, 16)
            sp.wait_ge(d_out, 16 * NB)

        @block.gpsimd
        def _(pool):
            steps = [0]

            def link(ins):
                steps[0] += 1
                ins.then_inc(pool_step, 1)
                pool.wait_ge(pool_step, steps[0])

            pool.memset(mhalf[:, :], -0.5)
            pool.memset(ones_row[:, :], 1.0)
            pool.memset(rv[:, :, :], -BIG)
            pool.memset(lg[:, :, :], -BIG)
            pool.memset(ss[:, :, :], 1.0).then_inc(pool_const, 1)
            pool.wait_ge(pool_const, 1)

            def inv_std(n):
                k, b = n // NB, n % NB
                pool.wait_ge(ve_ready, n + 1)
                last = pool.tensor_tensor(rstd[:, k, tiles(b)], ve[:, k, tiles(b)], mhalf[:, 0:TB], ALU.pow)
                if k == 2:
                    link(last)
                    link(pool.tensor_tensor(va[:, 0, tiles(b)], rstd[:, 2, tiles(b)], rstd[:, 2, tiles(b)], ALU.mult))
                    link(pool.tensor_tensor(va[:, 1, tiles(b)], va[:, 0, tiles(b)], mv[:, 2, tiles(b), 1], ALU.mult))
                    link(pool.tensor_scalar(va[:, 2, tiles(b)], va[:, 1, tiles(b)], 1.0, LN_EPS, ALU.mult, ALU.add))
                    link(pool.tensor_tensor(rstd[:, 5, tiles(b)], va[:, 2, tiles(b)], mhalf[:, 0:TB], ALU.pow))
                    last = pool.tensor_tensor(rstd[:, 6, tiles(b)], rstd[:, 5, tiles(b)], rstd[:, 2, tiles(b)], ALU.mult)
                last.then_inc(rstd_ready, 1)

            def add_bias(k, b, bias, nth):
                for t in range(TB * b, TB * b + TB):
                    last = pool.tensor_tensor(XB[:, t, :], X[k][:, t, :], bias, ALU.add)
                last.then_inc(xb_ready, 1)

            def low_halves(layer):
                for n in range(2):
                    pool.wait_ge(up_hi, 2 * layer + n + 1)
                    pool.tensor_tensor(upl[n][:, 0:WLEN[layer]], raw[:, n, 0:WLEN[layer]],
                                       uph[n][:, 0:WLEN[layer]].bitcast(F32), ALU.subtract).then_inc(up_lo, 1)

            inv_std(0)
            pool.wait_ge(d_vec, 32)
            for b in range(NB):
                pool.wait_ge(d_x[b], 16)
                add_bias(0, b, v("bo"), b)
            pool.wait_ge(d_w0, 32)
            for layer in range(2):
                pool.tensor_copy(rth[layer][:, :], rt_s[layer][:, :]).then_inc(rt_hi, 1)
                pool.wait_ge(rt_hi, layer + 1)
                pool.tensor_tensor(rtl[layer][:, :], rt_s[layer][:, :], rth[layer][:, :].bitcast(F32),
                                   ALU.subtract).then_inc(rt_lo, 1)
            inv_std(1)
            low_halves(0)
            inv_std(2)
            inv_std(3)
            pool.wait_ge(cve_ready, 1)
            pool.tensor_tensor(rstd[0:NK, 4, 0:NB], ve[0:NK, 4, 0:NB], mhalf[0:NK, 0:NB], ALU.pow).then_inc(crstd_ready, 1)
            for b in range(NB):
                inv_std(4 + b)
                pool.wait_ge(x_done, NB + b + 1)
                add_bias(2, b, v("bout"), NB + b)
                if b == 0:
                    low_halves(1)
                pool.wait_ge(ssm_ready, b + 1)
                pool.tensor_tensor(rs[:, :, :].rearrange("p a b -> p (a b)"), ssm[:, :, :].rearrange("p a b -> p (a b)"),
                                   mhalf[:, 0:4 * (TB + 1)], ALU.pow).then_inc(rs_ready, 1)
            inv_std(6)
            inv_std(7)

        @block.scalar
        def _(act):
            act.dma_start(vec[:, :], vecs).then_inc(d_vec, 16)
            act.dma_start(cst[:, :], consts).then_inc(d_vec, 16)
            act.dma_start(wa_s[:, :], wa).then_inc(d_wa, 16)
            act.dma_start(w2t_s[:, :], w2t).then_inc(d_wa, 16)

            def copy(dst, src):
                return act.activation(dst, src, ACT.Copy)

            def selector(layer):
                act.wait_ge(d_sel0 if layer == 0 else d_sel1, 16)
                if layer == 1:
                    act.wait_ge(wb_mm, NB * J0)
                rows, n = 2 * NE[layer], NWB[layer] * P
                copy(selr[0:rows, 0:n], raw[0:rows, 0, 0:n]).then_inc(sel_ready, 1)

            def high_halves(layer):
                act.wait_ge(d_up0 if layer == 0 else d_up1, 32)
                if layer == 1:
                    act.wait_ge(down_mm, NB * J0)
                for n in range(2):
                    copy(uph[n][:, 0:WLEN[layer]], raw[:, n, 0:WLEN[layer]]).then_inc(up_hi, 1)

            def split_k(src, nth, ready, value):
                act.wait_ge(ready, value)
                if nth:
                    act.wait_ge(k_ready, nth)
                copy(khi[:, :], src).then_inc(k_hi, 1)

            def attention0(b):
                split_k(kbd[:, b].rearrange("p g h k -> p (g h k)"), 2 * b, k_raw, NB)
                act.wait_ge(xnT_done, b + 1)
                copy(XT[:, :], PS[:, 0, :]).then_inc(XT_ready, 1)
                for g in range(NG):
                    act.wait_ge(q_mm, NG * b + g + 1)
                    act.activation(qst[:, b, g, :], PS[:, 1 + g, :], ACT.Identity, bias=v("bq")[:, g:g + 1],
                                   accum_out=qsum[:, b, g:g + 1]).then_inc(q_hi, 1)
                for t in range(TB):
                    act.wait_ge(sc1_out, TB * b + t + 1)
                    act.activation(sh[:, t % 2, :, :], sh[:, t % 2, :, :], ACT.Exp, scale=ISQ).then_inc(e1_ready, 1)
                act.wait_ge(hid_mm, 2 * b + 1)
                act.activation(h1[:, b, :], PS[0:MH, 0, 0:H], ACT.Gelu, bias=v("b1")[0:MH, :]).then_inc(hid_act, 1)
                act.wait_ge(hid_mm, 2 * b + 2)
                act.activation(h2[:, b, :], PS[0:MH, 1, 0:H], ACT.Gelu, bias=v("b2")[0:MH, :]).then_inc(hid_act, 1)
                act.wait_ge(logt_in, b + 1)
                act.activation(rt[:, b, :], lt[:, b, 1, :], ACT.Exp, scale=-1.0).then_inc(invt_raw, 1)
                split_k(kf2[:, :], 2 * b + 1, k_raw2, b + 1)
                for g in range(NG):
                    for c in range(NC):
                        i = NG * NC * b + NC * g + c
                        act.wait_ge(sc2_mm, i + 1)
                        if NG * b + g >= 2:
                            act.wait_ge(pv_mm, NG * b + g - 1)
                        r = crows(c)
                        act.activation(e2[0:r, g % 2, c, :], PS[0:r, NC * (g % 2) + c, :], ACT.Exp).then_inc(e2_ready, 1)
                act.wait_ge(aoT_done, b + 1)
                copy(aoT[:, :], PS[:, 0, :]).then_inc(aoT_copied, 1)

            def experts(layer, b):
                f = NB * layer + b
                act.wait_ge(xnT_done, NB * (2 * layer + 1) + b + 1)
                copy(xth[:, :], PS[:, 7, :]).then_inc(xth_ready, 1)
                act.wait_ge(gate_in, f + 1)
                if layer == 0:
                    act.activation(sc1[:, 1, :, 0:E0], sc1[:, 0, :, 0:E0], ACT.Exp).then_inc(gate_exp, 1)
                else:
                    act.activation(sc1[:, 1, :, :], sc1[:, 0, :, :], ACT.Exp, scale=-1.0).then_inc(gate_exp, 1)
                at = chunks_before(layer, b)

                def silu(j):
                    act.wait_ge(hid_up, at + j + 1)
                    if at + j >= 3:
                        act.wait_ge(u_ready, at + j - 2)
                    act.activation(sil[:, (at + j) % 3, :], PS[:, (at + j) % 2, :], ACT.Silu).then_inc(sil_ready, 1)

                silu(0)
                act.wait_ge(combT_done, f + 1)
                r = 2 * NE[layer]
                copy(cth[0:r, :], PS[0:r, 7, :]).then_inc(cth_ready, 1)
                for j in range(1, NCH[layer]):
                    silu(j)
                act.wait_ge(down_mm, at + NCH[layer])
                copy(yT[:, :], PS[:, 6, :]).then_inc(yT_copied, 1)

            def attention1(b):
                act.wait_ge(xnT_done, 2 * NB + b + 1)
                act.activation(LT[:, :], PS[:, 7, :], ACT.Identity, bias=v("llb"), scale=v("llg")).then_inc(LT_ready, 1)
                if b == 0:
                    act.wait_ge(xcT_done, 1)
                    act.activation(ctxnT[:, :, :].rearrange("p b k -> p (b k)"), PS[:, 6, 0:NB * NK], ACT.Identity,
                                   bias=v("lxb"), scale=v("lxg")).then_inc(ctxn_ready, 1)
                for t in range(TB + 1):
                    act.wait_ge(proj_mm, (TB + 1) * b + t + 1)
                    if t < TB:
                        act.activation(sq[:, t, :], PS[:, t, 0:2 * D], ACT.Square).then_inc(sq_ready, 1)
                    else:
                        act.activation(sq[0:NK, t, 0:D], PS[0:NK, t, 0:D], ACT.Square).then_inc(sq_ready, 1)
                copy(V1[:, 0:TB, :], PS[:, 0:TB, 2 * D:3 * D])
                copy(V1[0:NK, TB, :], PS[0:NK, TB, D:2 * D]).then_inc(V_ready, 1)
                act.wait_ge(qT_done, b + 1)
                copy(KT[:, 0:S], PS[:, 6, :])
                copy(KT[:, S:S + NK], PS[:, 7, 0:NK]).then_inc(KT_ready, 1)

                def last_keys(i):
                    act.wait_ge(ET_done, NI * b + i + 1)
                    if NI * b + i >= 2:
                        act.wait_ge(pv1_mm, NI * b + i - 1)
                    copy(ET[0:NK, i % 2, 4, :], PS[0:NK, 5, 0:P]).then_inc(ET_act, 1)

                for i in range(NI):
                    act.wait_ge(max_ready, NI * b + i + 1)
                    if NI * b + i >= 2:
                        act.wait_ge(ET_done, NI * b + i - 1)
                    act.activation(E[:, i % 2, :], PS[:, 2 * (i % 2):2 * (i % 2) + 2, :].rearrange("p a n -> p (a n)")[:, 0:S + NK],
                                   ACT.Exp, bias=nmx[:, i:i + 1], accum_out=den[:, i:i + 1]).then_inc(E_ready, 1)
                    if i >= 1:
                        last_keys(i - 1)
                last_keys(NI - 1)
                act.wait_ge(aoT_done, NB + b + 1)
                copy(aoT[:, :], PS[:, 7, :]).then_inc(aoT_copied, 1)

            act.wait_ge(d_oneh, 16)
            copy(onehr[:, :], raw[0:H, 1, 0:H * NK]).then_inc(onehot_ready, 1)
            selector(0)
            attention0(0)
            high_halves(0)
            attention0(1)
            for b in range(NB):
                experts(0, b)
            selector(1)
            high_halves(1)
            for b in range(NB):
                attention1(b)
            for b in range(NB):
                experts(1, b)

        @block.tensor
        def _(pe):
            def transposed(n, bank, free):
                pe.wait_ge(xn_ready, n + 1)
                for sem_, value in free:
                    pe.wait_ge(sem_, value)
                for t in range(TB):
                    last = pe.transpose(PS[:, bank, P * t:P * t + P], xn[:, t, :], ident)
                last.then_inc(xnT_done, 1)

            def project_out(n, bank_t, bank_o, w, free):
                pe.wait_ge(ao_ready, n + 1)
                for sem_, value in free:
                    pe.wait_ge(sem_, value)
                for t in range(TB):
                    last = pe.transpose(PS[:, bank_t, P * t:P * t + P], ao[:, t, :], ident)
                last.then_inc(aoT_done, 1)
                pe.wait_ge(aoT_copied, n + 1)
                for t in range(TB):
                    last = pe.matmul(PS[:, bank_o, P * t:P * t + P], aoT[:, P * t:P * t + P], w, start=True, stop=True)
                last.then_inc(oproj_mm, 1)

            def attention0(b):
                transposed(b, 0, [(ctxT_copied, 2)] if b == 0 else [(x_done, b), (xn_ready, b + 1)])
                pe.wait_ge(XT_ready, b + 1)
                if b == 0:
                    pe.wait_ge(k_raw, NB)
                    pe.wait_ge(v_ready, 1)
                for g in range(NG):
                    pe.matmul(PS[:, 1 + g, :], wqr[:, g].rearrange("p a j -> p (a j)"), XT[:, :], start=True,
                              stop=True).then_inc(q_mm, 1)
                pe.wait_ge(k_ready, 2 * b + 1)
                for t in range(TB):
                    if t < 2:
                        pe.wait_ge(q_ready, NG * (b + 1))
                    else:
                        pe.wait_ge(sc1_out, TB * b + t - 1)
                    for g in range(NG):
                        last = pe.matmul(PS[:, 4 * (t % 2) + g, 0:GW], qst[:, b, g, P * t:P * t + P],
                                         kst[:, GW * g:GW * g + GW], start=True, stop=True)
                    last.then_inc(sc1_mm, 1)
                pe.wait_ge(sc1_out, TB * (b + 1))
                for t in range(TB):
                    last = pe.transpose(PS[0:H, 3, P * t:P * t + P], mx[:, b, t, :], ident)
                last.then_inc(mxT_done, 1)
                pe.wait_ge(feats, b + 1)
                pe.matmul(PS[0:MH, 0, 0:H], w1s[:, 0, :], pk[:, b].rearrange("p g h -> p (g h)"), start=True, stop=False)
                for t in range(TB):
                    pe.matmul(PS[0:MH, 0, 0:H], w1s[:, 1, :], mx[:, b, t, :], start=False, stop=False)
                for t in range(TB):
                    last = pe.matmul(PS[0:MH, 0, 0:H], w1s[:, 2, :], vp[:, b, H * t:H * t + H], start=False,
                                     stop=(t == TB - 1))
                last.then_inc(hid_mm, 1)
                pe.wait_ge(hid_act, 2 * b + 1)
                pe.matmul(PS[0:MH, 1, 0:H], w2t_s[:, :], h1[:, b, :], start=True, stop=True).then_inc(hid_mm, 1)
                pe.wait_ge(hid_act, 2 * b + 2)
                pe.matmul(PS[:, 2, 0:H], w3r[:, :], h2[:, b, :], start=True, stop=True).then_inc(logt_mm, 1)
                pe.wait_ge(nm2_ready, b + 1)
                pe.wait_ge(onehot_ready, 1)
                pe.wait_ge(k_ready, 2 * b + 2)

                def values(g):
                    pe.wait_ge(e2_ready, NG * NC * b + NC * (g + 1))
                    for t in range(TB):
                        at = (t % 2) * H * (DK + 1) + g * HG * (DK + 1)
                        for c in range(NC):
                            r = crows(c)
                            last = pe.matmul(PS[:, 6 + t // 2, at:at + HG * (DK + 1)], e2[0:r, g % 2, c, P * t:P * t + P],
                                             vbd[0:r, b, c, g].rearrange("p h d -> p (h d)"), start=(c == 0),
                                             stop=(c == NC - 1))
                    last.then_inc(pv_mm, 1)

                for g in range(NG):
                    for c in range(NC):
                        if g >= 2:
                            pe.wait_ge(e2_ready, NG * NC * b + NC * (g - 2) + c + 1)
                        r, at = crows(c), GW * g + CW * c
                        bank = PS[0:r, NC * (g % 2) + c, :]
                        pe.matmul(bank, kst2[:, at:at + r], qst[:, b, g, :], start=True, stop=False)
                        pe.matmul(bank, onehr[:, at:at + r], nm2[:, b, :], start=False, stop=True).then_inc(sc2_mm, 1)
                    if g >= 1:
                        values(g - 1)
                values(NG - 1)
                project_out(b, 0, 1, wa_s[:, 3 * D:4 * D], [(e2_ready, NG * NC * (b + 1))])

            def split_mm(bank, wh, wl):
                pe.matmul(bank, wh, xth[:, :], start=True, stop=False)
                pe.matmul(bank, wl, xth[:, :], start=False, stop=False)
                return pe.matmul(bank, wh, xtl[:, :], start=False, stop=True)

            def experts(layer, b):
                f = NB * layer + b
                transposed(NB * (2 * layer + 1) + b, 7, [(x_done, NB * (2 * layer + 1) + b)] if b else
                           [(x_done, NB * (2 * layer + 1))])
                pe.wait_ge(rt_lo, layer + 1)
                pe.wait_ge(xtl_ready, f + 1)
                n = NE[layer]
                for t in range(TB):
                    lg_bank = PS[:, 7, n * t:n * t + n]
                    for i, (a, w) in enumerate([(xth, rth), (xtl, rth), (xth, rtl), (xtl, rtl)]):
                        last = pe.matmul(lg_bank, a[:, P * t:P * t + P], w[layer][:, :], start=(i == 0), stop=(i == 3))
                last.then_inc(lg_mm, 1)
                at, wat = chunks_before(layer, b), weighted_before(layer, b)
                pe.wait_ge(up_hi, 2 * layer + 2)
                pe.wait_ge(up_lo, 2 * layer + 2)

                def up(j):
                    i, c = at + j, slice(P * j, P * j + P)
                    if i >= 2:
                        pe.wait_ge(sil_ready, i - 1)
                    split_mm(PS[:, i % 2, :], uph[0][:, c], upl[0][:, c]).then_inc(hid_up, 1)
                    if i >= 2:
                        pe.wait_ge(u_ready, i - 1)
                    split_mm(PS[:, 4 + i % 2, :], uph[1][:, c], upl[1][:, c]).then_inc(gate_up, 1)

                def weights(j):
                    i = at + j
                    if j >= NWB[layer]:
                        return
                    if i >= 2:
                        pe.wait_ge(u_ready, i - 1)
                    pe.matmul(PS[:, 2 + i % 2, :], selr[0:2 * n, P * j:P * j + P], ct[0:2 * n, :], start=True,
                              stop=True).then_inc(wb_mm, 1)

                def down(j):
                    pe.wait_ge(u_ready, at + j + 1)
                    pe.matmul(PS[:, 6, :], wdn[:, D * j:D * j + D], u[:, (at + j) % 3, :], start=(j == 0),
                              stop=(j == NCH[layer] - 1)).then_inc(down_mm, 1)

                up(0)
                pe.wait_ge(comb_ready, f + 1)
                for t in range(TB):
                    last = pe.transpose(PS[0:2 * n, 7, P * t:P * t + P], comb[:, t, 0:2 * n], ident)
                last.then_inc(combT_done, 1)
                up(1)
                pe.wait_ge(sel_ready, layer + 1)
                pe.wait_ge(ct_ready, f + 1)
                weights(0)
                weights(1)
                pe.wait_ge(d_dn0 if layer == 0 else d_dn1, 16)
                for j in range(2, NCH[layer]):
                    up(j)
                    weights(j)
                    down(j - 2)
                down(NCH[layer] - 2)
                down(NCH[layer] - 1)
                pe.wait_ge(yT_copied, f + 1)
                for t in range(TB):
                    last = pe.transpose(PS[:, 7, P * t:P * t + P], yT[:, P * t:P * t + P], ident)
                last.then_inc(y_mm, 1)

            def attention1(b):
                transposed(2 * NB + b, 7, [(x_done, 2 * NB + b)])
                if b == 0:
                    pe.wait_ge(xc_ready, 1)
                    for k in range(NB):
                        last = pe.transpose(PS[:, 6, NK * k:NK * k + NK], xc[:, k, :], ident[0:NK, 0:NK])
                    last.then_inc(xcT_done, 1)
                    pe.wait_ge(d_l1, 16)
                pe.wait_ge(LT_ready, b + 1)
                for t in range(TB):
                    pe.matmul(PS[:, t, 0:3 * D], LT[:, P * t:P * t + P], wl1_s[:, 0:3 * D], start=True,
                              stop=True).then_inc(proj_mm, 1)
                pe.wait_ge(ctxn_ready, 1)
                pe.matmul(PS[0:NK, TB, 0:2 * D], ctxnT[:, b, :], wl1_s[:, D:3 * D], start=True, stop=True).then_inc(proj_mm, 1)
                pe.wait_ge(qkn_ready, b + 1)
                for t in range(TB):
                    pe.transpose(PS[:, 5, P * t:P * t + P], qkn[:, t, 0:D], ident)
                for t in range(TB):
                    pe.transpose(PS[:, 6, P * t:P * t + P], qkn[:, t, D:2 * D], ident)
                pe.transpose(PS[:, 7, 0:NK], qkn[0:NK, TB, 0:D], ident[0:NK, 0:NK]).then_inc(qT_done, 1)
                pe.wait_ge(QT_ready, b + 1)
                pe.wait_ge(KT_ready, b + 1)
                pe.wait_ge(V_ready, b + 1)

                def scores(i):
                    t, h = i // HEADS1, i % HEADS1
                    hs, bank = slice(DH1 * h, DH1 * h + DH1), 2 * (i % 2)
                    if i >= 2:
                        pe.wait_ge(E_ready, NI * b + i - 1)
                    q = QT[hs, P * t:P * t + P]
                    pe.matmul(PS[:, bank, :], q, KT[hs, 0:S], start=True, stop=True)
                    pe.matmul(PS[:, bank + 1, 0:NK], q, KT[hs, S:S + NK], start=True, stop=False)
                    pe.matmul(PS[:, bank + 1, 0:NK], ones_row[:, :], mneg[:, b, :], start=False, stop=True).then_inc(sc_mm, 1)

                def turn(i):
                    pe.wait_ge(E_ready, NI * b + i + 1)
                    if NI * b + i >= 1:
                        pe.wait_ge(ET_dve, NI * b + i)
                        pe.wait_ge(ET_act, NI * b + i)
                    for c in range(TB):
                        pe.transpose(PS[:, 4, P * c:P * c + P], E[:, i % 2, P * c:P * c + P], ident)
                    pe.transpose(PS[0:NK, 5, 0:P], E[:, i % 2, S:S + NK], ident).then_inc(ET_done, 1)

                def values(i):
                    h = i % HEADS1
                    pe.wait_ge(ET_dve, NI * b + i + 1)
                    pe.wait_ge(ET_act, NI * b + i + 1)
                    for c in range(TB + 1):
                        r = P if c < TB else NK
                        last = pe.matmul(PS[:, 6, DH1 * i:DH1 * i + DH1], ET[0:r, i % 2, c, :],
                                         V1[0:r, c, DH1 * h:DH1 * h + DH1], start=(c == 0), stop=(c == TB))
                    last.then_inc(pv1_mm, 1)

                scores(0)
                for i in range(NI):
                    if i + 1 < NI:
                        scores(i + 1)
                    turn(i)
                    if i >= 1:
                        values(i - 1)
                values(NI - 1)
                project_out(NB + b, 7, 0, wl1_s[:, 3 * D:4 * D], [])

            pe.wait_ge(d_vec, 32)
            pe.wait_ge(d_ctx, 32)
            for b in range(NB):
                last = pe.transpose(PS[:, 0, NK * b:NK * b + NK], ctx_s[:, b, :], ident[0:NK, 0:NK])
            last.then_inc(ctxT_done, 1)
            pe.wait_ge(w_small, 1)
            pe.wait_ge(ctxT_copied, 2)
            for g in range(NG):
                last = pe.matmul(PS[:, 1 + g // 2, NB * NK * (g % 2):NB * NK * (g % 2 + 1)],
                                 wkr[:, g].rearrange("p a j -> p (a j)"), ctxT[:, :, :].rearrange("p b k -> p (b k)"),
                                 start=True, stop=True)
            last.then_inc(krep_mm, 1)
            for b in range(NB):
                for c in range(NC):
                    n, r = NC * b + c, crows(c)
                    last = pe.matmul(PS[0:r, 3 + n // 4, D * (n % 4):D * (n % 4) + D],
                                     ctxr[:, b].rearrange("p h k -> p (h k)")[:, CW * c:CW * c + r], wa_s[:, 2 * D:3 * D],
                                     start=True, stop=True)
            last.then_inc(v_mm, 1)
            for b in range(NB):
                attention0(b)
            for b in range(NB):
                experts(0, b)
            for b in range(NB):
                attention1(b)
            for b in range(NB):
                experts(1, b)

        @block.vector
        def _(dve):
            steps = [0]

            def link(ins):
                steps[0] += 1
                ins.then_inc(dve_step, 1)
                dve.wait_ge(dve_step, steps[0])

            def norm(n):
                k, b = n // NB, n % NB
                if k == 0:
                    dve.wait_ge(d_x[b], 16)
                for t in range(TB * b, TB * b + TB):
                    last = dve.bn_stats(st[:, k, t, :], X[k][:, t, :])
                link(last)
                for t in range(TB * b, TB * b + TB):
                    last = dve.bn_aggr(mv[:, k, t, :], st[:, k, t, :])
                link(last)
                dve.tensor_scalar(ve[:, k, tiles(b)], mv[:, k, tiles(b), 1], LN_EPS, None, ALU.add).then_inc(ve_ready, 1)
                dve.wait_ge(rstd_ready, n + 1)
                if n:
                    dve.wait_ge(xnT_done, n)
                r = 6 if k == 2 else k
                for t in range(TB):
                    last = dve.tensor_scalar(xn[:, t, :], X[k][:, TB * b + t, :], mv[:, k, TB * b + t, 0:1],
                                             rstd[:, r, TB * b + t:TB * b + t + 1], ALU.subtract, ALU.mult)
                last.then_inc(xn_ready, 1)

            def small_weights():
                dve.wait_ge(d_vec, 32)
                dve.wait_ge(d_wa, 32)
                for dst, n in ((wqr, 0), (wkr, 1)):
                    dve.tensor_copy(dst[:, :, :, :], bc(wa_s[:, D * n:D * n + D].rearrange("p (g j) -> p g j", g=NG)
                                                        .unsqueeze(2), [P, NG, 4, 32]))
                for n, c in enumerate((ISQ / (S * NK * 4), ISQ / S, 1.0 / (S * (NK - 1)))):
                    dve.tensor_scalar(w1s[:, n, :], v("w1")[:, MH * n:MH * n + MH], c, None, ALU.mult)
                dve.tensor_copy(w3r[:, :], bc(v("w3")[0:MH, :], [MH, P]))
                dve.scalar_tensor_tensor(gqk[:, :], v("qg"), DH1 ** -0.5, v("kg"), ALU.mult, ALU.mult).then_inc(w_small, 1)

            def keys_and_values():
                dve.wait_ge(ctxT_done, 1)
                src = PS[:, 0, 0:NB * NK].rearrange("p (b k) -> p b k", b=NB)
                dve.tensor_copy(ctxT[:, :, :], src).then_inc(ctxT_copied, 1)
                dve.tensor_copy(ctxr[:, :, :, :], bc(src.unsqueeze(2), [P, NB, HG, NK])).then_inc(ctxT_copied, 1)
                dve.wait_ge(krep_mm, 1)
                for g in range(NG):
                    last = dve.tensor_scalar(krep[:, g].rearrange("p b k -> p (b k)"),
                                             PS[:, 1 + g // 2, NB * NK * (g % 2):NB * NK * (g % 2 + 1)],
                                             v("bk")[:, g:g + 1], None, ALU.add)
                link(last)
                dve.tensor_reduce(ksum[:, :, :], krep[:, :, :, :], X_AXIS, ALU.add)
                for b in range(NB):
                    for g in range(NG):
                        last = dve.tensor_tensor(kbd[:, b, g], bc(krep[:, g, b, :].unsqueeze(1), [P, HG, NK]),
                                                 bc(cst[:, CO["hm"]].unsqueeze(2), [P, HG, NK]), ALU.mult)
                    last.then_inc(k_raw, 1)
                dve.wait_ge(v_mm, 1)
                for b in range(NB):
                    for c in range(NC):
                        n, r = NC * b + c, crows(c)
                        last = dve.tensor_tensor(tmpv[0:r, b, c, :], PS[0:r, 3 + n // 4, D * (n % 4):D * (n % 4) + D],
                                                 v("bv")[0:r, :], ALU.add)
                link(last)
                for b in range(NB):
                    for c in range(NC):
                        r = crows(c)
                        own = cst[0:r, CO["vm"]].rearrange("p (c h) -> p c h", c=NC)[:, c, :]
                        dve.tensor_copy(vbd[0:r, b, c, :, :, DK], bc(own.unsqueeze(1), [r, NG, HG]))
                        last = dve.tensor_tensor(vbd[0:r, b, c, :, :, 0:DK],
                                                 tmpv[0:r, b, c, :].rearrange("p (g h d) -> p g h d", g=NG, h=HG),
                                                 bc(own.unsqueeze(1).unsqueeze(3), [r, NG, HG, DK]), ALU.mult)
                last.then_inc(v_ready, 1)

            def attention0(b):
                dve.wait_ge(k_hi, 2 * b + 1)
                dve.scalar_tensor_tensor(kst[:, :], khi[:, :].bitcast(F32), cst[:, CO["nlo"]],
                                         kbd[:, b].rearrange("p g h k -> p (g h k)"), ALU.mult, ALU.add
                                         ).then_inc(k_ready, 1)
                lo = slice(64, 128)
                for g in range(NG):
                    dve.wait_ge(q_hi, NG * b + g + 1)
                    dve.scalar_tensor_tensor(qst[lo, b, g, :], PS[lo, 1 + g, :], v("bq")[lo, g:g + 1],
                                             qst[lo, b, g, :].bitcast(F32), ALU.add, ALU.subtract).then_inc(q_ready, 1)

                def spread(t):
                    dve.wait_ge(e1_ready, TB * b + t + 1)
                    for h in range(H):
                        last = dve.bn_stats(stats[:, H * t + h, :], sh[:, t % 2, h, :])
                    link(last)

                for t in range(TB):
                    dve.wait_ge(sc1_mm, TB * b + t + 1)
                    sc = PS[:, 4 * (t % 2):4 * (t % 2) + 4, 0:GW].rearrange("p g (h k) -> p g h k", k=NK)
                    m = mx[:, b, t, :].rearrange("p (g h) -> p g h", g=NG)
                    link(dve.tensor_reduce(m, sc, X_AXIS, ALU.max))
                    dve.tensor_tensor(sh[:, t % 2].rearrange("p (g h) k -> p g h k", g=NG), sc,
                                      bc(m.unsqueeze(3), [P, NG, HG, NK]), ALU.subtract).then_inc(sc1_out, 1)
                    if t >= 1:
                        spread(t - 1)
                spread(TB - 1)
                me, s2e, mo, s2o = (stats[:, :, n] for n in (1, 2, 4, 5))
                ne, no = (NK + 1) // 2, NK // 2
                link(dve.tensor_scalar(sw[:, 0, :], me, float(ne), None, ALU.mult))
                link(dve.scalar_tensor_tensor(sw[:, 1, :], mo, float(no), sw[:, 0, :], ALU.mult, ALU.add))
                link(dve.tensor_tensor(sw[:, 2, :], me, mo, ALU.subtract))
                link(dve.scalar_tensor_tensor(sw[:, 3, :], sw[:, 2, :], ne * no / NK, sw[:, 2, :], ALU.mult, ALU.mult))
                link(dve.tensor_tensor(sw[:, 4, :], s2e, sw[:, 3, :], ALU.add))
                link(dve.tensor_tensor(sw[:, 5, :], s2o, sw[:, 4, :], ALU.add))
                link(dve.reciprocal(sw[:, 0, :], sw[:, 1, :]))
                link(dve.tensor_tensor(sw[:, 2, :], sw[:, 5, :], sw[:, 0, :], ALU.mult))
                dve.tensor_tensor(vp[:, b, :], sw[:, 2, :], sw[:, 0, :], ALU.mult)
                link(dve.tensor_tensor(qk1[:, b, :], qsum[:, b, :], ksum[:, :, b], ALU.mult))
                dve.tensor_tensor(pk[:, b], bc(qk1[:, b, :].unsqueeze(2), [P, NG, HG]),
                                  bc(cst[:, CO["hm"]].unsqueeze(1), [P, NG, HG]), ALU.mult).then_inc(feats, 1)
                dve.wait_ge(logt_mm, b + 1)
                link(dve.tensor_scalar(lt[:, b, 0, :], PS[:, 2, 0:H], v("b3"), LOG_T_MIN, ALU.add, ALU.max))
                dve.tensor_scalar(lt[:, b, 1, :], lt[:, b, 0, :], LOG_T_MAX, None, ALU.min).then_inc(logt_in, 1)
                dve.wait_ge(invt_raw, b + 1)
                link(dve.tensor_scalar(rt[:, b, :], rt[:, b, :], 0.5, None, ALU.mult))
                dve.tensor_tensor(kf2[:, :].rearrange("p (h k) -> p h k", k=NK),
                                  kbd[:, b].rearrange("p g h k -> p (g h) k"),
                                  bc(rt[:, b, :].unsqueeze(2), [P, H, NK]), ALU.mult).then_inc(k_raw2, 1)
                link(dve.tensor_tensor(rd[:, b, :], rt[0:H, b, :], cst[0:H, CO["eye"]], ALU.mult))
                link(dve.tensor_reduce(rneg[:, b:b + 1], rd[:, b, :], X_AXIS, ALU.add, negate=True))
                dve.wait_ge(mxT_done, b + 1)
                dve.tensor_scalar(nm2[:, b, :], PS[0:H, 3, :], rneg[:, b:b + 1], None, ALU.mult).then_inc(nm2_ready, 1)
                dve.wait_ge(k_hi, 2 * b + 2)
                dve.scalar_tensor_tensor(kst2[:, :], khi[:, :].bitcast(F32), cst[:, CO["nlo"]], kf2[:, :], ALU.mult,
                                         ALU.add).then_inc(k_ready, 1)
                dve.wait_ge(pv_mm, NG * (b + 1))
                raw_o = PS[:, 6:8, 0:2 * H * (DK + 1)]
                om, on = (m.rearrange("p (a n) -> p a n", a=2) for m in (omin, onum))
                nums = onum.rearrange("p (t h d) -> p t h d", t=TB, h=H)
                link(dve.tensor_scalar(om, raw_o, 0.0, None, ALU.min))
                link(dve.scalar_tensor_tensor(on, raw_o, 0.0, om, ALU.max, ALU.add))
                link(dve.tensor_scalar(oden[:, :, 0, :], nums[:, :, :, DK], 1e-30, None, ALU.max))
                link(dve.reciprocal(oden[:, :, 1, :], oden[:, :, 0, :]))
                dve.tensor_tensor(ao[:, :, :].rearrange("p t (h d) -> p t h d", h=H), nums[:, :, :, 0:DK],
                                  bc(oden[:, :, 1, :].unsqueeze(3), [P, TB, H, DK]), ALU.mult).then_inc(ao_ready, 1)
                residual(1, b, PS[:, 1, :], oproj_mm, b + 1, xb=b + 1)

            def residual(k, b, bank, ready, value, xb=None):
                dve.wait_ge(ready, value)
                src = X[k - 1]
                if xb is not None:
                    dve.wait_ge(xb_ready, xb)
                    src = XB
                dst = X[k % 4]
                dve.tensor_tensor(dst[:, tiles(b), :], src[:, tiles(b), :], bank.rearrange("p (t c) -> p t c", t=TB),
                                  ALU.add).then_inc(x_done, 1)
                dve.wait_ge(x_done, NB * (k - 1) + b + 1)

            def gate_top2(b):
                n = E0
                link(dve.tensor_copy(lg[:, :, 0:n], PS[:, 7, 0:TB * n].rearrange("p (t e) -> p t e", t=TB)))
                for t in range(TB):
                    last = dve.max(m8[:, t, :], lg[:, t, 0:n])
                link(last)
                link(dve.tensor_copy(rv[:, :, 0:2], m8[:, :, 0:2]))
                for t in range(TB):
                    last = dve.match_replace(rp[:, t, :], rv[:, t, :], lg[:, t, :], BIG)
                dve.tensor_tensor(sc1[:, 0, :, 0:n], lg[:, :, 0:n], bc(m8[:, :, 0:1], [P, TB, n]), ALU.subtract
                                  ).then_inc(gate_in, 1)
                dve.wait_ge(gate_in, b + 1)
                link(dve.tensor_tensor(sc1[:, 2, :, 0:n], rp[:, :, 0:n], lg[:, :, 0:n], ALU.not_equal))
                dve.wait_ge(gate_exp, b + 1)
                link(dve.tensor_tensor(sc1[:, 3, :, 0:n], sc1[:, 1, :, 0:n], sc1[:, 2, :, 0:n], ALU.mult))
                link(dve.tensor_reduce(gsm[:, 0, :], sc1[:, 3, :, 0:n], X_AXIS, ALU.add))
                link(dve.reciprocal(gsm[:, 1, :], gsm[:, 0, :]))
                copies = comb[:, :, 0:2 * n].rearrange("p t (a e) -> p t a e", a=2)
                dve.tensor_tensor(copies, bc(sc1[:, 3, :, 0:n].unsqueeze(2), [P, TB, 2, n]),
                                  bc(gsm[:, 1, :].unsqueeze(2).unsqueeze(3), [P, TB, 2, n]), ALU.mult).then_inc(comb_ready, 1)

            def gate_groups(b):
                n, ng = E1, 4
                link(dve.tensor_copy(sc1[:, 0, :, :], PS[:, 7, 0:TB * n].rearrange("p (t e) -> p t e", t=TB)))
                dve.tensor_copy(gsm[:, 0, :], sc1[:, 0, :, 0]).then_inc(gate_in, 1)
                dve.wait_ge(gate_exp, NB + b + 1)
                link(dve.tensor_scalar(sc1[:, 2, :, :], sc1[:, 1, :, :], 1.0, None, ALU.add))
                link(dve.reciprocal(sc1[:, 3, :, :], sc1[:, 2, :, :]))
                link(dve.tensor_tensor(sc1[:, 4, :, :], sc1[:, 3, :, :], bc(v("gb").unsqueeze(1), [P, TB, n]), ALU.add))
                for t in range(TB):
                    for g in range(ng):
                        last = dve.max(g8[:, t, g, :], sc1[:, 4, t, 8 * g:8 * g + 8])
                link(last)
                dve.memset(lg[:, :, ng:E0], -BIG)
                link(dve.tensor_tensor(lg[:, :, 0:ng], g8[:, :, :, 0], g8[:, :, :, 1], ALU.add))
                for t in range(TB):
                    last = dve.max(m8[:, t, :], lg[:, t, 0:8])
                link(last)
                link(dve.tensor_copy(rv[:, :, 0:2], m8[:, :, 0:2]))
                for t in range(TB):
                    last = dve.match_replace(rp[:, t, :], rv[:, t, :], lg[:, t, :], BIG)
                link(last)
                link(dve.tensor_tensor(rp[:, :, 8:8 + ng], rp[:, :, 0:ng], lg[:, :, 0:ng], ALU.not_equal))
                for t in range(TB):
                    last = dve.tensor_tensor(sc1[:, 5, t, :].rearrange("p (g e) -> p g e", g=ng),
                                             sc1[:, 4, t, :].rearrange("p (g e) -> p g e", g=ng),
                                             bc(rp[:, t, 8:8 + ng].unsqueeze(2), [P, ng, 8]), ALU.mult)
                link(last)
                link(dve.tensor_scalar(sc1[:, 5, :, :], sc1[:, 5, :, :], 0.0, None, ALU.add))
                for t in range(TB):
                    last = dve.max(m8[:, t, :], sc1[:, 5, t, :])
                link(last)
                for t in range(TB):
                    last = dve.match_replace(sc1[:, 6, t, :], m8[:, t, :], sc1[:, 5, t, :], BIG)
                link(last)
                link(dve.tensor_tensor(sc1[:, 7, :, :], sc1[:, 6, :, :], sc1[:, 5, :, :], ALU.not_equal))
                link(dve.tensor_tensor(sc1[:, 2, :, :], sc1[:, 7, :, :], sc1[:, 3, :, :], ALU.mult))
                link(dve.tensor_reduce(gsm[:, 0, :], sc1[:, 2, :, :], X_AXIS, ALU.add))
                link(dve.tensor_scalar(gsm[:, 0, :], gsm[:, 0, :], 1e-20, None, ALU.add))
                link(dve.reciprocal(gsm[:, 1, :], gsm[:, 0, :]))
                link(dve.tensor_scalar(gsm[:, 1, :], gsm[:, 1, :], 2.5, None, ALU.mult))
                copies = comb[:, :, :].rearrange("p t (a e) -> p t a e", a=2)
                dve.tensor_tensor(copies, bc(sc1[:, 2, :, :].unsqueeze(2), [P, TB, 2, n]),
                                  bc(gsm[:, 1, :].unsqueeze(2).unsqueeze(3), [P, TB, 2, n]), ALU.mult).then_inc(comb_ready, 1)

            def experts(layer, b):
                f = NB * layer + b
                norm(NB * (2 * layer + 1) + b)
                dve.wait_ge(xth_ready, f + 1)
                dve.tensor_tensor(xtl[:, :], PS[:, 7, :], xth[:, :].bitcast(F32), ALU.subtract).then_inc(xtl_ready, 1)
                dve.wait_ge(lg_mm, f + 1)
                (gate_top2, gate_groups)[layer](b)
                dve.wait_ge(cth_ready, f + 1)
                r = 2 * NE[layer]
                dve.scalar_tensor_tensor(ct[0:r, :], cth[0:r, :].bitcast(F32), cst[0:r, CO[f"nlo{layer}"]],
                                         PS[0:r, 7, :], ALU.mult, ALU.add).then_inc(ct_ready, 1)
                at, wat = chunks_before(layer, b), weighted_before(layer, b)
                for j in range(NCH[layer]):
                    i = at + j
                    dve.wait_ge(sil_ready, i + 1)
                    src = sil[:, i % 3, :]
                    if j < NWB[layer]:
                        dve.wait_ge(wb_mm, wat + j + 1)
                        dve.tensor_tensor(silw[:, i % 2, :], src, PS[:, 2 + i % 2, :], ALU.mult).then_inc(silw_ready, 1)
                        dve.wait_ge(silw_ready, wat + j + 1)
                        src = silw[:, i % 2, :]
                    dve.wait_ge(gate_up, i + 1)
                    if i >= 3:
                        dve.wait_ge(down_mm, i - 2)
                    dve.tensor_tensor(u[:, i % 3, :], src, PS[:, 4 + i % 2, :], ALU.mult).then_inc(u_ready, 1)
                residual(2 + 2 * layer, b, PS[:, 7, :], y_mm, f + 1)

            def context_norm():
                for b in range(NB):
                    last = dve.bn_stats(st[0:NK, 4, b, :], ctx_s[:, b, :])
                link(last)
                for b in range(NB):
                    last = dve.bn_aggr(mv[0:NK, 4, b, :], st[0:NK, 4, b, :])
                link(last)
                dve.tensor_scalar(ve[0:NK, 4, 0:NB], mv[0:NK, 4, 0:NB, 1], LN_EPS, None, ALU.add).then_inc(cve_ready, 1)
                dve.wait_ge(crstd_ready, 1)
                for b in range(NB):
                    last = dve.tensor_scalar(xc[:, b, :], ctx_s[:, b, :], mv[0:NK, 4, b, 0:1], rstd[0:NK, 4, b:b + 1],
                                             ALU.subtract, ALU.mult)
                last.then_inc(xc_ready, 1)
                dve.tensor_scalar(mneg[:, :, :].rearrange("p b k -> p (b k)"), mask_s[:, :], 1.0, 1e30, ALU.subtract, ALU.mult
                                  ).then_inc(xc_ready, 1)

            def attention1(b):
                norm(2 * NB + b)
                dve.wait_ge(sq_ready, (TB + 1) * (b + 1))
                dve.tensor_reduce(ss[:, 0:TB, :], sq[:, 0:TB, :].rearrange("p t (n d) -> p t n d", n=4), X_AXIS, ALU.add)
                link(dve.tensor_reduce(ss[0:NK, TB, 0:2], sq[0:NK, TB, 0:D].rearrange("p (n d) -> p n d", n=2), X_AXIS, ALU.add))
                dve.tensor_scalar(ssm[:, :, :], ss[:, :, :], 1.0 / DH1, 1e-16, ALU.mult, ALU.max).then_inc(ssm_ready, 1)
                dve.wait_ge(rs_ready, b + 1)
                dve.wait_ge(V_ready, b + 1)
                dve.tensor_tensor(qkn[:, 0:TB, :].rearrange("p t (n d) -> p t n d", n=4),
                                  PS[:, 0:TB, 0:2 * D].rearrange("p t (n d) -> p t n d", n=4),
                                  bc(rs[:, 0:TB, :].unsqueeze(3), [P, TB, 4, DH1]), ALU.mult)
                dve.tensor_tensor(qkn[0:NK, TB, 0:D].rearrange("p (n d) -> p n d", n=2),
                                  PS[0:NK, TB, 0:D].rearrange("p (n d) -> p n d", n=2),
                                  bc(rs[0:NK, TB, 0:2].unsqueeze(2), [NK, 2, DH1]), ALU.mult).then_inc(qkn_ready, 1)
                dve.wait_ge(qT_done, b + 1)
                dve.tensor_scalar(QT[:, :], PS[:, 5, :], gqk[:, :], None, ALU.mult).then_inc(QT_ready, 1)

                def first_keys(i):
                    dve.wait_ge(ET_done, NI * b + i + 1)
                    if NI * b + i >= 2:
                        dve.wait_ge(pv1_mm, NI * b + i - 1)
                    dve.tensor_copy(ET[:, i % 2, 0:TB, :], PS[:, 4, :].rearrange("p (c q) -> p c q", c=TB)).then_inc(ET_dve, 1)

                for i in range(NI):
                    dve.wait_ge(sc_mm, NI * b + i + 1)
                    dve.tensor_reduce(nmx[:, i:i + 1], PS[:, 2 * (i % 2):2 * (i % 2) + 2, :].rearrange("p a n -> p (a n)")[:, 0:S + NK],
                                      X_AXIS, ALU.max, negate=True).then_inc(max_ready, 1)
                    if i >= 1:
                        first_keys(i - 1)
                first_keys(NI - 1)
                dve.wait_ge(E_ready, NI * (b + 1))
                link(dve.reciprocal(rden[:, :], den[:, :]))
                dve.wait_ge(pv1_mm, NI * (b + 1))
                dve.tensor_tensor(ao[:, :, :].rearrange("p t (h d) -> p (t h) d", h=HEADS1),
                                  PS[:, 6, :].rearrange("p (i d) -> p i d", d=DH1),
                                  bc(rden[:, :].unsqueeze(2), [P, NI, DH1]), ALU.mult).then_inc(ao_ready, 1)
                residual(3, b, PS[:, 0, :], oproj_mm, NB + b + 1, xb=NB + b + 1)

            norm(0)
            small_weights()
            keys_and_values()
            attention0(0)
            norm(1)
            attention0(1)
            for b in range(NB):
                experts(0, b)
            context_norm()
            for b in range(NB):
                attention1(b)
            for b in range(NB):
                experts(1, b)


def shape_constants():
    import numpy as np
    p = np.arange(P)
    c = np.zeros((P, NCC), np.float32)
    c[:, CO["ident"]] = np.eye(P)
    c[:, CO["hm"]] = (p[:, None] % 32) // DK == np.arange(HG)[None]
    c[:, CO["nlo"]] = -1.0 * ((p[:, None] // 32 == 1) | (p[:, None] // 32 == 2))
    for n in range(NC):
        r = np.arange(min(CW, GW - CW * n))
        c[:len(r), CO["vm"].start + HG * n:CO["vm"].start + HG * (n + 1)] = (r[:, None] + CW * n) // NK == np.arange(HG)[None]
    c[:H, CO["eye"]] = np.eye(H)
    c[E0:2 * E0, CO["nlo0"]] = -1.0
    c[E1:2 * E1, CO["nlo1"]] = -1.0
    onehot = np.repeat(np.eye(H, dtype=np.float32), NK, axis=1)
    sel = [np.tile(np.repeat(np.eye(e, dtype=np.float32), n, axis=1), (2, 1)) for e, n in ((E0, HID0), (E1, HID1))]
    return c, onehot, sel


def kernel(**inputs):
    import numpy as np
    import concourse.bacc as bacc
    from concourse.bass_utils import run_bass_kernel_spmd as run

    i = {k: np.asarray(a) for k, a in inputs.items()}
    a, f, l, g = ({k[len(n):]: w for k, w in i.items() if k.startswith(n)}
                  for n in ("L0_xattn_", "L0_ffn_", "L1_xattn_", "L1_ffn_"))

    def channel_rows(w):
        return np.tile(w.reshape(NG, 32).T, (4, 1))

    def column(w):
        return np.tile(w.reshape(-1), P // w.size)[:, None]

    def rows(w):
        return np.broadcast_to(w.reshape(1, -1), (P, w.size))

    consts, onehot, (sel0, sel1) = shape_constants()
    vecs = dict(bq=channel_rows(a["bq"]), bk=channel_rows(a["bk"]), lxg=column(l["ln_x_g"]), lxb=column(l["ln_x_b"]),
                llg=column(l["ln_l_g"]), llb=column(l["ln_l_b"]), qg=column(l["q_gamma"]), kg=column(l["k_gamma"]),
                b1=column(a["b1"]), b2=column(a["b2"]), w3=column(a["w3"]), b3=column(a["b3"]), w1=rows(a["w1"].T),
                gb=rows(g["gate_bias"]), bo=rows(a["bo"]), bv=rows(a["bv"]), bout=rows(l["b_out"]))

    def hidden_last(w):
        return w.transpose(1, 0, 2).reshape(D, -1)

    arrays = dict(
        x=i["x"].reshape(NB * S, D), ctx=i["ctx_1024"], mask=i["mask_BxS2_bk0"].reshape(1, NB * NK).astype(np.int32),
        vecs=np.concatenate([vecs[k] for k in V_COLS], axis=1),
        wa=np.concatenate([a[k].T for k in ("Wq", "Wk", "Wv", "Wo")], axis=1), w2t=a["w2"].T, wr=f["Wr"],
        up0=np.stack([hidden_last(f["W1"]), hidden_last(f["W3"])]), wdn0=f["W2"].reshape(-1, D),
        wl1=np.concatenate([l["W_q"], l["W_kv"], l["W_out"]], axis=1), gw=g["gate_w"].T,
        up1=np.stack([np.concatenate([g[f"expert_{k}"].transpose(2, 0, 1).reshape(D, -1), g[f"shared_{k}"].T], axis=1)
                      for k in ("gate", "up")]),
        wdn1=np.concatenate([g["expert_down"].transpose(0, 2, 1).reshape(-1, D), g["shared_down"].T], axis=0),
        consts=consts, onehot=onehot, sel0=sel0, sel1=sel1)
    nc = bacc.Bacc("TRN2", target_bir_lowering=False, num_devices=1)
    fed, args = {}, {}
    for name, w in arrays.items():
        w = np.ascontiguousarray(w)
        fed[f"in_{name}"] = w
        args[name] = nc.dram_tensor(f"in_{name}", w.shape, mybir.dt.from_np(w.dtype), kind="ExternalInput").ap()
    out = nc.dram_tensor("out_x", (NB * S, D), F32, kind="ExternalOutput").ap()
    program(nc, out=out, **args)
    r = run(nc, [fed], core_ids=[0])
    return r.results[0]["out_x"].reshape(NB, S, D)
```

```python
from contextlib import ExitStack

import concourse.bass as bass
from concourse import mybir

F32 = mybir.dt.float32
F32R = mybir.dt.float32r
I32 = mybir.dt.int32
ALU = mybir.AluOpType
ACT = mybir.ActivationFunctionType
X_AXIS = mybir.AxisListType.X

P = 128
NB, S, D = 2, 512, 128
TB = S // P
NK = 77
H, DK = 16, 8
NG, HG = 4, 4
GW = HG * NK
NC, CW = 3, 103
PW = HG * (DK + 1)
MH = 64
E0, HID0 = 8, 192
E1, HID1 = 32, 64
J0 = E0 * HID0 // P
J1 = E1 * HID1 // P
HEADS1, DH1 = 2, 64
LN_EPS = 1e-5
BIG = 3.0e38
LOG_T_MIN, LOG_T_MAX = -2.302585092994046, 2.302585092994046

V_COLS = dict(bq=4, bk=4, lxg=1, lxb=1, llg=1, llb=1, qg=1, kg=1, b1=1, b2=1, w3=1, b3=1,
              w1=3 * MH, gb=E1, bo=D, bv=D, bout=D)
C_COLS = dict(ident=P, hm=HG, nlo=1, vm=NC * HG, eye=H, nlo0=1, nlo1=1)


def offsets(cols):
    at, out = 0, {}
    for name, n in cols.items():
        out[name] = slice(at, at + n)
        at += n
    return out, at


VO, NV = offsets(V_COLS)
CO, NCC = offsets(C_COLS)


def program(nc, x, ctx, mask, vecs, wa, w2t, wr, up0, wdn0, wl1, gw, up1, wdn1, consts, onehot,
            sel0, sel1, out):
    with ExitStack() as stack:
        def sb(name, shape, dt=F32):
            return stack.enter_context(nc.sbuf_tensor(name, shape, dt))

        def sem(name):
            return stack.enter_context(nc.semaphore(name))

        vec = sb("vec", [P, NV])
        cst = sb("cst", [P, NCC])
        ident = cst[:, CO["ident"]]

        def v(name):
            return vec[:, VO[name]]

        X = [sb(f"x_{n}", [P, NB * TB, D]) for n in range(3)]
        X += [X[1], X[0]]
        XB = sb("xb", [P, NB * TB, D])
        wa_s = sb("wa_s", [P, 4 * D])
        w2t_s = sb("w2t_s", [MH, MH])
        wqr = sb("wqr", [P, NG, 4, 32])
        wkr = sb("wkr", [P, NG, 4, 32])
        w1s = sb("w1s", [P, 3, MH])
        w3r = sb("w3r", [MH, P])
        ctx_s = sb("ctx_s", [NK, NB, D])
        mask_s = sb("mask_s", [1, NB * NK], I32)
        mneg = sb("mneg", [1, NB, NK])
        ones_row = sb("ones_row", [1, P])
        xc = sb("xc", [NK, NB, D])
        xcT = sb("xcT", [P, NB, NK])
        sqc = sb("sqc", [NK, NB, D])
        kcn = sb("kcn", [NK, NB, D])
        st = sb("st", [P, 5, NB * TB, 6])
        mv = sb("mv", [P, 5, NB * TB, 2])
        ve = sb("ve", [P, 5, NB * TB])
        va = sb("va", [P, 3, NB * TB])
        rstd = sb("rstd", [P, 7, NB * TB])
        mhalf = sb("mhalf", [P, 20])
        xn = sb("xn", [P, TB, D])
        onehr = sb("onehr", [H, H * NK], F32R)
        wl1_s = sb("wl1_s", [P, 4 * D])
        aoT = sb("aoT", [P, S])
        ao = sb("ao", [P, TB, D])
        gqk = sb("gqk", [P, 1])
        rt_s = [sb("wr_s", [P, E0]), sb("gw_s", [P, E1])]
        rth = [sb("wrh", [P, E0], F32R), sb("gwh", [P, E1], F32R)]
        rtl = [sb("wrl", [P, E0], F32R), sb("gwl", [P, E1], F32R)]
        lg = sb("lg", [P, TB, 2 * E0])
        m8 = sb("m8", [P, TB, 8])
        rv = sb("rv", [P, TB, 8])
        rp = sb("rp", [P, TB, 2 * E0])
        sc1 = sb("sc1", [P, 8, TB, E1])
        g8 = sb("g8", [P, TB, 4, 8])
        gsm = sb("gsm", [P, 2, TB])
        comb = sb("comb", [P, TB, 2 * E1])
        xth, xtl, ct = [sb("xth_0", [P, S], F32R)], [sb("xtl_0", [P, S], F32R)], [sb("ct_0", [2 * E1, S], F32R)]
        th = sb("th", [P, 2, S])
        hg = sb("hg", [P, 2, S])
        u = sb("u", [P, 2, S])
        yT = th[:, 0, :]
        ss = sb("ss", [P, TB, 4])
        ssm = sb("ssm", [P, TB, 4])
        rs = sb("rs", [P, TB, 4])
        ssc = sb("ssc", [NK, 3, NB, 2])
        kctxT = sb("kctxT", [P, NB, NK])
        vctx = sb("vctx", [NK, NB, D])
        NW = (J1 + 1) * P
        kept, stack = stack, stack.enter_context(ExitStack())
        raw0 = [sb(f"raw0_{n}", [P, J0 * P]) for n in range(2)]
        uph0 = [sb(f"uph0_{n}", [P, J0 * P], F32R) for n in range(2)]
        upl0 = [sb(f"upl0_{n}", [P, J0 * P], F32R) for n in range(2)]
        wdn0_s = sb("wdn0_s", [P, J0 * D])
        sel0r = sb("sel0r", [2 * E0, J0 * P], F32R)
        inner, stack = stack, stack.enter_context(ExitStack())
        ctxT = sb("ctxT", [P, NB, NK])
        ctxr = sb("ctxr", [P, NB, HG, NK])
        XT = sb("XT", [P, S])
        krep = sb("krep", [P, NG, NB, NK])
        ksum = sb("ksum", [P, NG, NB])
        kbd = sb("kbd", [P, NG, HG, NK])
        khi = sb("khi", [P, H * NK], F32R)
        kf2 = sb("kf2", [P, H * NK])
        kst = sb("kst", [P, H * NK], F32R)
        kst2 = sb("kst2", [P, H * NK], F32R)
        vbd = sb("vbd", [CW, NB, NC, 3 * NG * PW])
        qst = sb("qst", [P, NG, S], F32R)
        qsum = sb("qsum", [P, NB, NG])
        mx = sb("mx", [P, TB, H])
        sh = sb("sh", [P, 2, H, NK])
        stats = sb("stats", [P, TB * H, 6])
        sw = sb("sw", [P, 6, TB * H])
        vp = sb("vp", [P, NB, TB * H])
        pk = sb("pk", [P, NB, NG, HG])
        qk1 = sb("qk1", [P, NB, NG])
        h1 = sb("h1", [MH, NB, H])
        h2 = sb("h2", [MH, NB, H])
        lt = sb("lt", [P, NB, 2, H])
        rt = sb("rt", [P, NB, H])
        rd = sb("rd", [H, NB, H])
        rneg = sb("rneg", [H, NB])
        nm2 = sb("nm2", [H, S], F32R)
        e2 = sb("e2", [CW, 2, NC, S])
        tmpv = e2[:, 0, 0:2, :].rearrange("p a n -> p (a n)")[:, 0:NB * NC * D].rearrange("p (b c n) -> p b c n", b=NB, c=NC)
        oT = [m[0:2 * PW, :] for m in (ao[:, :, :].rearrange("p t c -> p (t c)"), aoT[:, :])]
        omin, onum = (kf2[:, 2 * TB * 2 * PW * n:2 * TB * 2 * PW * (n + 1)].rearrange("p (a t h d) -> p a t h d", a=2, t=TB, d=DK + 1)
                      for n in range(2))
        oden = sb("oden", [P, 2, 2, TB, 2 * HG])
        stack.close()
        stack = inner
        LT = sb("LT", [P, S])
        V1 = sb("V1", [P, TB, D])
        QT = sb("QT", [P, S])
        KT = sb("KT", [P, S])
        nmx = sb("nmx", [P, TB * HEADS1])
        E = sb("E", [P, 2, S + NK])
        ET = sb("ET", [P, 2, 5, P])
        sq, qkn = (m[:, 0:TB * 2 * D].rearrange("p (t n) -> p t n", t=TB) for m in (
            E[:, :, :].rearrange("p a n -> p (a n)"), ET[:, :, :, :].rearrange("p a c q -> p (a c q)")))
        xth.append(sb("xth_1", [P, S], F32R))
        xtl.append(sb("xtl_1", [P, S], F32R))
        ct.append(sb("ct_1", [2 * E1, S], F32R))
        den = sb("den", [P, TB * HEADS1])
        rden = sb("rden", [P, TB * HEADS1])
        uph1 = [sb(f"uph1_{n}", [P, NW], F32R) for n in range(2)]
        upl1 = [sb(f"upl1_{n}", [P, NW], F32R) for n in range(2)]
        wdn1_s = sb("wdn1_s", [P, NW])
        sel1r = sb("sel1r", [2 * E1, J1 * P], F32R)
        uph, upl, wdn_s, selr = (uph0, uph1), (upl0, upl1), (wdn0_s, wdn1_s), (sel0r, sel1r)

        PS = stack.enter_context(nc.psum_tensor("PS", [P, 8, 512], F32))

        def sems(names):
            return [sem(n) for n in names.split()]

        d_x, d_up0 = ([sem(f"d_{k}{n}") for n in range(2)] for k in ("x", "up0_"))
        d_piece = [sem(f"d_piece{n}") for n in range(6)]
        d_vec, d_cst, d_ctx, d_wa, d_oneh, d_w0, d_sel0, d_dn0, d_l1, d_dn1, d_out = sems(
            "d_vec d_cst d_ctx d_wa d_oneh d_w0 d_sel0 d_dn0 d_l1 d_dn1 d_out")
        d_dn = (d_dn0, d_dn1)
        dve_step, pool_step, k_raw2 = sems("dve_step pool_step k_raw2")
        pool_const, ve_ready, rstd_ready, xn_ready, xnT_done, xb_ready = sems(
            "pool_const ve_ready rstd_ready xn_ready xnT_done xb_ready")
        x_done = [None] + [sem(f"x{k}_done") for k in range(1, 5)]
        w_small, ctxT_done, ctxT_copied, krep_mm, k_raw, k_hi, k_ready, v_mm, v_ready = sems(
            "w_small ctxT_done ctxT_copied krep_mm k_raw k_hi k_ready v_mm v_ready")
        XT_ready, q_mm, q_hi, q_ready, sc1_mm, sc1_out, e1_ready, feats, hid_mm, hid_act, logt_mm, logt_in = sems(
            "XT_ready q_mm q_hi q_ready sc1_mm sc1_out e1_ready feats hid_mm hid_act logt_mm logt_in")
        invt_raw, mxT_done, nm2_ready, onehot_ready, sc2_mm, e2_ready, pv_mm, oT_copied, oback_mm = sems(
            "invt_raw mxT_done nm2_ready onehot_ready sc2_mm e2_ready pv_mm oT_copied oback_mm")
        ao_ready, aoT_done, aoT_copied, oproj_mm = sems("ao_ready aoT_done aoT_copied oproj_mm")
        sel_ready, up_hi, up_lo, rt_hi, rt_lo, xth_ready, xtl_ready, lg_mm, lg_copied, gate_in, gate_exp = sems(
            "sel_ready up_hi up_lo rt_hi rt_lo xth_ready xtl_ready lg_mm lg_copied gate_in gate_exp")
        comb_ready, combT_done, cth_ready, ct_ready, h_mm, g_mm, w_mm, th_ready, a_ready, b_ready, u_ready = sems(
            "comb_ready combT_done cth_ready ct_ready h_mm g_mm w_mm th_ready a_ready b_ready u_ready")
        down_mm, yT_copied, y_mm = sems("down_mm yT_copied y_mm")
        cve_ready, crstd_ready, xc_ready, xcT_done, xcT_ready, ckv_mm, cv_ready, cssm_ready, crs_ready, kcn_ready = sems(
            "cve_ready crstd_ready xc_ready xcT_done xcT_ready ckv_mm cv_ready cssm_ready crs_ready kcn_ready")
        kcT_done, kctx_ready, LT_ready, proj_mm, sq_ready, ssm_ready, rs_ready, qkn_ready, V_ready, qT_done = sems(
            "kcT_done kctx_ready LT_ready proj_mm sq_ready ssm_ready rs_ready qkn_ready V_ready qT_done")
        QT_ready, KT_ready, sc_mm, max_ready, E_ready, ET_done, ET_dve, ET_act, pv1_mm = sems(
            "QT_ready KT_ready sc_mm max_ready E_ready ET_done ET_dve ET_act pv1_mm")

        NCH = (J0, J1 + 1)
        NWB = (J0, J1)
        NE = (E0, E1)
        ISQ = DK ** -0.5
        NI = TB * HEADS1
        BH, BG, BW, BY = 4, 5, 6, 7
        HALF = NW // 2
        PIECES = [(0, 0), (0, 1), (1, 0), (1, 1), (2, 0), (2, 1)]
        ORDER = [(0, 0), (0, 1), (1, 0), (1, 1), (2, 0), (3, 0), (2, 1), (3, 1)]

        def nth_norm(k, b):
            return ORDER.index((k, b))

        def chunks_before(layer, b):
            return (0 if layer == 0 else NB * NCH[0]) + b * NCH[layer]

        def weighted_before(layer, b):
            return (0 if layer == 0 else NB * NWB[0]) + b * NWB[layer]

        def tiles(b):
            return slice(TB * b, TB * b + TB)

        def crows(c):
            return min(CW, GW - CW * c)

        def bc(ap, shape):
            return ap.broadcast_to(shape)

        PRE = 5
        BESIDE_A0 = dict(mlp1=1, mlp2=0, logt=0, keys=2, g0=3, g1=2, g2=1, g3=1, pv=1, o1=1, o2=1)
        BESIDE_A1 = dict(t2=2, t3=2, s=1, mlp1=1, mlp2=1, logt=1, keys=1, g0=1, g1=1, g2=0, g3=1, pv=1, o1=1, o2=0)
        BESIDE_B = [dict(n1=1, n2=1, n3=1, n4=1, pv=0, o1=1, o2=0), dict(n1=1, n2=1, n3=1, n4=1, pv=1, o1=1, o2=0)]
        BESIDE_B[0].update({f"i{i}": int(i in (1, 2, 5, 6)) for i in range(NI)})
        BESIDE_B[1].update({f"i{i}": int(i not in (0, 7)) for i in range(NI)})

        def beside(step, total, plan):
            at = [0]

            def fill(point=None):
                end = total if point is None else min(total, at[0] + plan.get(point, 0))
                for k in range(at[0], end):
                    step(k)
                at[0] = end
            return fill

        def schedule(prepare, queries, tile, context, begin, chunk, finish, attention0, attention1):
            def first(k):
                if k < 3:
                    context(k)
                elif k < 6:
                    prepare(1, k - 3)
                elif k < 6 + NG:
                    queries(1, k - 6)
                else:
                    tile(1, k - 6 - NG)

            def experts(layer, b):
                return lambda k: begin(layer, b, k) if k < PRE else chunk(layer, b, k - PRE)

            def between(layer, b, rest):
                for k in range(PRE):
                    begin(layer, b, k)
                    rest("between")
                rest()

            for k in range(3):
                prepare(0, k)
            for g in range(NG):
                queries(0, g)
            rest = beside(first, 6 + NG + 2, BESIDE_A0)
            attention0(0, rest)
            rest()
            rest = beside(experts(0, 0), PRE + NCH[0], dict(BESIDE_A1, between=1))
            attention0(1, rest)
            between(0, 1, rest)
            finish(0, 0)
            rest = beside(lambda k: chunk(0, 1, k), NCH[0], dict(BESIDE_B[0], between=1))
            attention1(0, rest)
            between(1, 0, rest)
            finish(0, 1)
            rest = beside(lambda k: chunk(1, 0, k), NCH[1], dict(BESIDE_B[1], between=1))
            attention1(1, rest)
            between(1, 1, rest)
            finish(1, 0)
            for j in range(NCH[1]):
                chunk(1, 1, j)
            finish(1, 1)

        def nothing(*_):
            pass

        A0_POINTS = [[p for p in ("t0", "t1", "t2", "t3", "s", "mlp1", "mlp2", "logt", "keys", "g0", "g1", "g2", "g3", "pv",
                                  "o1", "o2") if b == 0 or p not in ("t0", "t1")] for b in range(NB)]

        def begin_banks(layer, b):
            return (BH, BG, BW) if (layer, b) == (0, 0) else (0, 1, 2)

        def query_bank(b, g):
            return 4 + g if b else (1 + g) % 4

        def vbd_slots(r, b, c):
            return vbd[0:r, b, c, :].rearrange("p (g a h d) -> p g a h d", g=NG, a=3, h=HG)[:, :, 0]

        def tile_bank(b, t):
            return NG if b and t < 2 else 0

        block = stack.enter_context(nc.Block())

        @block.sync
        def _(sp):
            sp.dma_start(X[0][:, tiles(0), :], x[0:S].rearrange("(t p) c -> p t c", p=P)).then_inc(d_x[0], 16)
            sp.dma_start(ctx_s[:, :, :], ctx.rearrange("b k c -> k b c")).then_inc(d_ctx, 16)
            sp.dma_start(raw0[1][0:H, 0:H * NK], onehot).then_inc(d_oneh, 16)
            sp.dma_start(mask_s[:, :], mask).then_inc(d_ctx, 16)
            sp.dma_start(raw0[0][0:2 * E0, :], sel0).then_inc(d_sel0, 16)
            sp.dma_start(X[0][:, tiles(1), :], x[S:].rearrange("(t p) c -> p t c", p=P)).then_inc(d_x[1], 16)
            sp.dma_start(rt_s[0][:, :], wr).then_inc(d_w0, 16)
            sp.dma_start(rt_s[1][:, :], gw).then_inc(d_w0, 16)
            sp.wait_ge(sel_ready, 1)
            sp.dma_start(raw0[0][:, :], up0[0]).then_inc(d_up0[0], 16)
            sp.wait_ge(onehot_ready, 1)
            sp.dma_start(raw0[1][:, :], up0[1]).then_inc(d_up0[1], 16)
            sp.dma_start(wdn0_s[:, :].rearrange("p (j c) -> p j c", j=J0), wdn0.rearrange("(j p) c -> p j c", p=P)
                         ).then_inc(d_dn0, 16)
            sp.dma_start(wl1_s[:, :], wl1).then_inc(d_l1, 16)
            sp.wait_ge(x_done[1], NB)
            for n, (what, half) in enumerate(PIECES):
                if n < 2:
                    sp.wait_ge(up_lo, 2)
                elif n < 4:
                    sp.wait_ge(sel_ready, n)
                else:
                    sp.wait_ge(up_lo, n - 1)
                if what == 0:
                    w = J1 * P // 2
                    sp.dma_start(raw0[n % 2][0:2 * E1, 0:w], sel1[:, w * half:w * half + w]).then_inc(d_piece[n], 16)
                else:
                    sp.dma_start(raw0[n % 2][:, 0:HALF], up1[what - 1, :, HALF * half:HALF * half + HALF]
                                 ).then_inc(d_piece[n], 16)
            sp.dma_start(wdn1_s[:, :].rearrange("p (j c) -> p j c", c=D), wdn1.rearrange("(j p) c -> p j c", p=P)
                         ).then_inc(d_dn1, 16)
            for b in range(NB):
                sp.wait_ge(x_done[4], b + 1)
                sp.dma_start(out[S * b:S * b + S].rearrange("(t p) c -> p t c", p=P), X[4][:, tiles(b), :]
                             ).then_inc(d_out, 16)
            sp.wait_ge(d_out, 16 * NB)

        @block.gpsimd
        def _(pool):
            done = [0]

            def link(ins):
                done[0] += 1
                ins.then_inc(pool_step, 1)
                pool.wait_ge(pool_step, done[0])

            pool.memset(mhalf[:, :], -0.5)
            pool.memset(ones_row[:, :], 1.0)
            pool.memset(vbd[:, :, :, :], 0.0)
            pool.memset(rv[:, :, :], -BIG)
            pool.memset(lg[:, :, :], -BIG).then_inc(pool_const, 1)
            pool.wait_ge(pool_const, 1)

            def inv_std(k, b):
                pool.wait_ge(ve_ready, nth_norm(k, b) + 1)
                last = pool.tensor_tensor(rstd[:, k, tiles(b)], ve[:, k, tiles(b)], mhalf[:, 0:TB], ALU.pow)
                if k == 2:
                    link(last)
                    link(pool.tensor_tensor(va[:, 0, tiles(b)], rstd[:, 2, tiles(b)], rstd[:, 2, tiles(b)], ALU.mult))
                    link(pool.tensor_tensor(va[:, 1, tiles(b)], va[:, 0, tiles(b)], mv[:, 2, tiles(b), 1], ALU.mult))
                    link(pool.tensor_scalar(va[:, 2, tiles(b)], va[:, 1, tiles(b)], 1.0, LN_EPS, ALU.mult, ALU.add))
                    link(pool.tensor_tensor(rstd[:, 5, tiles(b)], va[:, 2, tiles(b)], mhalf[:, 0:TB], ALU.pow))
                    last = pool.tensor_tensor(rstd[:, 6, tiles(b)], rstd[:, 5, tiles(b)], rstd[:, 2, tiles(b)], ALU.mult)
                last.then_inc(rstd_ready, 1)

            def add_bias(k, b, bias):
                for t in range(TB * b, TB * b + TB):
                    last = pool.tensor_tensor(XB[:, t, :], X[k][:, t, :], bias, ALU.add)
                last.then_inc(xb_ready, 1)

            def prepare(b, k):
                if k == 0:
                    inv_std(0, b)
                if b or k:
                    return
                pool.wait_ge(d_vec, 16)
                for n in range(NB):
                    pool.wait_ge(d_x[n], 16)
                    add_bias(0, n, v("bo"))
                pool.wait_ge(d_w0, 32)
                for layer in range(2):
                    pool.tensor_copy(rth[layer][:, :], rt_s[layer][:, :]).then_inc(rt_hi, 1)
                    pool.wait_ge(rt_hi, layer + 1)
                    pool.tensor_tensor(rtl[layer][:, :], rt_s[layer][:, :], rth[layer][:, :].bitcast(F32),
                                       ALU.subtract).then_inc(rt_lo, 1)

            def attention0(b, fill):
                if b == 0:
                    for n in range(2):
                        pool.wait_ge(up_hi, n + 1)
                        pool.tensor_tensor(upl0[n][:, :], raw0[n][:, :], uph0[n][:, :].bitcast(F32), ALU.subtract
                                           ).then_inc(up_lo, 1)
                for point in A0_POINTS[b]:
                    fill(point)

            def begin(layer, b, k):
                if k == 0:
                    inv_std(2 * layer + 1, b)

            def context(k):
                if k == 0:
                    pool.wait_ge(cve_ready, 1)
                    pool.tensor_tensor(rstd[0:NK, 4, 0:NB], ve[0:NK, 4, 0:NB], mhalf[0:NK, 0:NB], ALU.pow
                                       ).then_inc(crstd_ready, 1)
                elif k == 1:
                    pool.wait_ge(cssm_ready, 1)
                    pool.tensor_tensor(ssc[:, 2].rearrange("p b h -> p (b h)"), ssc[:, 1].rearrange("p b h -> p (b h)"),
                                       mhalf[0:NK, 0:NB * HEADS1], ALU.pow).then_inc(crs_ready, 1)

            def attention1(b, fill):
                inv_std(2, b)
                pool.wait_ge(ssm_ready, b + 1)
                pool.tensor_tensor(rs[:, :, :].rearrange("p a b -> p (a b)"), ssm[:, :, :].rearrange("p a b -> p (a b)"),
                                   mhalf[:, 0:4 * TB], ALU.pow).then_inc(rs_ready, 1)
                add_bias(2, b, v("bout"))
                for n, (what, half) in enumerate(PIECES):
                    if b == 0 and what:
                        c = slice(HALF * half, HALF * half + HALF)
                        pool.wait_ge(up_hi, n + 1)
                        pool.tensor_tensor(upl1[what - 1][:, c], raw0[n % 2][:, 0:HALF],
                                           uph1[what - 1][:, c].bitcast(F32), ALU.subtract).then_inc(up_lo, 1)

            schedule(prepare, nothing, nothing, context, begin, nothing, nothing, attention0, attention1)

        @block.scalar
        def _(act):
            act.dma_start(cst[:, :], consts).then_inc(d_cst, 16)
            act.dma_start(wa_s[:, :], wa).then_inc(d_wa, 16)
            act.dma_start(vec[:, :], vecs).then_inc(d_vec, 16)
            act.dma_start(w2t_s[:, :], w2t).then_inc(d_wa, 16)

            def copy(dst, src):
                return act.activation(dst, src, ACT.Copy)

            def split_keys(src, nth, ready, value):
                for g in range(NG):
                    act.wait_ge(ready, value + g)
                    if nth:
                        act.wait_ge(k_ready, NG * (nth - 1) + g + 1)
                    copy(khi[:, GW * g:GW * g + GW], src(g)).then_inc(k_hi, 1)

            def prepare(b, k):
                if k == 1:
                    act.wait_ge(xnT_done, nth_norm(0, b) + 1)
                    copy(XT[:, :], PS[:, 7 * b, :]).then_inc(XT_ready, 1)
                elif k == 2:
                    split_keys(lambda g: kbd[:, g].rearrange("p h k -> p (h k)"), 2 * b, k_raw, NG * b + 1)

            def queries(b, g):
                act.wait_ge(q_mm, NG * b + g + 1)
                if b:
                    act.wait_ge(sc2_mm, NC * (g + 1))
                act.activation(qst[:, g, :], PS[:, query_bank(b, g), :], ACT.Identity, bias=v("bq")[:, g:g + 1],
                               accum_out=qsum[:, b, g:g + 1]).then_inc(q_hi, 1)

            def tile(b, t):
                if b == 0 and t == 0:
                    act.wait_ge(d_oneh, 16)
                    copy(onehr[:, :], raw0[1][0:H, 0:H * NK]).then_inc(onehot_ready, 1)
                    act.wait_ge(d_sel0, 16)
                    copy(sel0r[:, :], raw0[0][0:2 * E0, :]).then_inc(sel_ready, 1)
                act.wait_ge(sc1_out, TB * b + t + 1)
                act.activation(sh[:, t % 2, :, :], sh[:, t % 2, :, :], ACT.Exp, scale=ISQ).then_inc(e1_ready, 1)

            def attention0(b, fill):
                for t in range(2 * b, TB):
                    tile(b, t)
                    fill(f"t{t}")
                if b == 0:
                    for n in range(2):
                        act.wait_ge(d_up0[n], 16)
                        copy(uph0[n][:, :], raw0[n][:, :]).then_inc(up_hi, 1)
                fill("s")
                act.wait_ge(hid_mm, 2 * b + 1)
                act.activation(h1[:, b, :], PS[0:MH, 0, 0:H], ACT.Gelu, bias=v("b1")[0:MH, :]).then_inc(hid_act, 1)
                fill("mlp1")
                act.wait_ge(hid_mm, 2 * b + 2)
                act.activation(h2[:, b, :], PS[0:MH, 1, 0:H], ACT.Gelu, bias=v("b2")[0:MH, :]).then_inc(hid_act, 1)
                fill("mlp2")
                act.wait_ge(logt_in, b + 1)
                act.activation(rt[:, b, :], lt[:, b, 1, :], ACT.Exp, scale=-1.0).then_inc(invt_raw, 1)
                fill("logt")
                split_keys(lambda g: kf2[:, GW * g:GW * g + GW], 2 * b + 1, k_raw2, NG * b + 1)
                fill("keys")

                def pair_copied(a):
                    act.wait_ge(pv_mm, NG * b + 2 * a + 2)
                    copy(oT[a], PS[0:2 * PW, 2 + a, :]).then_inc(oT_copied, 1)

                for g in range(NG):
                    for c in range(NC):
                        i = NG * NC * b + NC * g + c
                        act.wait_ge(sc2_mm, i + 1)
                        if NG * b + g >= 2:
                            act.wait_ge(pv_mm, NG * b + g - 1)
                        r = crows(c)
                        act.activation(e2[0:r, g % 2, c, :], PS[0:r, (NC * g + c) % 2, :], ACT.Exp).then_inc(e2_ready, 1)
                    fill(f"g{g}")
                pair_copied(0)
                pair_copied(1)
                fill("pv")
                act.wait_ge(aoT_done, b + 1)
                copy(aoT[:, :], PS[:, 0, :]).then_inc(aoT_copied, 1)
                fill("o1")
                fill("o2")

            def begin(layer, b, k):
                f, r = NB * layer + b, 2 * NE[layer]
                bt, _, bw = begin_banks(layer, b)
                if k == 1:
                    act.wait_ge(xnT_done, nth_norm(2 * layer + 1, b) + 1)
                    copy(xth[b][:, :], PS[:, bt, :]).then_inc(xth_ready, 1)
                elif k == 3:
                    act.wait_ge(gate_in, f + 1)
                    if layer == 0:
                        act.activation(sc1[:, 1, :, 0:E0], sc1[:, 0, :, 0:E0], ACT.Exp).then_inc(gate_exp, 1)
                    else:
                        act.activation(sc1[:, 1, :, :], sc1[:, 0, :, :], ACT.Exp, scale=-1.0).then_inc(gate_exp, 1)
                elif k == 4:
                    act.wait_ge(combT_done, f + 1)
                    copy(ct[b][0:r, :], PS[0:r, bw, :]).then_inc(cth_ready, 1)

            def chunk(layer, b, j):
                i = chunks_before(layer, b) + j
                act.wait_ge(h_mm, i + 1)
                if i and j == 0:
                    act.wait_ge(y_mm, NB * layer + b)
                if i >= 2:
                    act.wait_ge(a_ready, i - 1)
                act.activation(th[:, i % 2, :], PS[:, BH, :], ACT.Tanh, scale=0.5).then_inc(th_ready, 1)

            def finish(layer, b):
                act.wait_ge(down_mm, chunks_before(layer, b) + NCH[layer])
                act.wait_ge(a_ready, chunks_before(layer, b) + NCH[layer])
                copy(yT, PS[:, BY, :]).then_inc(yT_copied, 1)

            def context(k):
                if k == 0:
                    act.wait_ge(xcT_done, 1)
                    act.activation(xcT[:, :, :].rearrange("p b k -> p (b k)"), PS[:, 4, 0:NB * NK], ACT.Identity,
                                   bias=v("lxb"), scale=v("lxg")).then_inc(xcT_ready, 1)
                elif k == 1:
                    act.wait_ge(ckv_mm, 1)
                    act.activation(sqc[:, :, :], PS[0:NK, 5:5 + NB, 0:D], ACT.Square)
                    copy(vctx[:, :, :], PS[0:NK, 5:5 + NB, D:2 * D]).then_inc(cv_ready, 1)
                else:
                    act.wait_ge(kcT_done, 1)
                    copy(kctxT[:, :, :].rearrange("p b k -> p (b k)"), PS[:, 4, 0:NB * NK]).then_inc(kctx_ready, 1)

            def reload(n):
                what, half = PIECES[n]
                act.wait_ge(d_piece[n], 16)
                if what == 0:
                    w = J1 * P // 2
                    copy(sel1r[:, w * half:w * half + w], raw0[n % 2][0:2 * E1, 0:w]).then_inc(sel_ready, 1)
                else:
                    copy(uph1[what - 1][:, HALF * half:HALF * half + HALF], raw0[n % 2][:, 0:HALF]).then_inc(up_hi, 1)

            def attention1(b, fill):
                fill("n1")
                act.wait_ge(xnT_done, nth_norm(2, b) + 1)
                act.activation(LT[:, :], PS[:, 0, :], ACT.Identity, bias=v("llb"), scale=v("llg")).then_inc(LT_ready, 1)
                fill("n2")
                for t in range(TB):
                    act.wait_ge(proj_mm, TB * b + t + 1)
                    act.activation(sq[:, t, :], PS[:, t, 0:2 * D], ACT.Square).then_inc(sq_ready, 1)
                copy(V1[:, :, :], PS[:, 0:TB, 2 * D:3 * D]).then_inc(V_ready, 1)
                fill("n3")
                fill("n4")
                act.wait_ge(qT_done, b + 1)
                copy(KT[:, :], PS[:, 1, :]).then_inc(KT_ready, 1)
                for i in range(NI):
                    n = NI * b + i
                    act.wait_ge(max_ready, n + 1)
                    if n >= 2:
                        act.wait_ge(ET_done, n - 1)
                    act.activation(E[:, i % 2, :], PS[:, 0:2, :].rearrange("p a n -> p (a n)")[:, 0:S + NK],
                                   ACT.Exp, bias=nmx[:, i:i + 1], accum_out=den[:, i:i + 1]).then_inc(E_ready, 1)
                    fill(f"i{i}")
                    if b == 0 and i < len(PIECES):
                        reload(i)
                    act.wait_ge(ET_done, n + 1)
                    if n >= 2:
                        act.wait_ge(pv1_mm, n - 1)
                    copy(ET[0:NK, i % 2, 4, :], PS[0:NK, 1, P:2 * P]).then_inc(ET_act, 1)
                fill("pv")
                act.wait_ge(aoT_done, NB + b + 1)
                copy(aoT[:, :], PS[:, 0, :]).then_inc(aoT_copied, 1)
                fill("o1")
                fill("o2")

            schedule(prepare, queries, tile, context, begin, chunk, finish, attention0, attention1)

        @block.tensor
        def _(pe):
            def transposed(k, b, bank):
                pe.wait_ge(xn_ready, nth_norm(k, b) + 1)
                for t in range(TB):
                    last = pe.transpose(PS[:, bank, P * t:P * t + P], xn[:, t, :], ident)
                last.then_inc(xnT_done, 1)

            def project_out(n, w, fill):
                pe.wait_ge(ao_ready, n + 1)
                for t in range(TB):
                    last = pe.transpose(PS[:, 0, P * t:P * t + P], ao[:, t, :], ident)
                last.then_inc(aoT_done, 1)
                fill("o1")
                pe.wait_ge(aoT_copied, n + 1)
                for t in range(TB):
                    last = pe.matmul(PS[:, 1, P * t:P * t + P], aoT[:, P * t:P * t + P], w, start=True, stop=True)
                last.then_inc(oproj_mm, 1)
                fill("o2")

            def layer0_keys_and_values():
                pe.wait_ge(d_cst, 16)
                pe.wait_ge(d_ctx, 32)
                for b in range(NB):
                    last = pe.transpose(PS[:, 0, NK * b:NK * b + NK], ctx_s[:, b, :], ident[0:NK, 0:NK])
                last.then_inc(ctxT_done, 1)
                pe.wait_ge(w_small, 1)
                pe.wait_ge(ctxT_copied, 2)
                for g in range(NG):
                    last = pe.matmul(PS[:, 1 + g // 2, NB * NK * (g % 2):NB * NK * (g % 2 + 1)],
                                     wkr[:, g].rearrange("p a j -> p (a j)"), ctxT[:, :, :].rearrange("p b k -> p (b k)"),
                                     start=True, stop=True)
                last.then_inc(krep_mm, 1)
                transposed(0, 0, 0)
                for b in range(NB):
                    for c in range(NC):
                        n, r = NC * b + c, crows(c)
                        last = pe.matmul(PS[0:r, 3 + n // 4, D * (n % 4):D * (n % 4) + D],
                                         ctxr[:, b].rearrange("p h k -> p (h k)")[:, CW * c:CW * c + r],
                                         wa_s[:, 2 * D:3 * D], start=True, stop=True)
                last.then_inc(v_mm, 1)

            def prepare(b, k):
                if k == 1 and b == 0:
                    layer0_keys_and_values()
                elif k == 1:
                    transposed(0, b, 7)

            def queries(b, g):
                if g == 0:
                    pe.wait_ge(XT_ready, b + 1)
                    pe.wait_ge(kctx_ready, 1) if b else pe.wait_ge(k_raw, 1)
                if b == 0 and g == 2:
                    pe.wait_ge(v_ready, 1)
                pe.matmul(PS[:, query_bank(b, g), :], wqr[:, g].rearrange("p a j -> p (a j)"), XT[:, :], start=True,
                          stop=True).then_inc(q_mm, 1)

            def tile(b, t):
                if t == 0:
                    pe.wait_ge(q_ready, NG * (b + 1))
                    pe.wait_ge(k_ready, NG * (2 * b + 1))
                elif b and t == 2:
                    pe.wait_ge(x_done[1], 1)
                else:
                    pe.wait_ge(sc1_out, TB * b + t)
                for g in range(NG):
                    last = pe.matmul(PS[:, tile_bank(b, t) + g, 0:GW], qst[:, g, P * t:P * t + P],
                                     kst[:, GW * g:GW * g + GW], start=True, stop=True)
                last.then_inc(sc1_mm, 1)

            def attention0(b, fill):
                for t in range(2 * b, TB):
                    tile(b, t)
                    fill(f"t{t}")
                pe.wait_ge(sc1_out, TB * (b + 1))
                for t in range(TB):
                    last = pe.transpose(PS[0:H, 3, P * t:P * t + P], mx[:, t, :], ident)
                last.then_inc(mxT_done, 1)
                fill("s")
                pe.wait_ge(feats, b + 1)
                pe.matmul(PS[0:MH, 0, 0:H], w1s[:, 0, :], pk[:, b].rearrange("p g h -> p (g h)"), start=True, stop=False)
                for t in range(TB):
                    pe.matmul(PS[0:MH, 0, 0:H], w1s[:, 1, :], mx[:, t, :], start=False, stop=False)
                for t in range(TB):
                    last = pe.matmul(PS[0:MH, 0, 0:H], w1s[:, 2, :], vp[:, b, H * t:H * t + H], start=False,
                                     stop=(t == TB - 1))
                last.then_inc(hid_mm, 1)
                fill("mlp1")
                pe.wait_ge(hid_act, 2 * b + 1)
                pe.matmul(PS[0:MH, 1, 0:H], w2t_s[:, :], h1[:, b, :], start=True, stop=True).then_inc(hid_mm, 1)
                fill("mlp2")
                pe.wait_ge(hid_act, 2 * b + 2)
                pe.matmul(PS[:, 2, 0:H], w3r[:, :], h2[:, b, :], start=True, stop=True).then_inc(logt_mm, 1)
                fill("logt")
                fill("keys")

                def values(g):
                    pe.wait_ge(e2_ready, NG * NC * b + NC * (g + 1))
                    for c in range(NC):
                        r, at = crows(c), PW * (3 * g - g % 2)
                        last = pe.matmul(PS[0:2 * PW, 2 + g // 2, :], vbd[0:r, b, c, at:at + 2 * PW], e2[0:r, g % 2, c, :],
                                         start=(g % 2 == 0 and c == 0), stop=(g % 2 == 1 and c == NC - 1))
                    last.then_inc(pv_mm, 1)

                def back(a):
                    pe.wait_ge(oT_copied, 2 * b + a + 1)
                    for t in range(TB):
                        last = pe.transpose(PS[:, 2 + a, 2 * PW * t:2 * PW * t + 2 * PW], oT[a][:, P * t:P * t + P],
                                            ident[0:2 * PW, 0:2 * PW])
                    last.then_inc(oback_mm, 1)

                pe.wait_ge(nm2_ready, b + 1)
                pe.wait_ge(onehot_ready, 1)
                for g in range(NG):
                    pe.wait_ge(k_ready, NG * (2 * b + 1) + g + 1)
                    for c in range(NC):
                        n = NC * g + c
                        if n >= 2:
                            pe.wait_ge(e2_ready, NG * NC * b + n - 1)
                        r, at = crows(c), GW * g + CW * c
                        bank = PS[0:r, n % 2, :]
                        pe.matmul(bank, kst2[:, at:at + r], qst[:, g, :], start=True, stop=False)
                        pe.matmul(bank, onehr[:, at:at + r], nm2[:, :], start=False, stop=True).then_inc(sc2_mm, 1)
                    if g >= 1:
                        values(g - 1)
                    fill(f"g{g}")
                values(NG - 1)
                back(0)
                fill("pv")
                back(1)
                project_out(b, wa_s[:, 3 * D:4 * D], fill)

            def split_mm(bank, wh, wl, b):
                pe.matmul(bank, wh, xth[b][:, :], start=True, stop=False)
                pe.matmul(bank, wl, xth[b][:, :], start=False, stop=False)
                return pe.matmul(bank, wh, xtl[b][:, :], start=False, stop=True)

            def begin(layer, b, k):
                f, n = NB * layer + b, NE[layer]
                bt, bg, bw = begin_banks(layer, b)
                if k == 1:
                    if f == 0:
                        pe.wait_ge(sc1_out, TB + 2)
                    transposed(2 * layer + 1, b, bt)
                elif k == 2:
                    pe.wait_ge(rt_lo, layer + 1)
                    pe.wait_ge(xtl_ready, f + 1)
                    for t in range(TB):
                        bank = PS[:, bg, n * t:n * t + n]
                        for i, (a, w) in enumerate([(xth, rth), (xtl, rth), (xth, rtl), (xtl, rtl)]):
                            last = pe.matmul(bank, a[b][:, P * t:P * t + P], w[layer][:, :], start=(i == 0), stop=(i == 3))
                    last.then_inc(lg_mm, 1)
                elif k == 4:
                    pe.wait_ge(comb_ready, f + 1)
                    for t in range(TB):
                        last = pe.transpose(PS[0:2 * n, bw, P * t:P * t + P], comb[:, t, 0:2 * n], ident)
                    last.then_inc(combT_done, 1)

            def down(layer, b, j):
                i = chunks_before(layer, b) + j
                pe.wait_ge(u_ready, i + 1)
                pe.matmul(PS[:, BY, :], wdn_s[layer][:, D * j:D * j + D], u[:, i % 2, :], start=(j == 0),
                          stop=(j == NCH[layer] - 1)).then_inc(down_mm, 1)

            def chunk(layer, b, j):
                n, i, c = NE[layer], chunks_before(layer, b) + j, slice(P * j, P * j + P)
                wi = weighted_before(layer, b) + j
                if j == 0:
                    pe.wait_ge(up_lo, 2 if layer == 0 else 6)
                    pe.wait_ge(sel_ready, 1 if layer == 0 else 3)
                    pe.wait_ge(ct_ready, NB * layer + b + 1)
                    pe.wait_ge(d_dn[layer], 16)
                    if i:
                        pe.wait_ge(x_done[2 + 2 * ((NB * layer + b - 1) // NB)], (NB * layer + b - 1) % NB + 1)
                else:
                    pe.wait_ge(a_ready, i)
                split_mm(PS[:, BH, :], uph[layer][0][:, c], upl[layer][0][:, c], b).then_inc(h_mm, 1)
                if j < NWB[layer]:
                    if j:
                        pe.wait_ge(b_ready, wi)
                    pe.matmul(PS[:, BW, :], selr[layer][0:2 * n, c], ct[b][0:2 * n, :], start=True, stop=True).then_inc(w_mm, 1)
                if j >= 2:
                    down(layer, b, j - 2)
                if j:
                    pe.wait_ge(u_ready, i)
                split_mm(PS[:, BG, :], uph[layer][1][:, c], upl[layer][1][:, c], b).then_inc(g_mm, 1)

            def finish(layer, b):
                down(layer, b, NCH[layer] - 2)
                down(layer, b, NCH[layer] - 1)
                pe.wait_ge(yT_copied, NB * layer + b + 1)
                for t in range(TB):
                    last = pe.transpose(PS[:, BH, P * t:P * t + P], yT[:, P * t:P * t + P], ident)
                last.then_inc(y_mm, 1)

            def context(k):
                if k == 0:
                    pe.wait_ge(xc_ready, 2)
                    for b in range(NB):
                        last = pe.transpose(PS[:, 4, NK * b:NK * b + NK], xc[:, b, :], ident[0:NK, 0:NK])
                    last.then_inc(xcT_done, 1)
                elif k == 1:
                    pe.wait_ge(d_l1, 16)
                    pe.wait_ge(xcT_ready, 1)
                    for b in range(NB):
                        last = pe.matmul(PS[0:NK, 5 + b, 0:2 * D], xcT[:, b, :], wl1_s[:, D:3 * D], start=True, stop=True)
                    last.then_inc(ckv_mm, 1)
                else:
                    pe.wait_ge(kcn_ready, 1)
                    for b in range(NB):
                        last = pe.transpose(PS[:, 4, NK * b:NK * b + NK], kcn[:, b, :], ident[0:NK, 0:NK])
                    last.then_inc(kcT_done, 1)

            def attention1(b, fill):
                fill("n1")
                transposed(2, b, 0)
                fill("n2")
                pe.wait_ge(LT_ready, b + 1)
                for t in range(TB):
                    pe.matmul(PS[:, t, 0:3 * D], LT[:, P * t:P * t + P], wl1_s[:, 0:3 * D], start=True,
                              stop=True).then_inc(proj_mm, 1)
                fill("n3")
                fill("n4")
                pe.wait_ge(qkn_ready, b + 1)
                for n in range(2):
                    for t in range(TB):
                        last = pe.transpose(PS[:, n, P * t:P * t + P], qkn[:, t, D * n:D * n + D], ident)
                last.then_inc(qT_done, 1)
                pe.wait_ge(QT_ready, b + 1)
                pe.wait_ge(KT_ready, b + 1)

                def values(i):
                    h = i % HEADS1
                    hs = slice(DH1 * h, DH1 * h + DH1)
                    pe.wait_ge(ET_dve, NI * b + i + 1)
                    pe.wait_ge(ET_act, NI * b + i + 1)
                    out_ = PS[:, 3, DH1 * i:DH1 * i + DH1]
                    for c in range(TB):
                        pe.matmul(out_, ET[:, i % 2, c, :], V1[:, c, hs], start=(c == 0), stop=False)
                    pe.matmul(out_, ET[0:NK, i % 2, TB, :], vctx[:, b, hs], start=False, stop=True).then_inc(pv1_mm, 1)

                for i in range(NI):
                    t, h, n = i // HEADS1, i % HEADS1, NI * b + i
                    hs = slice(DH1 * h, DH1 * h + DH1)
                    if i:
                        pe.wait_ge(ET_act, n)
                    q = QT[hs, P * t:P * t + P]
                    pe.matmul(PS[:, 0, :], q, KT[hs, :], start=True, stop=True)
                    pe.matmul(PS[:, 1, 0:NK], q, kctxT[hs, b, :], start=True, stop=False)
                    pe.matmul(PS[:, 1, 0:NK], ones_row[:, :], mneg[:, b, :], start=False, stop=True).then_inc(sc_mm, 1)
                    fill(f"i{i}")
                    pe.wait_ge(E_ready, n + 1)
                    if i:
                        pe.wait_ge(ET_dve, n)
                    for c in range(TB):
                        pe.transpose(PS[:, 2, P * c:P * c + P], E[:, i % 2, P * c:P * c + P], ident)
                    pe.transpose(PS[0:NK, 1, P:2 * P], E[:, i % 2, S:S + NK], ident).then_inc(ET_done, 1)
                    if i:
                        values(i - 1)
                values(NI - 1)
                fill("pv")
                project_out(NB + b, wl1_s[:, 3 * D:4 * D], fill)

            schedule(prepare, queries, tile, context, begin, chunk, finish, attention0, attention1)

        @block.vector
        def _(dve):
            done = [0]

            def link(ins):
                done[0] += 1
                ins.then_inc(dve_step, 1)
                dve.wait_ge(dve_step, done[0])

            def norm_stats(k, b):
                if k == 0:
                    dve.wait_ge(d_x[b], 16)
                for t in range(TB * b, TB * b + TB):
                    last = dve.bn_stats(st[:, k, t, :], X[k][:, t, :])
                link(last)
                for t in range(TB * b, TB * b + TB):
                    last = dve.bn_aggr(mv[:, k, t, :], st[:, k, t, :])
                link(last)
                dve.tensor_scalar(ve[:, k, tiles(b)], mv[:, k, tiles(b), 1], LN_EPS, None, ALU.add).then_inc(ve_ready, 1)

            def norm(k, b):
                n = nth_norm(k, b)
                dve.wait_ge(rstd_ready, n + 1)
                if n:
                    dve.wait_ge(xnT_done, n)
                r = 6 if k == 2 else k
                for t in range(TB):
                    last = dve.tensor_scalar(xn[:, t, :], X[k][:, TB * b + t, :], mv[:, k, TB * b + t, 0:1],
                                             rstd[:, r, TB * b + t:TB * b + t + 1], ALU.subtract, ALU.mult)
                last.then_inc(xn_ready, 1)

            def small_weights():
                dve.wait_ge(d_wa, 32)
                for dst, n in ((wkr, 1), (wqr, 0)):
                    dve.tensor_copy(dst[:, :, :, :], bc(wa_s[:, D * n:D * n + D].rearrange("p (g j) -> p g j", g=NG)
                                                        .unsqueeze(2), [P, NG, 4, 32]))
                dve.wait_ge(d_vec, 16)
                for n, c in enumerate((ISQ / (S * NK * 4), ISQ / S, 1.0 / (S * (NK - 1)))):
                    dve.tensor_scalar(w1s[:, n, :], v("w1")[:, MH * n:MH * n + MH], c, None, ALU.mult)
                dve.tensor_copy(w3r[:, :], bc(v("w3")[0:MH, :], [MH, P]))
                dve.scalar_tensor_tensor(gqk[:, :], v("qg"), DH1 ** -0.5, v("kg"), ALU.mult, ALU.mult).then_inc(w_small, 1)

            def context_turned():
                dve.wait_ge(ctxT_done, 1)
                src = PS[:, 0, 0:NB * NK].rearrange("p (b k) -> p b k", b=NB)
                dve.tensor_copy(ctxT[:, :, :], src).then_inc(ctxT_copied, 1)
                dve.tensor_copy(ctxr[:, :, :, :], bc(src.unsqueeze(2), [P, NB, HG, NK])).then_inc(ctxT_copied, 1)

            def keys():
                dve.wait_ge(krep_mm, 1)
                for g in range(NG):
                    last = dve.tensor_scalar(krep[:, g].rearrange("p b k -> p (b k)"),
                                             PS[:, 1 + g // 2, NB * NK * (g % 2):NB * NK * (g % 2 + 1)],
                                             v("bk")[:, g:g + 1], None, ALU.add)
                link(last)

            def values():
                dve.tensor_reduce(ksum[:, :, :], krep[:, :, :, :], X_AXIS, ALU.add)
                dve.wait_ge(v_mm, 1)
                for b in range(NB):
                    for c in range(NC):
                        n, r = NC * b + c, crows(c)
                        last = dve.tensor_tensor(tmpv[0:r, b, c, :], PS[0:r, 3 + n // 4, D * (n % 4):D * (n % 4) + D],
                                                 v("bv")[0:r, :], ALU.add)
                link(last)
                dve.wait_ge(pool_const, 1)
                for b in range(NB):
                    for c in range(NC):
                        r = crows(c)
                        slots = vbd_slots(r, b, c)
                        own = cst[0:r, CO["vm"]].rearrange("p (c h) -> p c h", c=NC)[:, c, :]
                        dve.tensor_copy(slots[:, :, :, DK], bc(own.unsqueeze(1), [r, NG, HG]))
                        last = dve.tensor_tensor(slots[:, :, :, 0:DK],
                                                 tmpv[0:r, b, c, :].rearrange("p (g h d) -> p g h d", g=NG, h=HG),
                                                 bc(own.unsqueeze(1).unsqueeze(3), [r, NG, HG, DK]), ALU.mult)
                last.then_inc(v_ready, 1)

            def low_keys(dst, src, nth):
                for g in range(NG):
                    c = slice(GW * g, GW * g + GW)
                    dve.wait_ge(k_hi, NG * nth + g + 1)
                    dve.scalar_tensor_tensor(dst[:, c], khi[:, c].bitcast(F32), cst[:, CO["nlo"]], src(g),
                                             ALU.mult, ALU.add).then_inc(k_ready, 1)

            def prepare(b, k):
                if k == 0:
                    norm_stats(0, b)
                elif k == 1:
                    norm(0, b)
                    if b == 0:
                        small_weights()
                        context_turned()
                        keys()
                else:
                    for g in range(NG):
                        dve.tensor_tensor(kbd[:, g], bc(krep[:, g, b, :].unsqueeze(1), [P, HG, NK]),
                                          bc(cst[:, CO["hm"]].unsqueeze(2), [P, HG, NK]), ALU.mult).then_inc(k_raw, 1)
                    if b == 0:
                        values()
                    low_keys(kst, lambda g: kbd[:, g].rearrange("p h k -> p (h k)"), 2 * b)

            def queries(b, g):
                lo = slice(64, 128)
                dve.wait_ge(q_hi, NG * b + g + 1)
                dve.scalar_tensor_tensor(qst[lo, g, :], PS[lo, query_bank(b, g), :], v("bq")[lo, g:g + 1],
                                         qst[lo, g, :].bitcast(F32), ALU.add, ALU.subtract).then_inc(q_ready, 1)

            def spread(b, t):
                dve.wait_ge(e1_ready, TB * b + t + 1)
                for h in range(H):
                    last = dve.bn_stats(stats[:, H * t + h, :], sh[:, t % 2, h, :])
                link(last)

            def tile(b, t):
                dve.wait_ge(sc1_mm, TB * b + t + 1)
                at = tile_bank(b, t)
                sc = PS[:, at:at + NG, 0:GW].rearrange("p g (h k) -> p g h k", k=NK)
                m = mx[:, t, :].rearrange("p (g h) -> p g h", g=NG)
                link(dve.tensor_reduce(m, sc, X_AXIS, ALU.max))
                dve.tensor_tensor(sh[:, t % 2].rearrange("p (g h) k -> p g h k", g=NG), sc,
                                  bc(m.unsqueeze(3), [P, NG, HG, NK]), ALU.subtract).then_inc(sc1_out, 1)
                if t >= 1:
                    spread(b, t - 1)

            def attention0(b, fill):
                for t in range(2 * b, TB):
                    tile(b, t)
                    fill(f"t{t}")
                spread(b, TB - 1)
                me, s2e, mo, s2o = (stats[:, :, n] for n in (1, 2, 4, 5))
                ne, no = (NK + 1) // 2, NK // 2
                link(dve.tensor_scalar(sw[:, 0, :], me, float(ne), None, ALU.mult))
                link(dve.scalar_tensor_tensor(sw[:, 1, :], mo, float(no), sw[:, 0, :], ALU.mult, ALU.add))
                link(dve.tensor_tensor(sw[:, 2, :], me, mo, ALU.subtract))
                link(dve.scalar_tensor_tensor(sw[:, 3, :], sw[:, 2, :], ne * no / NK, sw[:, 2, :], ALU.mult, ALU.mult))
                link(dve.tensor_tensor(sw[:, 4, :], s2e, sw[:, 3, :], ALU.add))
                link(dve.tensor_tensor(sw[:, 5, :], s2o, sw[:, 4, :], ALU.add))
                link(dve.reciprocal(sw[:, 0, :], sw[:, 1, :]))
                link(dve.tensor_tensor(sw[:, 2, :], sw[:, 5, :], sw[:, 0, :], ALU.mult))
                dve.tensor_tensor(vp[:, b, :], sw[:, 2, :], sw[:, 0, :], ALU.mult)
                link(dve.tensor_tensor(qk1[:, b, :], qsum[:, b, :], ksum[:, :, b], ALU.mult))
                dve.tensor_tensor(pk[:, b], bc(qk1[:, b, :].unsqueeze(2), [P, NG, HG]),
                                  bc(cst[:, CO["hm"]].unsqueeze(1), [P, NG, HG]), ALU.mult).then_inc(feats, 1)
                fill("s")
                fill("mlp1")
                fill("mlp2")
                dve.wait_ge(logt_mm, b + 1)
                link(dve.tensor_scalar(lt[:, b, 0, :], PS[:, 2, 0:H], v("b3"), LOG_T_MIN, ALU.add, ALU.max))
                dve.tensor_scalar(lt[:, b, 1, :], lt[:, b, 0, :], LOG_T_MAX, None, ALU.min).then_inc(logt_in, 1)
                dve.wait_ge(invt_raw, b + 1)
                link(dve.tensor_scalar(rt[:, b, :], rt[:, b, :], 0.5, None, ALU.mult))
                for g in range(NG):
                    dve.tensor_tensor(kf2[:, GW * g:GW * g + GW].rearrange("p (h k) -> p h k", k=NK), kbd[:, g],
                                      bc(rt[:, b, HG * g:HG * g + HG].unsqueeze(2), [P, HG, NK]), ALU.mult
                                      ).then_inc(k_raw2, 1)
                link(dve.tensor_tensor(rd[:, b, :], rt[0:H, b, :], cst[0:H, CO["eye"]], ALU.mult))
                link(dve.tensor_reduce(rneg[:, b:b + 1], rd[:, b, :], X_AXIS, ALU.add, negate=True))
                dve.wait_ge(mxT_done, b + 1)
                dve.tensor_scalar(nm2[:, :], PS[0:H, 3, :], rneg[:, b:b + 1], None, ALU.mult).then_inc(nm2_ready, 1)
                low_keys(kst2, lambda g: kf2[:, GW * g:GW * g + GW], 2 * b + 1)
                fill("logt")
                fill("keys")

                def divide(a):
                    dve.wait_ge(oback_mm, 2 * b + a + 1)
                    raw_o = PS[:, 2 + a, 0:TB * 2 * PW].rearrange("p (t h d) -> p t h d", t=TB, d=DK + 1)
                    link(dve.tensor_scalar(omin[:, a], raw_o, 0.0, None, ALU.min))
                    link(dve.scalar_tensor_tensor(onum[:, a], raw_o, 0.0, omin[:, a], ALU.max, ALU.add))
                    link(dve.tensor_scalar(oden[:, a, 0], onum[:, a, :, :, DK], 1e-30, None, ALU.max))
                    link(dve.reciprocal(oden[:, a, 1], oden[:, a, 0]))
                    w = 2 * HG * DK
                    return dve.tensor_tensor(ao[:, :, w * a:w * a + w].rearrange("p t (h d) -> p t h d", d=DK),
                                             onum[:, a, :, :, 0:DK], bc(oden[:, a, 1].unsqueeze(3), [P, TB, 2 * HG, DK]),
                                             ALU.mult)

                for g in range(NG):
                    fill(f"g{g}")
                divide(0)
                fill("pv")
                divide(1).then_inc(ao_ready, 1)
                fill("o1")
                fill("o2")
                attended(1, b, b + 1)

            def residual(k, b, src, bank):
                dve.tensor_tensor(X[k][:, tiles(b), :], src[:, tiles(b), :], bank.rearrange("p (t c) -> p t c", t=TB),
                                  ALU.add).then_inc(x_done[k], 1)
                dve.wait_ge(x_done[k], b + 1)

            def attended(k, b, n):
                dve.wait_ge(oproj_mm, n)
                dve.wait_ge(xb_ready, n)
                residual(k, b, XB, PS[:, 1, :])

            def gate_top2(b, bank):
                n = E0
                link(dve.tensor_copy(lg[:, :, 0:n], PS[:, bank, 0:TB * n].rearrange("p (t e) -> p t e", t=TB)))
                for t in range(TB):
                    last = dve.max(m8[:, t, :], lg[:, t, 0:n])
                last.then_inc(lg_copied, 1)
                dve.wait_ge(lg_copied, b + 1)
                link(dve.tensor_copy(rv[:, :, 0:2], m8[:, :, 0:2]))
                for t in range(TB):
                    last = dve.match_replace(rp[:, t, :], rv[:, t, :], lg[:, t, :], BIG)
                dve.tensor_tensor(sc1[:, 0, :, 0:n], lg[:, :, 0:n], bc(m8[:, :, 0:1], [P, TB, n]), ALU.subtract
                                  ).then_inc(gate_in, 1)
                dve.wait_ge(gate_in, b + 1)
                link(dve.tensor_tensor(sc1[:, 2, :, 0:n], rp[:, :, 0:n], lg[:, :, 0:n], ALU.not_equal))
                dve.wait_ge(gate_exp, b + 1)
                link(dve.tensor_tensor(sc1[:, 3, :, 0:n], sc1[:, 1, :, 0:n], sc1[:, 2, :, 0:n], ALU.mult))
                link(dve.tensor_reduce(gsm[:, 0, :], sc1[:, 3, :, 0:n], X_AXIS, ALU.add))
                link(dve.reciprocal(gsm[:, 1, :], gsm[:, 0, :]))
                link(dve.tensor_scalar(gsm[:, 1, :], gsm[:, 1, :], 0.5, None, ALU.mult))
                copies = comb[:, :, 0:2 * n].rearrange("p t (a e) -> p t a e", a=2)
                dve.tensor_tensor(copies, bc(sc1[:, 3, :, 0:n].unsqueeze(2), [P, TB, 2, n]),
                                  bc(gsm[:, 1, :].unsqueeze(2).unsqueeze(3), [P, TB, 2, n]), ALU.mult).then_inc(comb_ready, 1)

            def gate_groups(b, bank):
                n, ng = E1, 4
                dve.tensor_copy(sc1[:, 0, :, :], PS[:, bank, 0:TB * n].rearrange("p (t e) -> p t e", t=TB)
                                ).then_inc(lg_copied, 1)
                dve.wait_ge(lg_copied, NB + b + 1)
                dve.memset(lg[:, :, ng:E0], -BIG).then_inc(gate_in, 1)
                dve.wait_ge(gate_exp, NB + b + 1)
                link(dve.tensor_scalar(sc1[:, 2, :, :], sc1[:, 1, :, :], 1.0, None, ALU.add))
                link(dve.reciprocal(sc1[:, 3, :, :], sc1[:, 2, :, :]))
                link(dve.tensor_tensor(sc1[:, 4, :, :], sc1[:, 3, :, :], bc(v("gb").unsqueeze(1), [P, TB, n]), ALU.add))
                for t in range(TB):
                    for g in range(ng):
                        last = dve.max(g8[:, t, g, :], sc1[:, 4, t, 8 * g:8 * g + 8])
                link(last)
                link(dve.tensor_tensor(lg[:, :, 0:ng], g8[:, :, :, 0], g8[:, :, :, 1], ALU.add))
                for t in range(TB):
                    last = dve.max(m8[:, t, :], lg[:, t, 0:8])
                link(last)
                link(dve.tensor_copy(rv[:, :, 0:2], m8[:, :, 0:2]))
                for t in range(TB):
                    last = dve.match_replace(rp[:, t, :], rv[:, t, :], lg[:, t, :], BIG)
                link(last)
                link(dve.tensor_tensor(rp[:, :, 8:8 + ng], rp[:, :, 0:ng], lg[:, :, 0:ng], ALU.not_equal))
                for t in range(TB):
                    last = dve.tensor_tensor(sc1[:, 5, t, :].rearrange("p (g e) -> p g e", g=ng),
                                             sc1[:, 4, t, :].rearrange("p (g e) -> p g e", g=ng),
                                             bc(rp[:, t, 8:8 + ng].unsqueeze(2), [P, ng, 8]), ALU.mult)
                link(last)
                link(dve.tensor_scalar(sc1[:, 5, :, :], sc1[:, 5, :, :], 0.0, None, ALU.add))
                for t in range(TB):
                    last = dve.max(m8[:, t, :], sc1[:, 5, t, :])
                link(last)
                for t in range(TB):
                    last = dve.match_replace(sc1[:, 6, t, :], m8[:, t, :], sc1[:, 5, t, :], BIG)
                link(last)
                link(dve.tensor_tensor(sc1[:, 7, :, :], sc1[:, 6, :, :], sc1[:, 5, :, :], ALU.not_equal))
                link(dve.tensor_tensor(sc1[:, 2, :, :], sc1[:, 7, :, :], sc1[:, 3, :, :], ALU.mult))
                link(dve.tensor_reduce(gsm[:, 0, :], sc1[:, 2, :, :], X_AXIS, ALU.add))
                link(dve.tensor_scalar(gsm[:, 0, :], gsm[:, 0, :], 1e-20, None, ALU.add))
                link(dve.reciprocal(gsm[:, 1, :], gsm[:, 0, :]))
                link(dve.tensor_scalar(gsm[:, 1, :], gsm[:, 1, :], 1.25, None, ALU.mult))
                copies = comb[:, :, :].rearrange("p t (a e) -> p t a e", a=2)
                dve.tensor_tensor(copies, bc(sc1[:, 2, :, :].unsqueeze(2), [P, TB, 2, n]),
                                  bc(gsm[:, 1, :].unsqueeze(2).unsqueeze(3), [P, TB, 2, n]), ALU.mult).then_inc(comb_ready, 1)

            def begin(layer, b, k):
                f, r = NB * layer + b, 2 * NE[layer]
                bt, bg, bw = begin_banks(layer, b)
                if k == 0:
                    norm_stats(2 * layer + 1, b)
                elif k == 1:
                    norm(2 * layer + 1, b)
                elif k == 2:
                    dve.wait_ge(xth_ready, f + 1)
                    dve.tensor_tensor(xtl[b][:, :], PS[:, bt, :], xth[b][:, :].bitcast(F32), ALU.subtract
                                      ).then_inc(xtl_ready, 1)
                elif k == 3:
                    dve.wait_ge(lg_mm, f + 1)
                    (gate_top2, gate_groups)[layer](b, bg)
                else:
                    dve.wait_ge(cth_ready, f + 1)
                    dve.scalar_tensor_tensor(ct[b][0:r, :], ct[b][0:r, :].bitcast(F32), cst[0:r, CO[f"nlo{layer}"]],
                                             PS[0:r, bw, :], ALU.mult, ALU.add).then_inc(ct_ready, 1)

            def chunk(layer, b, j):
                i, wi = chunks_before(layer, b) + j, weighted_before(layer, b) + j
                a = hg[:, i % 2, :]
                dve.wait_ge(th_ready, i + 1)
                dve.scalar_tensor_tensor(a, th[:, i % 2, :], 1.0, PS[:, BH, :], ALU.add, ALU.mult).then_inc(a_ready, 1)
                dve.wait_ge(a_ready, i + 1)
                if i >= 2:
                    dve.wait_ge(down_mm, i - 1)
                if j < NWB[layer]:
                    dve.wait_ge(w_mm, wi + 1)
                    dve.tensor_tensor(a, a, PS[:, BW, :], ALU.mult).then_inc(b_ready, 1)
                    dve.wait_ge(b_ready, wi + 1)
                    dve.wait_ge(g_mm, i + 1)
                    dve.tensor_tensor(u[:, i % 2, :], a, PS[:, BG, :], ALU.mult).then_inc(u_ready, 1)
                else:
                    dve.wait_ge(g_mm, i + 1)
                    dve.scalar_tensor_tensor(u[:, i % 2, :], a, 0.5, PS[:, BG, :], ALU.mult, ALU.mult).then_inc(u_ready, 1)

            def finish(layer, b):
                k = 2 + 2 * layer
                dve.wait_ge(y_mm, NB * layer + b + 1)
                residual(k, b, X[k - 1], PS[:, BH, :])

            def context(k):
                by_head = "p b (h d) -> p b h d"
                if k == 0:
                    for b in range(NB):
                        last = dve.bn_stats(st[0:NK, 4, b, :], ctx_s[:, b, :])
                    link(last)
                    for b in range(NB):
                        last = dve.bn_aggr(mv[0:NK, 4, b, :], st[0:NK, 4, b, :])
                    link(last)
                    dve.tensor_scalar(ve[0:NK, 4, 0:NB], mv[0:NK, 4, 0:NB, 1], LN_EPS, None, ALU.add).then_inc(cve_ready, 1)
                    dve.tensor_scalar(mneg[:, :, :].rearrange("p b k -> p (b k)"), mask_s[:, :], 1.0, 1e30, ALU.subtract,
                                      ALU.mult).then_inc(xc_ready, 1)
                    dve.wait_ge(crstd_ready, 1)
                    for b in range(NB):
                        last = dve.tensor_scalar(xc[:, b, :], ctx_s[:, b, :], mv[0:NK, 4, b, 0:1], rstd[0:NK, 4, b:b + 1],
                                                 ALU.subtract, ALU.mult)
                    last.then_inc(xc_ready, 1)
                elif k == 1:
                    dve.wait_ge(cv_ready, 1)
                    link(dve.tensor_reduce(ssc[:, 0], sqc[:, :, :].rearrange(by_head, h=HEADS1), X_AXIS, ALU.add))
                    dve.tensor_scalar(ssc[:, 1], ssc[:, 0], 1.0 / DH1, 1e-16, ALU.mult, ALU.max).then_inc(cssm_ready, 1)
                else:
                    dve.wait_ge(crs_ready, 1)
                    dve.tensor_tensor(kcn[:, :, :].rearrange(by_head, h=HEADS1),
                                      PS[0:NK, 5:5 + NB, 0:D].rearrange(by_head, h=HEADS1),
                                      bc(ssc[:, 2].unsqueeze(3), [NK, NB, HEADS1, DH1]), ALU.mult).then_inc(kcn_ready, 1)

            def attention1(b, fill):
                norm_stats(2, b)
                fill("n1")
                norm(2, b)
                fill("n2")
                dve.wait_ge(sq_ready, TB * (b + 1))
                by_head = "p t (n d) -> p t n d"
                link(dve.tensor_reduce(ss[:, :, :], sq.rearrange(by_head, n=4), X_AXIS, ALU.add))
                dve.tensor_scalar(ssm[:, :, :], ss[:, :, :], 1.0 / DH1, 1e-16, ALU.mult, ALU.max).then_inc(ssm_ready, 1)
                fill("n3")
                dve.wait_ge(rs_ready, b + 1)
                dve.wait_ge(V_ready, b + 1)
                dve.tensor_tensor(qkn.rearrange(by_head, n=4), PS[:, 0:TB, 0:2 * D].rearrange(by_head, n=4),
                                  bc(rs[:, :, :].unsqueeze(3), [P, TB, 4, DH1]), ALU.mult).then_inc(qkn_ready, 1)
                fill("n4")
                dve.wait_ge(qT_done, b + 1)
                dve.tensor_scalar(QT[:, :], PS[:, 0, :], gqk[:, :], None, ALU.mult).then_inc(QT_ready, 1)
                for i in range(NI):
                    n = NI * b + i
                    dve.wait_ge(sc_mm, n + 1)
                    dve.tensor_reduce(nmx[:, i:i + 1], PS[:, 0:2, :].rearrange("p a n -> p (a n)")[:, 0:S + NK],
                                      X_AXIS, ALU.max, negate=True).then_inc(max_ready, 1)
                    fill(f"i{i}")
                    dve.wait_ge(ET_done, n + 1)
                    if n >= 2:
                        dve.wait_ge(pv1_mm, n - 1)
                    dve.tensor_copy(ET[:, i % 2, 0:TB, :], PS[:, 2, :].rearrange("p (c q) -> p c q", c=TB)).then_inc(ET_dve, 1)
                dve.wait_ge(E_ready, NI * (b + 1))
                link(dve.reciprocal(rden[:, :], den[:, :]))
                dve.wait_ge(pv1_mm, NI * (b + 1))
                dve.tensor_tensor(ao[:, :, :].rearrange("p t (h d) -> p (t h) d", h=HEADS1),
                                  PS[:, 3, :].rearrange("p (i d) -> p i d", d=DH1),
                                  bc(rden[:, :].unsqueeze(2), [P, NI, DH1]), ALU.mult).then_inc(ao_ready, 1)
                fill("pv")
                fill("o1")
                fill("o2")
                attended(3, b, NB + b + 1)

            schedule(prepare, queries, tile, context, begin, chunk, finish, attention0, attention1)


def shape_constants():
    import numpy as np
    p = np.arange(P)
    c = np.zeros((P, NCC), np.float32)
    c[:, CO["ident"]] = np.eye(P)
    c[:, CO["hm"]] = (p[:, None] % 32) // DK == np.arange(HG)[None]
    c[:, CO["nlo"]] = -1.0 * ((p[:, None] // 32 == 1) | (p[:, None] // 32 == 2))
    for n in range(NC):
        r = np.arange(min(CW, GW - CW * n))
        c[:len(r), CO["vm"].start + HG * n:CO["vm"].start + HG * (n + 1)] = (r[:, None] + CW * n) // NK == np.arange(HG)[None]
    c[:H, CO["eye"]] = np.eye(H)
    c[E0:2 * E0, CO["nlo0"]] = -1.0
    c[E1:2 * E1, CO["nlo1"]] = -1.0
    onehot = np.repeat(np.eye(H, dtype=np.float32), NK, axis=1)
    sel = [np.tile(np.repeat(np.eye(e, dtype=np.float32), n, axis=1), (2, 1)) for e, n in ((E0, HID0), (E1, HID1))]
    return c, onehot, sel


def kernel(**inputs):
    import numpy as np
    import concourse.bacc as bacc
    from concourse.bass_utils import run_bass_kernel_spmd as run

    i = {k: np.asarray(a) for k, a in inputs.items()}
    a, f, l, g = ({k[len(n):]: w for k, w in i.items() if k.startswith(n)}
                  for n in ("L0_xattn_", "L0_ffn_", "L1_xattn_", "L1_ffn_"))

    def channel_rows(w):
        return np.tile(w.reshape(NG, 32).T, (4, 1))

    def column(w):
        return np.tile(w.reshape(-1), P // w.size)[:, None]

    def rows(w):
        return np.broadcast_to(w.reshape(1, -1), (P, w.size))

    consts, onehot, (sel0, sel1) = shape_constants()
    vecs = dict(bq=channel_rows(a["bq"]), bk=channel_rows(a["bk"]), lxg=column(l["ln_x_g"]), lxb=column(l["ln_x_b"]),
                llg=column(l["ln_l_g"]), llb=column(l["ln_l_b"]), qg=column(l["q_gamma"]), kg=column(l["k_gamma"]),
                b1=column(a["b1"]), b2=column(a["b2"]), w3=column(a["w3"]), b3=column(a["b3"]), w1=rows(a["w1"].T),
                gb=rows(g["gate_bias"]), bo=rows(a["bo"]), bv=rows(a["bv"]), bout=rows(l["b_out"]))

    def hidden_last(w):
        return w.transpose(1, 0, 2).reshape(D, -1)

    arrays = dict(
        x=i["x"].reshape(NB * S, D), ctx=i["ctx_1024"], mask=i["mask_BxS2_bk0"].reshape(1, NB * NK).astype(np.int32),
        vecs=np.concatenate([vecs[k] for k in V_COLS], axis=1),
        wa=np.concatenate([a[k].T for k in ("Wq", "Wk", "Wv", "Wo")], axis=1), w2t=a["w2"].T, wr=f["Wr"],
        up0=np.stack([hidden_last(f["W1"]), hidden_last(f["W3"])]), wdn0=f["W2"].reshape(-1, D),
        wl1=np.concatenate([l["W_q"], l["W_kv"], l["W_out"]], axis=1), gw=g["gate_w"].T,
        up1=np.stack([np.concatenate([g[f"expert_{k}"].transpose(2, 0, 1).reshape(D, -1), g[f"shared_{k}"].T], axis=1)
                      for k in ("gate", "up")]),
        wdn1=np.concatenate([g["expert_down"].transpose(0, 2, 1).reshape(-1, D), g["shared_down"].T], axis=0),
        consts=consts, onehot=onehot, sel0=sel0, sel1=sel1)
    nc = bacc.Bacc("TRN2", target_bir_lowering=False, num_devices=1)
    fed, args = {}, {}
    for name, w in arrays.items():
        w = np.ascontiguousarray(w)
        fed[f"in_{name}"] = w
        args[name] = nc.dram_tensor(f"in_{name}", w.shape, mybir.dt.from_np(w.dtype), kind="ExternalInput").ap()
    out = nc.dram_tensor("out_x", (NB * S, D), F32, kind="ExternalOutput").ap()
    program(nc, out=out, **args)
    r = run(nc, [fed], core_ids=[0])
    return r.results[0]["out_x"].reshape(NB, S, D)
```

```python
from contextlib import ExitStack

import concourse.bass as bass
from concourse import mybir

F32 = mybir.dt.float32
F32R = mybir.dt.float32r
I32 = mybir.dt.int32
ALU = mybir.AluOpType
ACT = mybir.ActivationFunctionType
X_AXIS = mybir.AxisListType.X

P = 128
NB, S, D = 2, 512, 128
TB = S // P
NK = 77
H, DK = 16, 8
NG, HG = 4, 4
GW = HG * NK
NC, CW = 3, 103
PW = HG * (DK + 1)
MH = 64
E0, HID0 = 8, 192
E1, HID1 = 32, 64
J0 = E0 * HID0 // P
J1 = E1 * HID1 // P
HEADS1, DH1 = 2, 64
LN_EPS = 1e-5
BIG = 3.0e38
LOG_T_MIN, LOG_T_MAX = -2.302585092994046, 2.302585092994046

V_COLS = dict(bq=4, bk=4, lxg=1, lxb=1, llg=1, llb=1, qg=1, kg=1, b1=1, b2=1, w3=1, b3=1,
              w1=3 * MH, gb=E1, bo=D, bv=D, bout=D)
C_COLS = dict(ident=P, hm=HG, nlo=1, vm=NC * HG, eye=H, nlo0=1, nlo1=1)


def offsets(cols):
    at, out = 0, {}
    for name, n in cols.items():
        out[name] = slice(at, at + n)
        at += n
    return out, at


VO, NV = offsets(V_COLS)
CO, NCC = offsets(C_COLS)


def program(nc, x, ctx, mask, vecs, wa, w2t, wr, up0, wdn0, wl1, gw, up1, wdn1, consts, onehot,
            sel0, sel1, out):
    with ExitStack() as stack:
        def sb(name, shape, dt=F32):
            return stack.enter_context(nc.sbuf_tensor(name, shape, dt))

        def sem(name):
            return stack.enter_context(nc.semaphore(name))

        vec = sb("vec", [P, NV])
        cst = sb("cst", [P, NCC])
        ident = cst[:, CO["ident"]]

        def v(name):
            return vec[:, VO[name]]

        X = [sb(f"x_{n}", [P, NB * TB, D]) for n in range(3)]
        X += [X[1], X[0]]
        XB = sb("xb", [P, NB * TB, D])
        wa_s = sb("wa_s", [P, 4 * D])
        w2t_s = sb("w2t_s", [MH, MH])
        wqr = sb("wqr", [P, NG, 4, 32])
        wkr = sb("wkr", [P, NG, 4, 32])
        w1s = sb("w1s", [P, 3, MH])
        w3r = sb("w3r", [MH, P])
        ctx_s = sb("ctx_s", [NK, NB, D])
        mask_s = sb("mask_s", [1, NB * NK], I32)
        mneg = sb("mneg", [1, NB, NK])
        ones_row = sb("ones_row", [1, P])
        xc = sb("xc", [NK, NB, D])
        xcT = sb("xcT", [P, NB, NK])
        sqc = sb("sqc", [NK, NB, D])
        kcn = sb("kcn", [NK, NB, D])
        st = sb("st", [P, 5, NB * TB, 6])
        mv = sb("mv", [P, 5, NB * TB, 2])
        ve = sb("ve", [P, 5, NB * TB])
        rstd = sb("rstd", [P, 5, NB * TB])
        mhalf = sb("mhalf", [P, 20])
        xn = sb("xn", [P, TB, D])
        onehr = sb("onehr", [H, H * NK], F32R)
        wl1_s = sb("wl1_s", [P, 4 * D])
        aoT = sb("aoT", [P, S])
        ao = sb("ao", [P, TB, D])
        gqk = sb("gqk", [P, 1])
        rt_s = [sb("wr_s", [P, E0]), sb("gw_s", [P, E1])]
        rhl = [sb("wr_hl", [P, 2 * E0], F32R), sb("gw_hl", [P, 2 * E1], F32R)]
        rth, rtl = [m[:, 0:n] for m, n in zip(rhl, (E0, E1))], [m[:, n:2 * n] for m, n in zip(rhl, (E0, E1))]
        lg = sb("lg", [P, TB, 2 * E0])
        m8 = sb("m8", [P, TB, 8])
        rv = sb("rv", [P, TB, 8])
        rp = sb("rp", [P, TB, 2 * E0])
        sc1 = sb("sc1", [P, 8, TB, E1])
        g8 = sb("g8", [P, TB, 4, 8])
        gsm = sb("gsm", [P, 2, TB])
        comb = sb("comb", [P, TB, 2 * E1])
        xth, xtl, ct = [sb("xth_0", [P, S], F32R)], [sb("xtl_0", [P, S], F32R)], [sb("ct_0", [2 * E1, S], F32R)]
        th = sb("th", [P, 2, S])
        hg = sb("hg", [P, 2, S])
        u = sb("u", [P, 2, S])
        yT = th[:, 0, :]
        ss = sb("ss", [P, TB, 4])
        ssm = sb("ssm", [P, TB, 4])
        rs = sb("rs", [P, TB, 4])
        ssc = sb("ssc", [NK, 3, NB, 2])
        kctxT = sb("kctxT", [P, NB, NK])
        vctx = sb("vctx", [NK, NB, D])
        NW = (J1 + 1) * P
        kept, stack = stack, stack.enter_context(ExitStack())
        raw0 = [sb(f"raw0_{n}", [P, J0 * P]) for n in range(2)]
        uph0 = [sb(f"uph0_{n}", [P, J0 * P], F32R) for n in range(2)]
        upl0 = [sb(f"upl0_{n}", [P, J0 * P], F32R) for n in range(2)]
        wdn0_s = sb("wdn0_s", [P, J0 * D])
        sel0r = sb("sel0r", [2 * E0, J0 * P], F32R)
        inner, stack = stack, stack.enter_context(ExitStack())
        ctxT = sb("ctxT", [P, NB, NK])
        ctxr = sb("ctxr", [P, NB, HG, NK])
        XT = hg[:, 0, :]
        krep = sb("krep", [P, NG, NB, NK])
        ksum = sb("ksum", [P, NG, NB])
        kbd = sb("kbd", [P, NG, HG, NK])
        khi = sb("khi", [P, H * NK], F32R)
        kst = sb("kst", [P, H * NK], F32R)
        sh = sb("sh", [P, 2, H, NK])
        stats = sb("stats", [P, TB * H, 6])
        kf2 = sb("kf2", [P, H * NK])
        kst2 = sb("kst2", [P, H * NK], F32R)
        vbd = sb("vbd", [CW, NB, NC, 3 * NG * PW])
        qst = sb("qst", [P, NB, NG, S], F32R)
        qsum = sb("qsum", [P, NB, NG])
        mx = sb("mx", [P, TB, H])
        sw = sb("sw", [P, 6, TB * H])
        vp = sb("vp", [P, NB, TB * H])
        pk = sb("pk", [P, NB, NG, HG])
        qk1 = sb("qk1", [P, NB, NG])
        h1 = sb("h1", [MH, NB, H])
        h2 = sb("h2", [MH, NB, H])
        lt = sb("lt", [P, NB, 2, H])
        rt = sb("rt", [P, NB, H])
        rd = sb("rd", [H, NB, H])
        rneg = sb("rneg", [H, NB])
        nm2 = sb("nm2", [H, S], F32R)
        e2 = sb("e2", [CW, 2, NC, S])
        tmpv = e2[:, 0, 0:2, :].rearrange("p a n -> p (a n)")[:, 0:NB * NC * D].rearrange("p (b c n) -> p b c n", b=NB, c=NC)
        oT = [m[0:2 * PW, :] for m in (ao[:, :, :].rearrange("p t c -> p (t c)"), aoT[:, :])]
        omin, onum = (kf2[:, 2 * TB * 2 * PW * n:2 * TB * 2 * PW * (n + 1)].rearrange(
            "p (a t h d) -> p a t h d", a=2, t=TB, d=DK + 1)
                      for n in range(2))
        oden = sb("oden", [P, 2, 2, TB, 2 * HG])
        stack.close()
        stack = inner
        LT = sb("LT", [P, S])
        V1, QT, KT = ([sb(f"{n}_0", [P, S])] for n in ("V1", "QT", "KT"))
        for n, m in enumerate((V1, QT, KT)):
            m.append(wdn0_s[:, S * n:S * n + S])
        nmx = sb("nmx", [P, TB * HEADS1])
        E = sb("E", [P, 2, S + NK])
        ET = sb("ET", [P, 2, 5, P])
        sq = [m[:, 0:TB * 2 * D].rearrange("p (t n) -> p t n", t=TB) for m in (
            E[:, :, :].rearrange("p a n -> p (a n)"), sc1[:, :, :, :].rearrange("p a t e -> p (a t e)"))]
        qkn = sq
        xth.append(sb("xth_1", [P, S], F32R))
        xtl.append(sb("xtl_1", [P, S], F32R))
        ct.append(sb("ct_1", [2 * E1, S], F32R))
        den = sb("den", [P, TB * HEADS1])
        rden = sb("rden", [P, TB * HEADS1])
        uph1 = [sb(f"uph1_{n}", [P, NW], F32R) for n in range(2)]
        upl1 = [sb(f"upl1_{n}", [P, NW], F32R) for n in range(2)]
        wdn1_s = sb("wdn1_s", [P, NW])
        sel1r = sb("sel1r", [2 * E1, J1 * P], F32R)
        uph, upl, wdn_s, selr = (uph0, uph1), (upl0, upl1), (wdn0_s, wdn1_s), (sel0r, sel1r)

        PS = stack.enter_context(nc.psum_tensor("PS", [P, 8, 512], F32))

        def sems(names):
            return [sem(n) for n in names.split()]

        d_x, d_up0 = ([sem(f"d_{k}{n}") for n in range(2)] for k in ("x", "up0_"))
        d_piece = [sem(f"d_piece{n}") for n in range(6)]
        d_vec, d_cst, d_ctx, d_wa, d_oneh, d_w0, d_sel0, d_dn0, d_l1, d_dn1, d_mask, d_w2, d_out = sems(
            "d_vec d_cst d_ctx d_wa d_oneh d_w0 d_sel0 d_dn0 d_l1 d_dn1 d_mask d_w2 d_out")
        d_dn = (d_dn0, d_dn1)
        dve_step, k_raw2 = sems("dve_step k_raw2")
        pool_const, ve_ready, rstd_ready, xn_ready, xnT_done, xb_ready = sems(
            "pool_const ve_ready rstd_ready xn_ready xnT_done xb_ready")
        x_done = [None] + [sem(f"x{k}_done") for k in range(1, 5)]
        w_small, ctxT_done, ctxT_copied, krep_mm, k_raw, k_hi, k_ready, v_mm, v_ready = sems(
            "w_small ctxT_done ctxT_copied krep_mm k_raw k_hi k_ready v_mm v_ready")
        mx_ready, e1_read, w_copied = sems("mx_ready e1_read w_copied")
        XT_ready, q_mm, q_hi, q_ready, sc1_mm, sc1_out, e1_ready, feats, hid_mm, hid_act, logt_mm, logt_in = sems(
            "XT_ready q_mm q_hi q_ready sc1_mm sc1_out e1_ready feats hid_mm hid_act logt_mm logt_in")
        invt_raw, mxT_done, nm2_ready, onehot_ready, sc2_mm, e2_ready, pv_mm, oT_copied, oback_mm = sems(
            "invt_raw mxT_done nm2_ready onehot_ready sc2_mm e2_ready pv_mm oT_copied oback_mm")
        ao_ready, aoT_done, aoT_copied, oproj_mm = sems("ao_ready aoT_done aoT_copied oproj_mm")
        sel_ready, up_hi, up_lo, rt_hi, rt_lo, xth_ready, xtl_ready, lg_mm, lg_copied, gate_in, gate_exp = sems(
            "sel_ready up_hi up_lo rt_hi rt_lo xth_ready xtl_ready lg_mm lg_copied gate_in gate_exp")
        comb_ready, combT_done, cth_ready, ct_ready, h_mm, g_mm, w_mm, th_ready, a_ready, b_ready, u_ready = sems(
            "comb_ready combT_done cth_ready ct_ready h_mm g_mm w_mm th_ready a_ready b_ready u_ready")
        down_mm, yT_copied, y_mm = sems("down_mm yT_copied y_mm")
        cve_ready, crstd_ready, xc_ready, xcT_done, xcT_ready, ckv_mm, cv_ready, cssm_ready, crs_ready, kcn_ready = sems(
            "cve_ready crstd_ready xc_ready xcT_done xcT_ready ckv_mm cv_ready cssm_ready crs_ready kcn_ready")
        kcT_done, kctx_ready, LT_ready, proj_mm, sq_ready, ssm_ready, rs_ready, qkn_ready, V_ready, qT_done = sems(
            "kcT_done kctx_ready LT_ready proj_mm sq_ready ssm_ready rs_ready qkn_ready V_ready qT_done")
        QT_ready, KT_ready, sc_mm, max_ready, E_ready, ET_done, ET_dve, ET_act, pv1_mm = sems(
            "QT_ready KT_ready sc_mm max_ready E_ready ET_done ET_dve ET_act pv1_mm")

        NCH = (J0, J1 + 1)
        NWB = (J0, J1)
        NE = (E0, E1)
        ISQ = DK ** -0.5
        NI = TB * HEADS1
        BH, BG, BW, BY = 4, 5, 6, 7
        HALF = NW // 2
        PIECES = [(0, 0), (0, 1), (1, 0), (1, 1), (2, 0), (2, 1)]
        ORDER = [(0, 0), (0, 1), (1, 0), (2, 0), (1, 1), (2, 1), (3, 0), (3, 1)]

        def nth_norm(k, b):
            return ORDER.index((k, b))

        def chunks_before(layer, b):
            return (0 if layer == 0 else NB * NCH[0]) + b * NCH[layer]

        def weighted_before(layer, b):
            return (0 if layer == 0 else NB * NWB[0]) + b * NWB[layer]

        def tiles(b):
            return slice(TB * b, TB * b + TB)

        def crows(c):
            return min(CW, GW - CW * c)

        def bc(ap, shape):
            return ap.broadcast_to(shape)

        HEAD1 = 4
        PRE = 7
        BESIDE_A0 = dict(mlp1=1, mlp2=1, keys=3, g0=6, g1=1, g2=1, g3=1, o2=1)
        BESIDE_A1 = dict(s1=1, s=3, mlp1=5, mlp2=5, logt=1, keys=2, g0=2, g1=2, g2=2, o1=2, o2=2)
        BESIDE_B = [dict(i0=2, i1=7, i2=5, i3=1, i4=3, i5=1, i6=2, i7=2, o1=2),
                    dict(i0=4, i1=2, i2=1, i3=1, i4=1, i5=2, i6=1, i7=2, pv=4, o2=1, between=1)]
        assert sum(BESIDE_A1.get(p, 0) for p in ("s0", "s1", "s", "mlp1", "mlp2", "logt", "keys")) <= PRE + NCH[0] + 1

        def beside(step, total, plan):
            at = [0]

            def fill(point=None):
                end = total if point is None else min(total, at[0] + plan.get(point, 0))
                for k in range(at[0], end):
                    step(k)
                at[0] = end
            return fill

        def schedule(prepare, queries, tile, tiles_end, context, begin, chunk, finish, attention0, head1, attention1):
            def first(k):
                if k < 3:
                    context(k)
                elif k < 6:
                    prepare(1, k - 3)
                elif k < 6 + NG:
                    queries(1, k - 6)
                elif k < 6 + NG + TB:
                    tile(1, k - 6 - NG)
                else:
                    tiles_end(1, k - 6 - NG - TB)

            def experts(layer, b):
                def step(k):
                    if k < PRE:
                        begin(layer, b, k)
                    elif k < PRE + NCH[layer]:
                        chunk(layer, b, k - PRE)
                    elif k == PRE + NCH[layer]:
                        finish(layer, b)
                    else:
                        head1(b, k - PRE - NCH[layer] - 1)
                return step

            for k in range(3):
                prepare(0, k)
            for g in range(NG):
                queries(0, g)
            rest = beside(first, 6 + NG + TB + 2, BESIDE_A0)
            attention0(0, rest)
            rest()
            rest = beside(experts(0, 0), PRE + NCH[0] + 1 + HEAD1, BESIDE_A1)
            attention0(1, rest)
            rest()
            rest = beside(experts(0, 1), PRE + NCH[0] + 1 + HEAD1, BESIDE_B[0])
            attention1(0, rest)
            rest()
            rest = beside(experts(1, 0), PRE + NCH[1] + 1, BESIDE_B[1])
            attention1(1, rest)
            for k in range(PRE):
                begin(1, 1, k)
                rest("between")
            rest()
            for k in range(PRE, PRE + NCH[1] + 1):
                experts(1, 1)(k)

        def nothing(*_):
            pass

        A0_POINTS = ("t0", "t1", "t2", "t3", "s0", "s1", "s", "mlp1", "mlp2", "logt", "keys", "g0", "g1", "g2", "g3", "pv",
                     "o1", "o2")

        def begin_banks(layer, b):
            return (0, 1, 2) if (layer, b) == (1, 1) else (BH, BG, BW)

        XT_BANK = (BH, BY)

        def vbd_slots(r, b, c):
            return vbd[0:r, b, c, :].rearrange("p (g a h d) -> p g a h d", g=NG, a=3, h=HG)[:, :, 0]

        block = stack.enter_context(nc.Block())

        @block.sync
        def _(sp):
            sp.dma_start(X[0][:, tiles(0), :], x[0:S].rearrange("(t p) c -> p t c", p=P)).then_inc(d_x[0], 16)
            sp.dma_start(raw0[1][0:H, 0:H * NK], onehot).then_inc(d_oneh, 16)
            sp.dma_start(mask_s[:, :], mask).then_inc(d_mask, 16)
            sp.dma_start(raw0[0][0:2 * E0, :], sel0).then_inc(d_sel0, 16)
            sp.dma_start(X[0][:, tiles(1), :], x[S:].rearrange("(t p) c -> p t c", p=P)).then_inc(d_x[1], 16)
            sp.dma_start(rt_s[0][:, :], wr).then_inc(d_w0, 16)
            sp.dma_start(rt_s[1][:, :], gw).then_inc(d_w0, 16)
            sp.wait_ge(sel_ready, 1)
            sp.dma_start(raw0[0][:, :], up0[0]).then_inc(d_up0[0], 16)
            sp.wait_ge(onehot_ready, 1)
            sp.dma_start(raw0[1][:, :], up0[1]).then_inc(d_up0[1], 16)
            sp.dma_start(wdn0_s[:, :].rearrange("p (j c) -> p j c", j=J0), wdn0.rearrange("(j p) c -> p j c", p=P)
                         ).then_inc(d_dn0, 16)
            sp.dma_start(wl1_s[:, :], wl1).then_inc(d_l1, 16)
            sp.wait_ge(x_done[1], NB)
            for n, (what, half) in enumerate(PIECES):
                if n < 2:
                    sp.wait_ge(up_lo, 2)
                elif n < 4:
                    sp.wait_ge(sel_ready, n)
                else:
                    sp.wait_ge(up_lo, n - 1)
                if what == 0:
                    w = J1 * P // 2
                    sp.dma_start(raw0[n % 2][0:2 * E1, 0:w], sel1[:, w * half:w * half + w]).then_inc(d_piece[n], 16)
                else:
                    sp.dma_start(raw0[n % 2][:, 0:HALF], up1[what - 1, :, HALF * half:HALF * half + HALF]
                                 ).then_inc(d_piece[n], 16)
            sp.dma_start(wdn1_s[:, :].rearrange("p (j c) -> p j c", c=D), wdn1.rearrange("(j p) c -> p j c", p=P)
                         ).then_inc(d_dn1, 16)
            for b in range(NB):
                sp.wait_ge(x_done[4], b + 1)
                sp.dma_start(out[S * b:S * b + S].rearrange("(t p) c -> p t c", p=P), X[4][:, tiles(b), :]
                             ).then_inc(d_out, 16)
            sp.wait_ge(d_out, 16 * NB)

        @block.gpsimd
        def _(pool):
            pool.dma_start(ctx_s[:, :, :], ctx.rearrange("b k c -> k b c")).then_inc(d_ctx, 16)
            pool.memset(mhalf[:, :], -0.5)
            pool.memset(ones_row[:, :], 1.0)
            pool.memset(vbd[:, :, :, :], 0.0)
            pool.memset(rv[:, :, :], -BIG)
            pool.memset(lg[:, :, :], -BIG).then_inc(pool_const, 1)
            pool.wait_ge(pool_const, 1)

            def inv_std(k, b):
                pool.wait_ge(ve_ready, nth_norm(k, b) + 1)
                pool.tensor_tensor(rstd[:, k, tiles(b)], ve[:, k, tiles(b)], mhalf[:, 0:TB], ALU.pow).then_inc(rstd_ready, 1)

            def add_bias(k, b, bias):
                for t in range(TB * b, TB * b + TB):
                    last = pool.tensor_tensor(XB[:, t, :], X[k][:, t, :], bias, ALU.add)
                last.then_inc(xb_ready, 1)

            def prepare(b, k):
                if k == 0:
                    inv_std(0, b)
                if b or k:
                    return
                pool.wait_ge(d_vec, 16)
                for n in range(NB):
                    pool.wait_ge(d_x[n], 16)
                    add_bias(0, n, v("bo"))
                pool.wait_ge(d_w0, 32)
                for layer in range(2):
                    pool.tensor_copy(rth[layer][:, :], rt_s[layer][:, :]).then_inc(rt_hi, 1)
                    pool.wait_ge(rt_hi, layer + 1)
                    pool.tensor_tensor(rtl[layer][:, :], rt_s[layer][:, :], rth[layer][:, :].bitcast(F32),
                                       ALU.subtract).then_inc(rt_lo, 1)

            def attention0(b, fill):
                for point in A0_POINTS[TB * b:]:
                    fill(point)
                    if point == "keys" and b == 0:
                        for n in range(2):
                            pool.wait_ge(up_hi, n + 1)
                            pool.tensor_tensor(upl0[n][:, :], raw0[n][:, :], uph0[n][:, :].bitcast(F32), ALU.subtract
                                               ).then_inc(up_lo, 1)

            def chunk(layer, b, j):
                i = chunks_before(layer, b) + j
                pool.wait_ge(a_ready, i + 1)
                pool.wait_ge(b_ready, i + 1)
                pool.tensor_tensor(u[:, i % 2, :], u[:, i % 2, :], hg[:, i % 2, :], ALU.mult).then_inc(u_ready, 1)

            def begin(layer, b, k):
                if k == 0:
                    inv_std(2 * layer + 1, b)

            def context(k):
                if k == 0:
                    pool.wait_ge(cve_ready, 1)
                    pool.tensor_tensor(rstd[0:NK, 4, 0:NB], ve[0:NK, 4, 0:NB], mhalf[0:NK, 0:NB], ALU.pow
                                       ).then_inc(crstd_ready, 1)
                elif k == 1:
                    pool.wait_ge(cssm_ready, 1)
                    pool.tensor_tensor(ssc[:, 2].rearrange("p b h -> p (b h)"), ssc[:, 1].rearrange("p b h -> p (b h)"),
                                       mhalf[0:NK, 0:NB * HEADS1], ALU.pow).then_inc(crs_ready, 1)

            def head1(b, k):
                if k == 0:
                    inv_std(2, b)
                elif k == 2:
                    add_bias(2, b, v("bout"))
                    pool.wait_ge(ssm_ready, b + 1)
                    pool.tensor_tensor(rs[:, :, :].rearrange("p a b -> p (a b)"), ssm[:, :, :].rearrange("p a b -> p (a b)"),
                                       mhalf[:, 0:4 * TB], ALU.pow).then_inc(rs_ready, 1)

            def attention1(b, fill):
                for i in range(NI):
                    fill(f"i{i}")
                    if b == 0 and i < len(PIECES) and PIECES[i][0]:
                        what, half = PIECES[i]
                        c = slice(HALF * half, HALF * half + HALF)
                        pool.wait_ge(up_hi, i + 1)
                        pool.tensor_tensor(upl1[what - 1][:, c], raw0[i % 2][:, 0:HALF],
                                           uph1[what - 1][:, c].bitcast(F32), ALU.subtract).then_inc(up_lo, 1)
                fill("pv")
                fill("o1")
                fill("o2")

            schedule(prepare, nothing, nothing, nothing, context, begin, chunk, nothing, attention0, head1, attention1)

        @block.scalar
        def _(act):
            act.dma_start(cst[:, :], consts).then_inc(d_cst, 16)
            act.dma_start(wa_s[:, :], wa).then_inc(d_wa, 16)
            act.dma_start(vec[:, :], vecs).then_inc(d_vec, 16)
            act.dma_start(w2t_s[:, :], w2t).then_inc(d_w2, 16)

            def copy(dst, src):
                return act.activation(dst, src, ACT.Copy)

            def split_keys(src, nth, ready, value):
                for g in range(NG):
                    act.wait_ge(ready, value + g)
                    if nth:
                        act.wait_ge(k_ready, NG * (nth - 1) + g + 1)
                    copy(khi[:, GW * g:GW * g + GW], src(g)).then_inc(k_hi, 1)

            def prepare(b, k):
                if k == 1:
                    act.wait_ge(xnT_done, nth_norm(0, b) + 1)
                    copy(XT[:, :], PS[:, XT_BANK[b], :]).then_inc(XT_ready, 1)
                elif k == 2:
                    split_keys(lambda g: kbd[:, g].rearrange("p h k -> p (h k)"), 2 * b, k_raw, NG * b + 1)

            def queries(b, g):
                act.wait_ge(q_mm, NG * b + g + 1)
                act.activation(qst[:, b, g, :], PS[:, BH + g, :], ACT.Identity, bias=v("bq")[:, g:g + 1],
                               accum_out=qsum[:, b, g:g + 1]).then_inc(q_hi, 1)

            def tile(b, t):
                if b == 0 and t == 0:
                    act.wait_ge(d_oneh, 16)
                    copy(onehr[:, :], raw0[1][0:H, 0:H * NK]).then_inc(onehot_ready, 1)
                    act.wait_ge(d_sel0, 16)
                    copy(sel0r[:, :], raw0[0][0:2 * E0, :]).then_inc(sel_ready, 1)
                if b == 0:
                    tile_exp(b, t)
                elif t:
                    tile_exp(b, t - 1)

            def tiles_end(b, k):
                if k == 0 and b:
                    tile_exp(b, TB - 1)

            def tile_exp(b, t):
                act.wait_ge(sc1_out, TB * b + t + 1)
                act.activation(sh[:, t % 2, :, :], sh[:, t % 2, :, :], ACT.Exp, scale=ISQ).then_inc(e1_ready, 1)

            def attention0(b, fill):
                for t in range(TB if b == 0 else 0):
                    tile(b, t)
                    fill(f"t{t}")
                if b == 0:
                    for n in range(2):
                        act.wait_ge(d_up0[n], 16)
                        copy(uph0[n][:, :], raw0[n][:, :]).then_inc(up_hi, 1)
                fill("s0")
                fill("s1")
                fill("s")
                act.wait_ge(hid_mm, 2 * b + 1)
                act.activation(h1[:, b, :], PS[0:MH, 0, 0:H], ACT.Gelu, bias=v("b1")[0:MH, :]).then_inc(hid_act, 1)
                fill("mlp1")
                act.wait_ge(hid_mm, 2 * b + 2)
                act.activation(h2[:, b, :], PS[0:MH, 0, 0:H], ACT.Gelu, bias=v("b2")[0:MH, :]).then_inc(hid_act, 1)
                fill("mlp2")
                act.wait_ge(logt_in, b + 1)
                act.activation(rt[:, b, :], lt[:, b, 1, :], ACT.Exp, scale=-1.0).then_inc(invt_raw, 1)
                fill("logt")
                split_keys(lambda g: kf2[:, GW * g:GW * g + GW], 2 * b + 1, k_raw2, NG * b + 1)
                fill("keys")

                def pair_copied(a):
                    act.wait_ge(pv_mm, NG * b + 2 * a + 2)
                    copy(oT[a], PS[0:2 * PW, 2 + a, :]).then_inc(oT_copied, 1)

                for g in range(NG):
                    for c in range(NC):
                        i = NG * NC * b + NC * g + c
                        act.wait_ge(sc2_mm, i + 1)
                        if NG * b + g >= 2:
                            act.wait_ge(pv_mm, NG * b + g - 1)
                        r = crows(c)
                        act.activation(e2[0:r, g % 2, c, :], PS[0:r, (NC * g + c) % 2, :], ACT.Exp).then_inc(e2_ready, 1)
                    fill(f"g{g}")
                pair_copied(0)
                pair_copied(1)
                fill("pv")
                act.wait_ge(aoT_done, b + 1)
                copy(aoT[:, :], PS[:, 0, :]).then_inc(aoT_copied, 1)
                fill("o1")
                fill("o2")

            def begin(layer, b, k):
                f, r = NB * layer + b, 2 * NE[layer]
                bt, _, bw = begin_banks(layer, b)
                if k == 1:
                    act.wait_ge(xnT_done, nth_norm(2 * layer + 1, b) + 1)
                    copy(xth[b][:, :], PS[:, bt, :]).then_inc(xth_ready, 1)
                elif k == 3:
                    act.wait_ge(gate_in, f + 1)
                    if layer == 0:
                        act.activation(sc1[:, 1, :, 0:E0], sc1[:, 0, :, 0:E0], ACT.Exp).then_inc(gate_exp, 1)
                    else:
                        act.activation(sc1[:, 1, :, :], sc1[:, 0, :, :], ACT.Exp, scale=-1.0).then_inc(gate_exp, 1)
                elif k == 6:
                    act.wait_ge(combT_done, f + 1)
                    copy(ct[b][0:r, :], PS[0:r, bw, :]).then_inc(cth_ready, 1)

            def chunk(layer, b, j):
                i = chunks_before(layer, b) + j
                act.wait_ge(h_mm, i + 1)
                if i and j == 0:
                    act.wait_ge(y_mm, NB * layer + b)
                if i >= 2:
                    act.wait_ge(a_ready, i - 1)
                act.activation(th[:, i % 2, :], PS[:, BH, :], ACT.Tanh, scale=0.5).then_inc(th_ready, 1)
                if j < NWB[layer]:
                    wi = weighted_before(layer, b) + j
                    act.wait_ge(w_mm, wi + 1)
                    if i >= 2:
                        act.wait_ge(down_mm, i - 1)
                    copy(u[:, i % 2, :], PS[:, BW, :]).then_inc(w_copied, 1)

            def finish(layer, b):
                act.wait_ge(down_mm, chunks_before(layer, b) + NCH[layer])
                act.wait_ge(a_ready, chunks_before(layer, b) + NCH[layer])
                copy(yT, PS[:, BY, :]).then_inc(yT_copied, 1)

            def context(k):
                if k == 0:
                    act.wait_ge(xcT_done, 1)
                    act.activation(xcT[:, :, :].rearrange("p b k -> p (b k)"), PS[:, 4, 0:NB * NK], ACT.Identity,
                                   bias=v("lxb"), scale=v("lxg")).then_inc(xcT_ready, 1)
                elif k == 1:
                    act.wait_ge(ckv_mm, 1)
                    act.activation(sqc[:, :, :], PS[0:NK, 5:5 + NB, 0:D], ACT.Square)
                    copy(vctx[:, :, :], PS[0:NK, 5:5 + NB, D:2 * D]).then_inc(cv_ready, 1)
                else:
                    act.wait_ge(kcT_done, 1)
                    copy(kctxT[:, :, :].rearrange("p b k -> p (b k)"), PS[:, 4, 0:NB * NK]).then_inc(kctx_ready, 1)

            def reload(n):
                what, half = PIECES[n]
                act.wait_ge(d_piece[n], 16)
                if what == 0:
                    w = J1 * P // 2
                    copy(sel1r[:, w * half:w * half + w], raw0[n % 2][0:2 * E1, 0:w]).then_inc(sel_ready, 1)
                else:
                    copy(uph1[what - 1][:, HALF * half:HALF * half + HALF], raw0[n % 2][:, 0:HALF]).then_inc(up_hi, 1)

            def head1(b, k):
                if k == 1:
                    act.wait_ge(xnT_done, nth_norm(2, b) + 1)
                    act.activation(LT[:, :], PS[:, BH, :], ACT.Identity, bias=v("llb"), scale=v("llg")).then_inc(LT_ready, 1)
                elif k == 2:
                    for t in range(TB):
                        act.wait_ge(proj_mm, TB * b + t + 1)
                        act.activation(sq[b][:, t, :], PS[:, BH + t, 0:2 * D], ACT.Square).then_inc(sq_ready, 1)
                    copy(V1[b].rearrange("p (t c) -> p t c", t=TB), PS[:, BH:BH + TB, 2 * D:3 * D]).then_inc(V_ready, 1)
                elif k == 3:
                    act.wait_ge(qT_done, b + 1)
                    copy(KT[b][:, :], PS[:, BG, :]).then_inc(KT_ready, 1)

            def attention1(b, fill):
                for i in range(NI):
                    n = NI * b + i
                    act.wait_ge(max_ready, n + 1)
                    if n >= 2:
                        act.wait_ge(ET_done, n - 1)
                    act.activation(E[:, i % 2, :], PS[:, 0:2, :].rearrange("p a n -> p (a n)")[:, 0:S + NK],
                                   ACT.Exp, bias=nmx[:, i:i + 1], accum_out=den[:, i:i + 1]).then_inc(E_ready, 1)
                    fill(f"i{i}")
                    act.wait_ge(ET_done, n + 1)
                    if n >= 2:
                        act.wait_ge(pv1_mm, n - 1)
                    copy(ET[0:NK, i % 2, 4, :], PS[0:NK, 1, P:2 * P]).then_inc(ET_act, 1)
                    if b == 0 and i < len(PIECES):
                        reload(i)
                fill("pv")
                act.wait_ge(aoT_done, NB + b + 1)
                copy(aoT[:, :], PS[:, 0, :]).then_inc(aoT_copied, 1)
                fill("o1")
                fill("o2")

            schedule(prepare, queries, tile, tiles_end, context, begin, chunk, finish, attention0, head1, attention1)

        @block.tensor
        def _(pe):
            def queries_and_keys(b):
                pe.wait_ge(QT_ready, b + 1)
                pe.wait_ge(KT_ready, b + 1)

            def transposed(k, b, bank):
                pe.wait_ge(xn_ready, nth_norm(k, b) + 1)
                for t in range(TB):
                    last = pe.transpose(PS[:, bank, P * t:P * t + P], xn[:, t, :], ident)
                last.then_inc(xnT_done, 1)

            def project_out(n, w, fill):
                pe.wait_ge(ao_ready, n + 1)
                for t in range(TB):
                    last = pe.transpose(PS[:, 0, P * t:P * t + P], ao[:, t, :], ident)
                last.then_inc(aoT_done, 1)
                fill("o1")
                pe.wait_ge(aoT_copied, n + 1)
                for t in range(TB):
                    last = pe.matmul(PS[:, 1, P * t:P * t + P], aoT[:, P * t:P * t + P], w, start=True, stop=True)
                last.then_inc(oproj_mm, 1)
                fill("o2")

            def layer0_keys_and_values():
                pe.wait_ge(d_cst, 16)
                pe.wait_ge(d_ctx, 16)
                for b in range(NB):
                    last = pe.transpose(PS[:, 0, NK * b:NK * b + NK], ctx_s[:, b, :], ident[0:NK, 0:NK])
                last.then_inc(ctxT_done, 1)
                pe.wait_ge(w_small, 1)
                pe.wait_ge(ctxT_copied, 1)
                for g in range(NG):
                    last = pe.matmul(PS[:, 5 + g // 2, NB * NK * (g % 2):NB * NK * (g % 2 + 1)],
                                     wkr[:, g].rearrange("p a j -> p (a j)"), ctxT[:, :, :].rearrange("p b k -> p (b k)"),
                                     start=True, stop=True)
                last.then_inc(krep_mm, 1)
                transposed(0, 0, XT_BANK[0])
                pe.wait_ge(ctxT_copied, 2)
                for b in range(NB):
                    for c in range(NC):
                        n, r = NC * b + c, crows(c)
                        last = pe.matmul(PS[0:r, 2 + n // 4, D * (n % 4):D * (n % 4) + D],
                                         ctxr[:, b].rearrange("p h k -> p (h k)")[:, CW * c:CW * c + r],
                                         wa_s[:, 2 * D:3 * D], start=True, stop=True)
                last.then_inc(v_mm, 1)

            def prepare(b, k):
                if k == 1 and b == 0:
                    layer0_keys_and_values()
                elif k == 1:
                    transposed(0, b, XT_BANK[b])

            def queries(b, g):
                if g == 0:
                    pe.wait_ge(XT_ready, b + 1)
                    pe.wait_ge(w_small, 2)
                    pe.wait_ge(kctx_ready, 1) if b else pe.wait_ge(k_raw, 1)
                pe.matmul(PS[:, BH + g, :], wqr[:, g].rearrange("p a j -> p (a j)"), XT[:, :], start=True,
                          stop=True).then_inc(q_mm, 1)

            def tile(b, t):
                if t == 0:
                    pe.wait_ge(q_ready, NG * (b + 1))
                    pe.wait_ge(k_ready, NG * (2 * b + 1))
                else:
                    pe.wait_ge(sc1_out, TB * b + t)
                for g in range(NG):
                    last = pe.matmul(PS[:, BH + g, 0:GW], qst[:, b, g, P * t:P * t + P],
                                     kst[:, GW * g:GW * g + GW], start=True, stop=True)
                last.then_inc(sc1_mm, 1)

            def attention0(b, fill):
                for t in range(TB if b == 0 else 0):
                    tile(b, t)
                    fill(f"t{t}")
                fill("s0")
                fill("s1")
                if b:
                    pe.wait_ge(x_done[1], 1)
                pe.wait_ge(sc1_out, TB * (b + 1))
                for t in range(TB):
                    last = pe.transpose(PS[0:H, 1, P * t:P * t + P], mx[:, t, :], ident)
                last.then_inc(mxT_done, 1)
                fill("s")
                pe.wait_ge(feats, b + 1)
                pe.matmul(PS[0:MH, 0, 0:H], w1s[:, 0, :], pk[:, b].rearrange("p g h -> p (g h)"), start=True, stop=False)
                for t in range(TB):
                    pe.matmul(PS[0:MH, 0, 0:H], w1s[:, 1, :], mx[:, t, :], start=False, stop=False)
                for t in range(TB):
                    last = pe.matmul(PS[0:MH, 0, 0:H], w1s[:, 2, :], vp[:, b, H * t:H * t + H], start=False,
                                     stop=(t == TB - 1))
                last.then_inc(hid_mm, 1)
                fill("mlp1")
                pe.wait_ge(d_w2, 16)
                pe.wait_ge(hid_act, 2 * b + 1)
                pe.matmul(PS[0:MH, 0, 0:H], w2t_s[:, :], h1[:, b, :], start=True, stop=True).then_inc(hid_mm, 1)
                fill("mlp2")
                pe.wait_ge(hid_act, 2 * b + 2)
                pe.wait_ge(v_ready, 1)
                pe.matmul(PS[:, 2, 0:H], w3r[:, :], h2[:, b, :], start=True, stop=True).then_inc(logt_mm, 1)
                fill("logt")
                fill("keys")

                def values(g):
                    pe.wait_ge(e2_ready, NG * NC * b + NC * (g + 1))
                    for c in range(NC):
                        r, at = crows(c), PW * (3 * g - g % 2)
                        last = pe.matmul(PS[0:2 * PW, 2 + g // 2, :], vbd[0:r, b, c, at:at + 2 * PW], e2[0:r, g % 2, c, :],
                                         start=(g % 2 == 0 and c == 0), stop=(g % 2 == 1 and c == NC - 1))
                    last.then_inc(pv_mm, 1)

                def back(a):
                    pe.wait_ge(oT_copied, 2 * b + a + 1)
                    for t in range(TB):
                        last = pe.transpose(PS[:, 2 + a, 2 * PW * t:2 * PW * t + 2 * PW], oT[a][:, P * t:P * t + P],
                                            ident[0:2 * PW, 0:2 * PW])
                    last.then_inc(oback_mm, 1)

                pe.wait_ge(nm2_ready, b + 1)
                pe.wait_ge(onehot_ready, 1)
                for g in range(NG):
                    pe.wait_ge(k_ready, NG * (2 * b + 1) + g + 1)
                    for c in range(NC):
                        n = NC * g + c
                        if n >= 2:
                            pe.wait_ge(e2_ready, NG * NC * b + n - 1)
                        r, at = crows(c), GW * g + CW * c
                        bank = PS[0:r, n % 2, :]
                        pe.matmul(bank, kst2[:, at:at + r], qst[:, b, g, :], start=True, stop=False)
                        pe.matmul(bank, onehr[:, at:at + r], nm2[:, :], start=False, stop=True).then_inc(sc2_mm, 1)
                    if g >= 1:
                        values(g - 1)
                    fill(f"g{g}")
                values(NG - 1)
                back(0)
                fill("pv")
                back(1)
                project_out(b, wa_s[:, 3 * D:4 * D], fill)

            def split_mm(bank, wh, wl, b):
                pe.matmul(bank, wh, xth[b][:, :], start=True, stop=False)
                pe.matmul(bank, wl, xth[b][:, :], start=False, stop=False)
                return pe.matmul(bank, wh, xtl[b][:, :], start=False, stop=True)

            def begin(layer, b, k):
                f, n = NB * layer + b, NE[layer]
                bt, bg, bw = begin_banks(layer, b)
                if k == 1:
                    if f == 0:
                        pe.wait_ge(sc1_out, 2 * TB)
                    if f in (1, 2):
                        queries_and_keys(f - 1)
                    transposed(2 * layer + 1, b, bt)
                elif k == 2:
                    pe.wait_ge(rt_lo, layer + 1)
                    pe.wait_ge(xtl_ready, f + 1)
                    for t in range(TB):
                        for i, a in enumerate((xth, xtl)):
                            last = pe.matmul(PS[:, bg, 2 * n * t:2 * n * t + 2 * n], a[b][:, P * t:P * t + P],
                                             rhl[layer][:, :], start=(i == 0), stop=(i == 1))
                    last.then_inc(lg_mm, 1)
                elif k == 6:
                    pe.wait_ge(comb_ready, f + 1)
                    for t in range(TB):
                        last = pe.transpose(PS[0:2 * n, bw, P * t:P * t + P], comb[:, t, 0:2 * n], ident)
                    last.then_inc(combT_done, 1)

            def down(layer, b, j):
                i = chunks_before(layer, b) + j
                pe.wait_ge(u_ready, i + 1)
                pe.matmul(PS[:, BY, :], wdn_s[layer][:, D * j:D * j + D], u[:, i % 2, :], start=(j == 0),
                          stop=(j == NCH[layer] - 1)).then_inc(down_mm, 1)

            def chunk(layer, b, j):
                n, i, c = NE[layer], chunks_before(layer, b) + j, slice(P * j, P * j + P)
                if j == 0:
                    pe.wait_ge(up_lo, 2 if layer == 0 else 6)
                    pe.wait_ge(sel_ready, 1 if layer == 0 else 3)
                    pe.wait_ge(ct_ready, NB * layer + b + 1)
                    pe.wait_ge(d_dn[layer], 16)
                    if i:
                        pe.wait_ge(x_done[2 + 2 * ((NB * layer + b - 1) // NB)], (NB * layer + b - 1) % NB + 1)
                else:
                    pe.wait_ge(a_ready, i)
                split_mm(PS[:, BH, :], uph[layer][0][:, c], upl[layer][0][:, c], b).then_inc(h_mm, 1)
                if j < NWB[layer]:
                    if j:
                        pe.wait_ge(w_copied, weighted_before(layer, b) + j)
                    pe.matmul(PS[:, BW, :], selr[layer][0:2 * n, c], ct[b][0:2 * n, :], start=True, stop=True).then_inc(w_mm, 1)
                if j >= 2:
                    down(layer, b, j - 2)
                if j:
                    pe.wait_ge(b_ready, i)
                split_mm(PS[:, BG, :], uph[layer][1][:, c], upl[layer][1][:, c], b).then_inc(g_mm, 1)

            def finish(layer, b):
                down(layer, b, NCH[layer] - 2)
                down(layer, b, NCH[layer] - 1)
                pe.wait_ge(yT_copied, NB * layer + b + 1)
                for t in range(TB):
                    last = pe.transpose(PS[:, BH, P * t:P * t + P], yT[:, P * t:P * t + P], ident)
                last.then_inc(y_mm, 1)

            def context(k):
                if k == 0:
                    pe.wait_ge(xc_ready, 2)
                    for b in range(NB):
                        last = pe.transpose(PS[:, 4, NK * b:NK * b + NK], xc[:, b, :], ident[0:NK, 0:NK])
                    last.then_inc(xcT_done, 1)
                elif k == 1:
                    pe.wait_ge(d_l1, 16)
                    pe.wait_ge(xcT_ready, 1)
                    for b in range(NB):
                        last = pe.matmul(PS[0:NK, 5 + b, 0:2 * D], xcT[:, b, :], wl1_s[:, D:3 * D], start=True, stop=True)
                    last.then_inc(ckv_mm, 1)
                else:
                    pe.wait_ge(kcn_ready, 1)
                    for b in range(NB):
                        last = pe.transpose(PS[:, 4, NK * b:NK * b + NK], kcn[:, b, :], ident[0:NK, 0:NK])
                    last.then_inc(kcT_done, 1)

            def head1(b, k):
                if k == 1:
                    transposed(2, b, BH)
                elif k == 2:
                    pe.wait_ge(LT_ready, b + 1)
                    for t in range(TB):
                        pe.matmul(PS[:, BH + t, 0:3 * D], LT[:, P * t:P * t + P], wl1_s[:, 0:3 * D], start=True,
                                  stop=True).then_inc(proj_mm, 1)
                elif k == 3:
                    pe.wait_ge(qkn_ready, b + 1)
                    for n in range(2):
                        for t in range(TB):
                            last = pe.transpose(PS[:, BH + n, P * t:P * t + P], qkn[b][:, t, D * n:D * n + D], ident)
                    last.then_inc(qT_done, 1)

            def attention1(b, fill):
                queries_and_keys(b)
                pe.wait_ge(*((x_done[3], 1) if b else (x_done[1], NB)))

                def values(i):
                    h = i % HEADS1
                    hs = slice(DH1 * h, DH1 * h + DH1)
                    pe.wait_ge(ET_dve, NI * b + i + 1)
                    pe.wait_ge(ET_act, NI * b + i + 1)
                    out_ = PS[:, 3, DH1 * i:DH1 * i + DH1]
                    for c in range(TB):
                        pe.matmul(out_, ET[:, i % 2, c, :], V1[b][:, D * c + DH1 * h:D * c + DH1 * h + DH1], start=(c == 0), stop=False)
                    pe.matmul(out_, ET[0:NK, i % 2, TB, :], vctx[:, b, hs], start=False, stop=True).then_inc(pv1_mm, 1)

                for i in range(NI):
                    t, h, n = i // HEADS1, i % HEADS1, NI * b + i
                    hs = slice(DH1 * h, DH1 * h + DH1)
                    if i:
                        pe.wait_ge(ET_act, n)
                    q = QT[b][hs, P * t:P * t + P]
                    pe.matmul(PS[:, 0, :], q, KT[b][hs, :], start=True, stop=True)
                    pe.matmul(PS[:, 1, 0:NK], q, kctxT[hs, b, :], start=True, stop=False)
                    pe.matmul(PS[:, 1, 0:NK], ones_row[:, :], mneg[:, b, :], start=False, stop=True).then_inc(sc_mm, 1)
                    fill(f"i{i}")
                    pe.wait_ge(E_ready, n + 1)
                    if i:
                        pe.wait_ge(ET_dve, n)
                    for c in range(TB):
                        pe.transpose(PS[:, 2, P * c:P * c + P], E[:, i % 2, P * c:P * c + P], ident)
                    pe.transpose(PS[0:NK, 1, P:2 * P], E[:, i % 2, S:S + NK], ident).then_inc(ET_done, 1)
                    if i:
                        values(i - 1)
                values(NI - 1)
                fill("pv")
                project_out(NB + b, wl1_s[:, 3 * D:4 * D], fill)

            schedule(prepare, queries, tile, nothing, context, begin, chunk, finish, attention0, head1, attention1)

        @block.vector
        def _(dve):
            done = [0]

            def link(ins):
                done[0] += 1
                ins.then_inc(dve_step, 1)
                dve.wait_ge(dve_step, done[0])

            def norm_stats(k, b):
                if k == 0:
                    dve.wait_ge(d_x[b], 16)
                for t in range(TB * b, TB * b + TB):
                    last = dve.bn_stats(st[:, k, t, :], X[k][:, t, :])
                link(last)
                for t in range(TB * b, TB * b + TB):
                    last = dve.bn_aggr(mv[:, k, t, :], st[:, k, t, :])
                link(last)
                scale, eps = (1.0 + LN_EPS, LN_EPS * LN_EPS) if k == 2 else (1.0, LN_EPS)
                dve.tensor_scalar(ve[:, k, tiles(b)], mv[:, k, tiles(b), 1], scale, eps, ALU.mult, ALU.add
                                  ).then_inc(ve_ready, 1)

            def norm(k, b):
                n = nth_norm(k, b)
                dve.wait_ge(rstd_ready, n + 1)
                if n:
                    dve.wait_ge(xnT_done, n)
                for t in range(TB):
                    last = dve.tensor_scalar(xn[:, t, :], X[k][:, TB * b + t, :], mv[:, k, TB * b + t, 0:1],
                                             rstd[:, k, TB * b + t:TB * b + t + 1], ALU.subtract, ALU.mult)
                last.then_inc(xn_ready, 1)

            def spread_weight(dst, n):
                dve.wait_ge(d_wa, 16)
                dve.tensor_copy(dst[:, :, :, :], bc(wa_s[:, D * n:D * n + D].rearrange("p (g j) -> p g j", g=NG)
                                                    .unsqueeze(2), [P, NG, 4, 32])).then_inc(w_small, 1)

            def small_weights():
                dve.wait_ge(d_vec, 16)
                for n, c in enumerate((ISQ / (S * NK * 4), ISQ / S, 1.0 / (S * (NK - 1)))):
                    dve.tensor_scalar(w1s[:, n, :], v("w1")[:, MH * n:MH * n + MH], c, None, ALU.mult)
                dve.tensor_copy(w3r[:, :], bc(v("w3")[0:MH, :], [MH, P]))
                dve.scalar_tensor_tensor(gqk[:, :], v("qg"), DH1 ** -0.5, v("kg"), ALU.mult, ALU.mult).then_inc(w_small, 1)

            def context_turned(k):
                dve.wait_ge(ctxT_done, 1)
                src = PS[:, 0, 0:NB * NK].rearrange("p (b k) -> p b k", b=NB)
                if k == 0:
                    dve.tensor_copy(ctxT[:, :, :], src).then_inc(ctxT_copied, 1)
                else:
                    dve.tensor_copy(ctxr[:, :, :, :], bc(src.unsqueeze(2), [P, NB, HG, NK])).then_inc(ctxT_copied, 1)

            def keys():
                dve.wait_ge(krep_mm, 1)
                for g in range(NG):
                    last = dve.tensor_scalar(krep[:, g].rearrange("p b k -> p (b k)"),
                                             PS[:, 5 + g // 2, NB * NK * (g % 2):NB * NK * (g % 2 + 1)],
                                             v("bk")[:, g:g + 1], None, ALU.add)
                link(last)

            def values():
                dve.wait_ge(v_mm, 1)
                for b in range(NB):
                    for c in range(NC):
                        n, r = NC * b + c, crows(c)
                        last = dve.tensor_tensor(tmpv[0:r, b, c, :], PS[0:r, 2 + n // 4, D * (n % 4):D * (n % 4) + D],
                                                 v("bv")[0:r, :], ALU.add)
                link(last)
                dve.wait_ge(pool_const, 1)
                for b in range(NB):
                    for c in range(NC):
                        r = crows(c)
                        slots = vbd_slots(r, b, c)
                        own = cst[0:r, CO["vm"]].rearrange("p (c h) -> p c h", c=NC)[:, c, :]
                        dve.tensor_copy(slots[:, :, :, DK], bc(own.unsqueeze(1), [r, NG, HG]))
                        last = dve.tensor_tensor(slots[:, :, :, 0:DK],
                                                 tmpv[0:r, b, c, :].rearrange("p (g h d) -> p g h d", g=NG, h=HG),
                                                 bc(own.unsqueeze(1).unsqueeze(3), [r, NG, HG, DK]), ALU.mult)
                last.then_inc(v_ready, 1)

            def low_keys(dst, src, nth):
                for g in range(NG):
                    c = slice(GW * g, GW * g + GW)
                    dve.wait_ge(k_hi, NG * nth + g + 1)
                    dve.scalar_tensor_tensor(dst[:, c], khi[:, c].bitcast(F32), cst[:, CO["nlo"]], src(g),
                                             ALU.mult, ALU.add).then_inc(k_ready, 1)

            def prepare(b, k):
                if k == 0:
                    norm_stats(0, b)
                elif k == 1:
                    if b == 0:
                        spread_weight(wkr, 1)
                        context_turned(0)
                    norm(0, b)
                    if b == 0:
                        spread_weight(wqr, 0)
                        context_turned(1)
                        small_weights()
                        keys()
                else:
                    for g in range(NG):
                        dve.tensor_tensor(kbd[:, g], bc(krep[:, g, b, :].unsqueeze(1), [P, HG, NK]),
                                          bc(cst[:, CO["hm"]].unsqueeze(2), [P, HG, NK]), ALU.mult).then_inc(k_raw, 1)
                    if b == 0:
                        dve.tensor_reduce(ksum[:, :, :], krep[:, :, :, :], X_AXIS, ALU.add)
                    low_keys(kst, lambda g: kbd[:, g].rearrange("p h k -> p (h k)"), 2 * b)

            def queries(b, g):
                lo = slice(64, 128)
                dve.wait_ge(q_hi, NG * b + g + 1)
                dve.scalar_tensor_tensor(qst[lo, b, g, :], PS[lo, BH + g, :], v("bq")[lo, g:g + 1],
                                         qst[lo, b, g, :].bitcast(F32), ALU.add, ALU.subtract).then_inc(q_ready, 1)

            def spread(b, t):
                dve.wait_ge(e1_ready, TB * b + t + 1)
                for h in range(H):
                    last = dve.bn_stats(stats[:, H * t + h, :], sh[:, t % 2, h, :])
                last.then_inc(e1_read, 1)

            def tile(b, t):
                if t >= 2:
                    spread(b, t - 2)
                dve.wait_ge(sc1_mm, TB * b + t + 1)
                sc = PS[:, BH:BH + NG, 0:GW].rearrange("p g (h k) -> p g h k", k=NK)
                m = mx[:, t, :].rearrange("p (g h) -> p g h", g=NG)
                dve.tensor_reduce(m, sc, X_AXIS, ALU.max).then_inc(mx_ready, 1)
                dve.wait_ge(mx_ready, TB * b + t + 1)
                dve.tensor_tensor(sh[:, t % 2].rearrange("p (g h) k -> p g h k", g=NG), sc,
                                  bc(m.unsqueeze(3), [P, NG, HG, NK]), ALU.subtract).then_inc(sc1_out, 1)

            def tiles_end(b, k):
                spread(b, TB - 2 + k)

            def attention0(b, fill):
                for t in range(TB if b == 0 else 0):
                    tile(b, t)
                    fill(f"t{t}")
                if b == 0:
                    tiles_end(b, 0)
                    tiles_end(b, 1)
                fill("s0")
                dve.wait_ge(e1_read, TB * (b + 1))
                me, s2e, mo, s2o = (stats[:, :, n] for n in (1, 2, 4, 5))
                ne, no = (NK + 1) // 2, NK // 2
                link(dve.tensor_scalar(sw[:, 0, :], me, float(ne), None, ALU.mult))
                link(dve.scalar_tensor_tensor(sw[:, 1, :], mo, float(no), sw[:, 0, :], ALU.mult, ALU.add))
                link(dve.tensor_tensor(sw[:, 2, :], me, mo, ALU.subtract))
                link(dve.scalar_tensor_tensor(sw[:, 3, :], sw[:, 2, :], ne * no / NK, sw[:, 2, :], ALU.mult, ALU.mult))
                fill("s1")
                link(dve.tensor_tensor(sw[:, 4, :], s2e, sw[:, 3, :], ALU.add))
                link(dve.tensor_tensor(sw[:, 5, :], s2o, sw[:, 4, :], ALU.add))
                link(dve.reciprocal(sw[:, 0, :], sw[:, 1, :]))
                link(dve.tensor_tensor(sw[:, 2, :], sw[:, 5, :], sw[:, 0, :], ALU.mult))
                dve.tensor_tensor(vp[:, b, :], sw[:, 2, :], sw[:, 0, :], ALU.mult)
                link(dve.tensor_tensor(qk1[:, b, :], qsum[:, b, :], ksum[:, :, b], ALU.mult))
                dve.tensor_tensor(pk[:, b], bc(qk1[:, b, :].unsqueeze(2), [P, NG, HG]),
                                  bc(cst[:, CO["hm"]].unsqueeze(1), [P, NG, HG]), ALU.mult).then_inc(feats, 1)
                if b == 0:
                    values()
                fill("s")
                fill("mlp1")
                fill("mlp2")
                dve.wait_ge(logt_mm, b + 1)
                link(dve.tensor_scalar(lt[:, b, 0, :], PS[:, 2, 0:H], v("b3"), LOG_T_MIN, ALU.add, ALU.max))
                dve.tensor_scalar(lt[:, b, 1, :], lt[:, b, 0, :], LOG_T_MAX, None, ALU.min).then_inc(logt_in, 1)
                fill("logt")
                dve.wait_ge(invt_raw, b + 1)
                link(dve.tensor_scalar(rt[:, b, :], rt[:, b, :], 0.5, None, ALU.mult))
                for g in range(NG):
                    dve.tensor_tensor(kf2[:, GW * g:GW * g + GW].rearrange("p (h k) -> p h k", k=NK), kbd[:, g],
                                      bc(rt[:, b, HG * g:HG * g + HG].unsqueeze(2), [P, HG, NK]), ALU.mult
                                      ).then_inc(k_raw2, 1)
                link(dve.tensor_tensor(rd[:, b, :], rt[0:H, b, :], cst[0:H, CO["eye"]], ALU.mult))
                link(dve.tensor_reduce(rneg[:, b:b + 1], rd[:, b, :], X_AXIS, ALU.add, negate=True))
                dve.wait_ge(mxT_done, b + 1)
                dve.tensor_scalar(nm2[:, :], PS[0:H, 1, :], rneg[:, b:b + 1], None, ALU.mult).then_inc(nm2_ready, 1)
                low_keys(kst2, lambda g: kf2[:, GW * g:GW * g + GW], 2 * b + 1)
                fill("keys")

                def divide(a):
                    dve.wait_ge(oback_mm, 2 * b + a + 1)
                    raw_o = PS[:, 2 + a, 0:TB * 2 * PW].rearrange("p (t h d) -> p t h d", t=TB, d=DK + 1)
                    link(dve.tensor_scalar(omin[:, a], raw_o, 0.0, None, ALU.min))
                    link(dve.scalar_tensor_tensor(onum[:, a], raw_o, 0.0, omin[:, a], ALU.max, ALU.add))
                    link(dve.tensor_scalar(oden[:, a, 0], onum[:, a, :, :, DK], 1e-30, None, ALU.max))
                    link(dve.reciprocal(oden[:, a, 1], oden[:, a, 0]))
                    w = 2 * HG * DK
                    return dve.tensor_tensor(ao[:, :, w * a:w * a + w].rearrange("p t (h d) -> p t h d", d=DK),
                                             onum[:, a, :, :, 0:DK], bc(oden[:, a, 1].unsqueeze(3), [P, TB, 2 * HG, DK]),
                                             ALU.mult)

                for g in range(NG):
                    fill(f"g{g}")
                divide(0)
                fill("pv")
                divide(1).then_inc(ao_ready, 1)
                fill("o1")
                fill("o2")
                attended(1, b, b + 1)

            def residual(k, b, src, bank):
                dve.tensor_tensor(X[k][:, tiles(b), :], src[:, tiles(b), :], bank.rearrange("p (t c) -> p t c", t=TB),
                                  ALU.add).then_inc(x_done[k], 1)
                dve.wait_ge(x_done[k], b + 1)

            def attended(k, b, n):
                dve.wait_ge(oproj_mm, n)
                dve.wait_ge(xb_ready, n)
                residual(k, b, XB, PS[:, 1, :])

            def both_halves(bank, n):
                return PS[:, bank, 0:TB * 2 * n].rearrange("p (t a e) -> p t e a", t=TB, a=2)

            def gate_top2(b, bank, part):
                n = E0
                if part == 0:
                    link(dve.tensor_reduce(lg[:, :, 0:n], both_halves(bank, n), X_AXIS, ALU.add))
                    for t in range(TB):
                        last = dve.max(m8[:, t, :], lg[:, t, 0:n])
                    last.then_inc(lg_copied, 1)
                    dve.wait_ge(lg_copied, b + 1)
                    link(dve.tensor_copy(rv[:, :, 0:2], m8[:, :, 0:2]))
                    for t in range(TB):
                        last = dve.match_replace(rp[:, t, :], rv[:, t, :], lg[:, t, :], BIG)
                    dve.tensor_tensor(sc1[:, 0, :, 0:n], lg[:, :, 0:n], bc(m8[:, :, 0:1], [P, TB, n]), ALU.subtract
                                      ).then_inc(gate_in, 1)
                elif part == 1:
                    dve.wait_ge(gate_in, b + 1)
                    link(dve.tensor_tensor(sc1[:, 2, :, 0:n], rp[:, :, 0:n], lg[:, :, 0:n], ALU.not_equal))
                    dve.wait_ge(gate_exp, b + 1)
                    link(dve.tensor_tensor(sc1[:, 3, :, 0:n], sc1[:, 1, :, 0:n], sc1[:, 2, :, 0:n], ALU.mult))
                    link(dve.tensor_reduce(gsm[:, 0, :], sc1[:, 3, :, 0:n], X_AXIS, ALU.add))
                    link(dve.reciprocal(gsm[:, 1, :], gsm[:, 0, :]))
                    link(dve.tensor_scalar(gsm[:, 1, :], gsm[:, 1, :], 0.5, None, ALU.mult))
                    copies = comb[:, :, 0:2 * n].rearrange("p t (a e) -> p t a e", a=2)
                    dve.tensor_tensor(copies, bc(sc1[:, 3, :, 0:n].unsqueeze(2), [P, TB, 2, n]),
                                      bc(gsm[:, 1, :].unsqueeze(2).unsqueeze(3), [P, TB, 2, n]), ALU.mult).then_inc(comb_ready, 1)

            def gate_groups(b, bank, part):
                n, ng = E1, 4
                if part == 0:
                    dve.tensor_reduce(sc1[:, 0, :, :], both_halves(bank, n), X_AXIS, ALU.add).then_inc(lg_copied, 1)
                    dve.wait_ge(lg_copied, NB + b + 1)
                    dve.memset(lg[:, :, ng:E0], -BIG).then_inc(gate_in, 1)
                    dve.wait_ge(gate_exp, NB + b + 1)
                    link(dve.tensor_scalar(sc1[:, 2, :, :], sc1[:, 1, :, :], 1.0, None, ALU.add))
                    link(dve.reciprocal(sc1[:, 3, :, :], sc1[:, 2, :, :]))
                    link(dve.tensor_tensor(sc1[:, 4, :, :], sc1[:, 3, :, :], bc(v("gb").unsqueeze(1), [P, TB, n]), ALU.add))
                    for t in range(TB):
                        for g in range(ng):
                            last = dve.max(g8[:, t, g, :], sc1[:, 4, t, 8 * g:8 * g + 8])
                    link(last)
                elif part == 1:
                    link(dve.tensor_tensor(lg[:, :, 0:ng], g8[:, :, :, 0], g8[:, :, :, 1], ALU.add))
                    for t in range(TB):
                        last = dve.max(m8[:, t, :], lg[:, t, 0:8])
                    link(last)
                    link(dve.tensor_copy(rv[:, :, 0:2], m8[:, :, 0:2]))
                    for t in range(TB):
                        last = dve.match_replace(rp[:, t, :], rv[:, t, :], lg[:, t, :], BIG)
                    link(last)
                    link(dve.tensor_tensor(rp[:, :, 8:8 + ng], rp[:, :, 0:ng], lg[:, :, 0:ng], ALU.not_equal))
                    for t in range(TB):
                        last = dve.tensor_tensor(sc1[:, 5, t, :].rearrange("p (g e) -> p g e", g=ng),
                                                 sc1[:, 4, t, :].rearrange("p (g e) -> p g e", g=ng),
                                                 bc(rp[:, t, 8:8 + ng].unsqueeze(2), [P, ng, 8]), ALU.mult)
                    link(last)
                    link(dve.tensor_scalar(sc1[:, 5, :, :], sc1[:, 5, :, :], 0.0, None, ALU.add))
                elif part == 2:
                    for t in range(TB):
                        last = dve.max(m8[:, t, :], sc1[:, 5, t, :])
                    link(last)
                    for t in range(TB):
                        last = dve.match_replace(sc1[:, 6, t, :], m8[:, t, :], sc1[:, 5, t, :], BIG)
                    link(last)
                    link(dve.tensor_tensor(sc1[:, 7, :, :], sc1[:, 6, :, :], sc1[:, 5, :, :], ALU.not_equal))
                    link(dve.tensor_tensor(sc1[:, 2, :, :], sc1[:, 7, :, :], sc1[:, 3, :, :], ALU.mult))
                    link(dve.tensor_reduce(gsm[:, 0, :], sc1[:, 2, :, :], X_AXIS, ALU.add))
                    link(dve.tensor_scalar(gsm[:, 0, :], gsm[:, 0, :], 1e-20, None, ALU.add))
                    link(dve.reciprocal(gsm[:, 1, :], gsm[:, 0, :]))
                    link(dve.tensor_scalar(gsm[:, 1, :], gsm[:, 1, :], 1.25, None, ALU.mult))
                    copies = comb[:, :, :].rearrange("p t (a e) -> p t a e", a=2)
                    dve.tensor_tensor(copies, bc(sc1[:, 2, :, :].unsqueeze(2), [P, TB, 2, n]),
                                      bc(gsm[:, 1, :].unsqueeze(2).unsqueeze(3), [P, TB, 2, n]), ALU.mult).then_inc(comb_ready, 1)

            def begin(layer, b, k):
                f, r = NB * layer + b, 2 * NE[layer]
                bt, bg, bw = begin_banks(layer, b)
                if k == 0:
                    norm_stats(2 * layer + 1, b)
                elif k == 1:
                    norm(2 * layer + 1, b)
                elif k == 2:
                    dve.wait_ge(xth_ready, f + 1)
                    dve.tensor_tensor(xtl[b][:, :], PS[:, bt, :], xth[b][:, :].bitcast(F32), ALU.subtract
                                      ).then_inc(xtl_ready, 1)
                elif k < 6:
                    if k == 3:
                        dve.wait_ge(lg_mm, f + 1)
                    (gate_top2, gate_groups)[layer](b, bg, k - 3)
                else:
                    dve.wait_ge(cth_ready, f + 1)
                    dve.scalar_tensor_tensor(ct[b][0:r, :], ct[b][0:r, :].bitcast(F32), cst[0:r, CO[f"nlo{layer}"]],
                                             PS[0:r, bw, :], ALU.mult, ALU.add).then_inc(ct_ready, 1)

            def chunk(layer, b, j):
                i = chunks_before(layer, b) + j
                dve.wait_ge(th_ready, i + 1)
                if i >= 2:
                    dve.wait_ge(u_ready, i - 1)
                dve.scalar_tensor_tensor(hg[:, i % 2, :], th[:, i % 2, :], 1.0, PS[:, BH, :], ALU.add, ALU.mult
                                         ).then_inc(a_ready, 1)
                dve.wait_ge(g_mm, i + 1)
                if j < NWB[layer]:
                    dve.wait_ge(w_copied, weighted_before(layer, b) + j + 1)
                    dve.tensor_tensor(u[:, i % 2, :], u[:, i % 2, :], PS[:, BG, :], ALU.mult).then_inc(b_ready, 1)
                else:
                    dve.wait_ge(down_mm, i - 1)
                    dve.tensor_scalar(u[:, i % 2, :], PS[:, BG, :], 0.5, None, ALU.mult).then_inc(b_ready, 1)

            def finish(layer, b):
                k = 2 + 2 * layer
                dve.wait_ge(y_mm, NB * layer + b + 1)
                residual(k, b, X[k - 1], PS[:, BH, :])

            def context(k):
                by_head = "p b (h d) -> p b h d"
                if k == 0:
                    dve.wait_ge(d_ctx, 16)
                    for b in range(NB):
                        last = dve.bn_stats(st[0:NK, 4, b, :], ctx_s[:, b, :])
                    link(last)
                    for b in range(NB):
                        last = dve.bn_aggr(mv[0:NK, 4, b, :], st[0:NK, 4, b, :])
                    link(last)
                    dve.tensor_scalar(ve[0:NK, 4, 0:NB], mv[0:NK, 4, 0:NB, 1], LN_EPS, None, ALU.add).then_inc(cve_ready, 1)
                    dve.wait_ge(d_mask, 16)
                    dve.tensor_scalar(mneg[:, :, :].rearrange("p b k -> p (b k)"), mask_s[:, :], 1.0, 1e30, ALU.subtract,
                                      ALU.mult).then_inc(xc_ready, 1)
                    dve.wait_ge(crstd_ready, 1)
                    for b in range(NB):
                        last = dve.tensor_scalar(xc[:, b, :], ctx_s[:, b, :], mv[0:NK, 4, b, 0:1], rstd[0:NK, 4, b:b + 1],
                                                 ALU.subtract, ALU.mult)
                    last.then_inc(xc_ready, 1)
                elif k == 1:
                    dve.wait_ge(cv_ready, 1)
                    link(dve.tensor_reduce(ssc[:, 0], sqc[:, :, :].rearrange(by_head, h=HEADS1), X_AXIS, ALU.add))
                    dve.tensor_scalar(ssc[:, 1], ssc[:, 0], 1.0 / DH1, 1e-16, ALU.mult, ALU.max).then_inc(cssm_ready, 1)
                else:
                    dve.wait_ge(crs_ready, 1)
                    dve.tensor_tensor(kcn[:, :, :].rearrange(by_head, h=HEADS1),
                                      PS[0:NK, 5:5 + NB, 0:D].rearrange(by_head, h=HEADS1),
                                      bc(ssc[:, 2].unsqueeze(3), [NK, NB, HEADS1, DH1]), ALU.mult).then_inc(kcn_ready, 1)

            def head1(b, k):
                by_head = "p t (n d) -> p t n d"
                if k == 0:
                    norm_stats(2, b)
                elif k == 1:
                    norm(2, b)
                elif k == 2:
                    dve.wait_ge(sq_ready, TB * (b + 1))
                    link(dve.tensor_reduce(ss[:, :, :], sq[b].rearrange(by_head, n=4), X_AXIS, ALU.add))
                    dve.tensor_scalar(ssm[:, :, :], ss[:, :, :], 1.0 / DH1, 1e-16, ALU.mult, ALU.max).then_inc(ssm_ready, 1)
                else:
                    dve.wait_ge(rs_ready, b + 1)
                    dve.wait_ge(V_ready, b + 1)
                    dve.tensor_tensor(qkn[b].rearrange(by_head, n=4), PS[:, BH:BH + TB, 0:2 * D].rearrange(by_head, n=4),
                                      bc(rs[:, :, :].unsqueeze(3), [P, TB, 4, DH1]), ALU.mult).then_inc(qkn_ready, 1)
                    dve.wait_ge(qT_done, b + 1)
                    dve.tensor_scalar(QT[b][:, :], PS[:, BH, :], gqk[:, :], None, ALU.mult).then_inc(QT_ready, 1)

            def attention1(b, fill):
                for i in range(NI):
                    n = NI * b + i
                    dve.wait_ge(sc_mm, n + 1)
                    dve.tensor_reduce(nmx[:, i:i + 1], PS[:, 0:2, :].rearrange("p a n -> p (a n)")[:, 0:S + NK],
                                      X_AXIS, ALU.max, negate=True).then_inc(max_ready, 1)
                    fill(f"i{i}")
                    dve.wait_ge(ET_done, n + 1)
                    if n >= 2:
                        dve.wait_ge(pv1_mm, n - 1)
                    dve.tensor_copy(ET[:, i % 2, 0:TB, :], PS[:, 2, :].rearrange("p (c q) -> p c q", c=TB)).then_inc(ET_dve, 1)
                dve.wait_ge(E_ready, NI * (b + 1))
                link(dve.reciprocal(rden[:, :], den[:, :]))
                dve.wait_ge(pv1_mm, NI * (b + 1))
                dve.tensor_tensor(ao[:, :, :].rearrange("p t (h d) -> p (t h) d", h=HEADS1),
                                  PS[:, 3, :].rearrange("p (i d) -> p i d", d=DH1),
                                  bc(rden[:, :].unsqueeze(2), [P, NI, DH1]), ALU.mult).then_inc(ao_ready, 1)
                fill("pv")
                fill("o1")
                fill("o2")
                attended(3, b, NB + b + 1)

            schedule(prepare, queries, tile, tiles_end, context, begin, chunk, finish, attention0, head1, attention1)


def shape_constants():
    import numpy as np
    p = np.arange(P)
    c = np.zeros((P, NCC), np.float32)
    c[:, CO["ident"]] = np.eye(P)
    c[:, CO["hm"]] = (p[:, None] % 32) // DK == np.arange(HG)[None]
    c[:, CO["nlo"]] = -1.0 * ((p[:, None] // 32 == 1) | (p[:, None] // 32 == 2))
    for n in range(NC):
        r = np.arange(min(CW, GW - CW * n))
        c[:len(r), CO["vm"].start + HG * n:CO["vm"].start + HG * (n + 1)] = (r[:, None] + CW * n) // NK == np.arange(HG)[None]
    c[:H, CO["eye"]] = np.eye(H)
    c[E0:2 * E0, CO["nlo0"]] = -1.0
    c[E1:2 * E1, CO["nlo1"]] = -1.0
    onehot = np.repeat(np.eye(H, dtype=np.float32), NK, axis=1)
    sel = [np.tile(np.repeat(np.eye(e, dtype=np.float32), n, axis=1), (2, 1)) for e, n in ((E0, HID0), (E1, HID1))]
    return c, onehot, sel


def kernel(**inputs):
    import numpy as np
    import concourse.bacc as bacc
    from concourse.bass_utils import run_bass_kernel_spmd as run

    i = {k: np.asarray(a) for k, a in inputs.items()}
    a, f, l, g = ({k[len(n):]: w for k, w in i.items() if k.startswith(n)}
                  for n in ("L0_xattn_", "L0_ffn_", "L1_xattn_", "L1_ffn_"))

    def channel_rows(w):
        return np.tile(w.reshape(NG, 32).T, (4, 1))

    def column(w):
        return np.tile(w.reshape(-1), P // w.size)[:, None]

    def rows(w):
        return np.broadcast_to(w.reshape(1, -1), (P, w.size))

    consts, onehot, (sel0, sel1) = shape_constants()
    vecs = dict(bq=channel_rows(a["bq"]), bk=channel_rows(a["bk"]), lxg=column(l["ln_x_g"]), lxb=column(l["ln_x_b"]),
                llg=column(l["ln_l_g"]), llb=column(l["ln_l_b"]), qg=column(l["q_gamma"]), kg=column(l["k_gamma"]),
                b1=column(a["b1"]), b2=column(a["b2"]), w3=column(a["w3"]), b3=column(a["b3"]), w1=rows(a["w1"].T),
                gb=rows(g["gate_bias"]), bo=rows(a["bo"]), bv=rows(a["bv"]), bout=rows(l["b_out"]))

    def hidden_last(w):
        return w.transpose(1, 0, 2).reshape(D, -1)

    arrays = dict(
        x=i["x"].reshape(NB * S, D), ctx=i["ctx_1024"], mask=i["mask_BxS2_bk0"].reshape(1, NB * NK).astype(np.int32),
        vecs=np.concatenate([vecs[k] for k in V_COLS], axis=1),
        wa=np.concatenate([a[k].T for k in ("Wq", "Wk", "Wv", "Wo")], axis=1), w2t=a["w2"].T, wr=f["Wr"],
        up0=np.stack([hidden_last(f["W1"]), hidden_last(f["W3"])]), wdn0=f["W2"].reshape(-1, D),
        wl1=np.concatenate([l["W_q"], l["W_kv"], l["W_out"]], axis=1), gw=g["gate_w"].T,
        up1=np.stack([np.concatenate([g[f"expert_{k}"].transpose(2, 0, 1).reshape(D, -1), g[f"shared_{k}"].T], axis=1)
                      for k in ("gate", "up")]),
        wdn1=np.concatenate([g["expert_down"].transpose(0, 2, 1).reshape(-1, D), g["shared_down"].T], axis=0),
        consts=consts, onehot=onehot, sel0=sel0, sel1=sel1)
    nc = bacc.Bacc("TRN2", target_bir_lowering=False, num_devices=1)
    fed, args = {}, {}
    for name, w in arrays.items():
        w = np.ascontiguousarray(w)
        fed[f"in_{name}"] = w
        args[name] = nc.dram_tensor(f"in_{name}", w.shape, mybir.dt.from_np(w.dtype), kind="ExternalInput").ap()
    out = nc.dram_tensor("out_x", (NB * S, D), F32, kind="ExternalOutput").ap()
    program(nc, out=out, **args)
    r = run(nc, [fed], core_ids=[0])
    return r.results[0]["out_x"].reshape(NB, S, D)
```
